# Optimizing a Trainium2 kernel written in Bass

```python
import numpy as np
import jax
import jax.numpy as jnp

def _softmax(x, axis=-1):
    return jax.nn.softmax(x, axis=axis)

def _gelu(x):
    return jax.nn.gelu(x, approximate=True)

def _silu(x):
    return jax.nn.silu(x)

def _sigmoid(x):
    return jax.nn.sigmoid(x)

def _layernorm(x, axis=-1, eps=1e-05):
    m = jnp.mean(x, axis=axis, keepdims=True)
    v = jnp.var(x, axis=axis, keepdims=True)
    return (x - m) / jnp.sqrt(v + eps)

def _scatter_add(tgt, idx, src, axis=0):
    return tgt.at[idx].add(src)

def _segment_sum(src, seg, n):
    return jax.ops.segment_sum(src, seg, n)
kernel_name = 'mk_gnn_preln_d4_gnn_r32_df067b'

def setup_inputs(seed: int=0):
    np.random.seed(seed)
    _w = jnp.asarray

    def _rec_inputs():
        import jax
        import jax.numpy as jnp
        _gk = jax.random.key(seed)
        x = -0.000202 + 1 * jax.random.normal(jax.random.fold_in(_gk, 1), (3125, 128), jnp.float32)
        _s = jax.random.randint(jax.random.fold_in(_gk, 2), (50000,), 0, 3125, jnp.int32)
        _d = jax.random.randint(jax.random.fold_in(_gk, 3), (50000,), 0, 3125, jnp.int32)
        _loop = jnp.arange(3125, dtype=jnp.int32)
        src = jnp.concatenate([_s, _d, _loop])
        dst = jnp.concatenate([_d, _s, _loop])
        _o = jnp.argsort(dst, stable=True)
        src = src[_o]
        dst = dst[_o]
        edge_type_200 = jax.random.randint(jax.random.fold_in(_gk, 12), (103125,), 0, 200, jnp.int32)
        edge_weight = -0.000492943 + 0.999642 * jax.random.normal(jax.random.fold_in(_gk, 13), (103125,), jnp.float32)
        return (x, src, dst, edge_type_200, edge_weight)
    x, src, dst, edge_type_200, edge_weight = _rec_inputs()

    def _L0_gnn_setup():
        import jax, jax.numpy as jnp
        import numpy as np
        EPS = 1e-09
        LN_EPS = 1e-05

        def _proj_normalize(v):
            return v / (jnp.linalg.norm(v, axis=-1, keepdims=True) + EPS)
        N, E, Fin, Fout = (50000, 18750, 128, 128)
        key = jax.random.key(seed)
        ks = jax.random.split(key, 8)
        x = jax.random.normal(ks[0], (N, Fin), jnp.float32)
        edge_index = jax.random.randint(ks[1], (2, E), 0, N, dtype=jnp.int64)
        edge_weight = jax.random.normal(ks[2], (E,), jnp.float32)
        W_self = jax.random.normal(ks[3], (Fin, Fout), jnp.float32) / np.sqrt(Fin)
        b_self = jnp.zeros((Fout,), jnp.float32)
        W_nb = jax.random.normal(ks[4], (Fin, Fout), jnp.float32) / np.sqrt(Fin)
        b_nb = jnp.zeros((Fout,), jnp.float32)
        gamma = jnp.ones((Fout,), jnp.float32)
        beta = jnp.zeros((Fout,), jnp.float32)
        return dict(x=x, edge_index=edge_index, edge_weight=edge_weight, W_self=W_self, b_self=b_self, W_nb=W_nb, b_nb=b_nb, gamma=gamma, beta=beta)
    _L0_gnn_all = _L0_gnn_setup()
    _L0_gnn_in = {k: v for k, v in _L0_gnn_all.items() if k in ('W_self', 'b_self', 'W_nb', 'b_nb', 'gamma', 'beta')}
    del _L0_gnn_all

    def _L1_gnn_setup():
        import jax, jax.numpy as jnp
        import numpy as np
        N_NODES = 50000
        N_EDGES = 25000
        IN_CH = 128
        OUT_CH = 128
        MLP_HID = 64
        key = jax.random.key(seed)
        ks = jax.random.split(key, 8)
        x = jax.random.normal(ks[0], (N_NODES, IN_CH), dtype=jnp.float32)
        edge_index = jax.random.randint(ks[1], (2, N_EDGES), 0, N_NODES, dtype=jnp.int64)
        s1 = 1.0 / np.sqrt(2 * IN_CH)
        mlp_w1 = jax.random.uniform(ks[2], (2 * IN_CH, MLP_HID), jnp.float32, -s1, s1)
        mlp_b1 = jax.random.uniform(ks[3], (MLP_HID,), jnp.float32, -s1, s1)
        s2 = 1.0 / np.sqrt(MLP_HID)
        mlp_w2 = jax.random.uniform(ks[4], (MLP_HID, 1), jnp.float32, -s2, s2)
        mlp_b2 = jax.random.uniform(ks[5], (1,), jnp.float32, -s2, s2)
        s3 = 1.0 / np.sqrt(IN_CH)
        conv_w = jax.random.uniform(ks[6], (IN_CH, OUT_CH), jnp.float32, -s3, s3)
        conv_b = jnp.zeros((OUT_CH,), jnp.float32)
        return {'x': x, 'edge_index': edge_index, 'mlp_w1': mlp_w1, 'mlp_b1': mlp_b1, 'mlp_w2': mlp_w2, 'mlp_b2': mlp_b2, 'conv_w': conv_w, 'conv_b': conv_b}
    _L1_gnn_all = _L1_gnn_setup()
    _L1_gnn_in = {k: v for k, v in _L1_gnn_all.items() if k in ('mlp_w1', 'mlp_b1', 'mlp_w2', 'mlp_b2', 'conv_w', 'conv_b')}
    del _L1_gnn_all

    def _L2_gnn_setup():
        import jax, jax.numpy as jnp
        import numpy as np
        N_NODES = 50000
        N_EDGES = 20000
        N_REL = 200
        D_IN = 128
        D_OUT = 128
        key = jax.random.key(seed)
        k1, k2, k3, k4, k5, k6 = jax.random.split(key, 6)
        x = jax.random.normal(k1, (N_NODES, D_IN), dtype=jnp.float32)
        edge_index = jax.random.randint(k2, (2, N_EDGES), 0, N_NODES, dtype=jnp.int64)
        edge_type = jax.random.randint(k3, (N_EDGES,), 0, N_REL, dtype=jnp.int64)
        rel_emb = jax.random.normal(k4, (N_REL, D_IN), dtype=jnp.float32)
        W_lin = jax.random.normal(k5, (D_OUT, D_IN), dtype=jnp.float32) * (1.0 / np.sqrt(D_IN))
        limit = np.sqrt(6.0 / (1 + D_IN))
        W_attn = jax.random.uniform(k6, (1, D_IN), dtype=jnp.float32, minval=-limit, maxval=limit)
        return {'x': x, 'edge_index': edge_index, 'edge_type': edge_type, 'rel_emb': rel_emb, 'W_lin': W_lin, 'W_attn': W_attn}
    _L2_gnn_all = _L2_gnn_setup()
    _L2_gnn_in = {k: v for k, v in _L2_gnn_all.items() if k in ('rel_emb', 'W_lin', 'W_attn')}
    del _L2_gnn_all

    def _L3_gnn_setup():
        import jax, jax.numpy as jnp
        import numpy as np
        N = 50000
        E = 20000
        D = 128
        NUM_LAYERS = 2
        key = jax.random.key(seed)
        k1, k2 = jax.random.split(key)
        emb = jax.random.normal(k1, (N, D), dtype=jnp.float32)
        edge_index = jax.random.randint(k2, (2, E), 0, N, dtype=jnp.int64)
        return {'emb': emb, 'edge_index': edge_index}
    _L3_gnn_all = _L3_gnn_setup()
    _L3_gnn_in = {k: v for k, v in _L3_gnn_all.items() if k in ()}
    del _L3_gnn_all
    return {'x': x, 'src': src, 'dst': dst, 'edge_type_200': edge_type_200, 'edge_weight': edge_weight, 'L0_gnn_W_self': _L0_gnn_in['W_self'], 'L0_gnn_b_self': _L0_gnn_in['b_self'], 'L0_gnn_W_nb': _L0_gnn_in['W_nb'], 'L0_gnn_b_nb': _L0_gnn_in['b_nb'], 'L0_gnn_gamma': _L0_gnn_in['gamma'], 'L0_gnn_beta': _L0_gnn_in['beta'], 'L1_gnn_mlp_w1': _L1_gnn_in['mlp_w1'], 'L1_gnn_mlp_b1': _L1_gnn_in['mlp_b1'], 'L1_gnn_mlp_w2': _L1_gnn_in['mlp_w2'], 'L1_gnn_mlp_b2': _L1_gnn_in['mlp_b2'], 'L1_gnn_conv_w': _L1_gnn_in['conv_w'], 'L1_gnn_conv_b': _L1_gnn_in['conv_b'], 'L2_gnn_rel_emb': _L2_gnn_in['rel_emb'], 'L2_gnn_W_lin': _L2_gnn_in['W_lin'], 'L2_gnn_W_attn': _L2_gnn_in['W_attn']}

def reference(x, src, dst, edge_type_200, edge_weight, L0_gnn_W_self, L0_gnn_b_self, L0_gnn_W_nb, L0_gnn_b_nb, L0_gnn_gamma, L0_gnn_beta, L1_gnn_mlp_w1, L1_gnn_mlp_b1, L1_gnn_mlp_w2, L1_gnn_mlp_b2, L1_gnn_conv_w, L1_gnn_conv_b, L2_gnn_rel_emb, L2_gnn_W_lin, L2_gnn_W_attn):
    import jax
    import jax.numpy as jnp

    def _L0_gnn_ref(x, edge_index, edge_weight, W_self, b_self, W_nb, b_nb, gamma, beta):
        import jax, jax.numpy as jnp
        import numpy as np
        EPS = 1e-09
        LN_EPS = 1e-05

        def _proj_normalize(v):
            return v / (jnp.linalg.norm(v, axis=-1, keepdims=True) + EPS)
        N = x.shape[0]
        src, tgt = (edge_index[0], edge_index[1])
        seg_max = jax.ops.segment_max(edge_weight, tgt, num_segments=N)
        ew = jnp.exp(edge_weight - seg_max[tgt])
        denom = jax.ops.segment_sum(ew, tgt, num_segments=N)
        alpha = ew / denom[tgt]
        agg = jax.ops.segment_sum(alpha[:, None] * x[src], tgt, num_segments=N)
        agg = _proj_normalize(agg)
        self_feat = x @ W_self + b_self
        nb_feat = agg @ W_nb + b_nb
        comb = _proj_normalize(0.5 * (self_feat + nb_feat))
        mu = jnp.mean(comb, axis=-1, keepdims=True)
        var = jnp.var(comb, axis=-1, keepdims=True)
        out = (comb - mu) / jnp.sqrt(var + LN_EPS) * gamma + beta
        return out

    def _L1_gnn_ref(x, edge_index, mlp_w1, mlp_b1, mlp_w2, mlp_b2, conv_w, conv_b):
        import jax, jax.numpy as jnp
        import numpy as np
        N_NODES = 50000
        N_EDGES = 25000
        IN_CH = 128
        OUT_CH = 128
        MLP_HID = 64
        n = x.shape[0]
        row, col = (edge_index[0], edge_index[1])
        edge_feat = jnp.concatenate([x[row], x[col]], axis=-1)
        h = jax.nn.gelu(edge_feat @ mlp_w1 + mlp_b1, approximate=False)
        edge_weight = jax.nn.sigmoid(h @ mlp_w2 + mlp_b2)[:, 0]
        loop = jnp.arange(n, dtype=row.dtype)
        row_f = jnp.concatenate([row, loop])
        col_f = jnp.concatenate([col, loop])
        ew_f = jnp.concatenate([edge_weight, jnp.ones((n,), x.dtype)])
        deg = jax.ops.segment_sum(ew_f, col_f, num_segments=n)
        dinv = jnp.where(deg > 0, jax.lax.rsqrt(deg), 0.0)
        norm = dinv[row_f] * ew_f * dinv[col_f]
        xt = x @ conv_w
        msg = xt[row_f] * norm[:, None]
        out = jax.ops.segment_sum(msg, col_f, num_segments=n)
        return out + conv_b

    def _L2_gnn_ref(x, edge_index, edge_type, rel_emb, W_lin, W_attn):
        import jax, jax.numpy as jnp
        import numpy as np
        N_NODES = 50000
        N_EDGES = 20000
        N_REL = 200
        D_IN = 128
        D_OUT = 128
        x_trans = x @ W_lin.T
        src_idx, tgt_idx = (edge_index[0], edge_index[1])
        h_src = x[src_idx]
        h_rel = rel_emb[edge_type]
        sum_feat = h_src + h_rel
        attn = jax.nn.sigmoid(sum_feat @ W_attn.T)
        msg = x_trans[src_idx] * attn
        out = jax.ops.segment_sum(msg, tgt_idx, num_segments=x.shape[0])
        return jax.nn.relu(out)

    def _L3_gnn_ref(emb, edge_index):
        import jax, jax.numpy as jnp
        import numpy as np
        N = 50000
        E = 20000
        D = 128
        NUM_LAYERS = 2
        row, col = (edge_index[0], edge_index[1])
        n = emb.shape[0]
        ones = jnp.ones(row.shape[0], dtype=emb.dtype)
        deg = jax.ops.segment_sum(ones, col, num_segments=n)
        deg_inv_sqrt = jnp.where(deg > 0, jax.lax.rsqrt(deg), 0.0).astype(emb.dtype)
        norm = deg_inv_sqrt[row] * deg_inv_sqrt[col]
        x = emb
        out = x
        for _ in range(NUM_LAYERS):
            msgs = x[row] * norm[:, None]
            x = jax.ops.segment_sum(msgs, col, num_segments=n)
            out = out + x
        return out / (NUM_LAYERS + 1)
    edge_index = jnp.stack([src, dst])
    h = jnp.maximum(_layernorm(x, axis=-1), 0.0)
    x = x + _L0_gnn_ref(h, edge_index, edge_weight, L0_gnn_W_self, L0_gnn_b_self, L0_gnn_W_nb, L0_gnn_b_nb, L0_gnn_gamma, L0_gnn_beta)
    h = jnp.maximum(_layernorm(x, axis=-1), 0.0)
    x = x + _L1_gnn_ref(h, edge_index, L1_gnn_mlp_w1, L1_gnn_mlp_b1, L1_gnn_mlp_w2, L1_gnn_mlp_b2, L1_gnn_conv_w, L1_gnn_conv_b)
    h = jnp.maximum(_layernorm(x, axis=-1), 0.0)
    x = x + _L2_gnn_ref(h, edge_index, edge_type_200, L2_gnn_rel_emb, L2_gnn_W_lin, L2_gnn_W_attn)
    h = jnp.maximum(_layernorm(x, axis=-1), 0.0)
    x = x + _L3_gnn_ref(h, edge_index)
    return x

_drawn_inputs = setup_inputs


def setup_inputs(seed=0):
    import zlib

    import numpy as np

    out = dict(_drawn_inputs(seed))
    spreads = {'L0_gnn_b_self': (0.0, 0.1),
     'L0_gnn_b_nb': (0.0, 0.1),
     'L0_gnn_gamma': (1.0, 0.2),
     'L0_gnn_beta': (0.0, 0.1),
     'L1_gnn_conv_b': (0.0, 0.1)}
    factors = {'edge_weight': 6.546, 'L1_gnn_mlp_w1': 8.0, 'L1_gnn_mlp_b1': 54.861, 'L1_gnn_mlp_w2': 8.0}
    for name, (base, spread) in spreads.items():
        noise = np.random.default_rng([zlib.crc32(name.encode()), seed]).standard_normal(out[name].shape)
        drawn = base * np.exp(spread * noise) if base else spread * noise
        out[name] = jnp.asarray(drawn.astype(out[name].dtype))
    for name, factor in factors.items():
        out[name] = (out[name] * factor).astype(out[name].dtype)
    return out
```

```python
from contextlib import ExitStack

import concourse.bass as bass
from concourse import mybir

F32 = mybir.dt.float32
BF16 = mybir.dt.bfloat16
I32 = mybir.dt.int32
ALU = mybir.AluOpType
ACT = mybir.ActivationFunctionType
AX = mybir.AxisListType

P = 128
N = 3125
F = 128
HID = 64
NREL = 200
E = 103125
B = (N + P - 1) // P
SLOT = 64
NG = -(-B // 4)
PB = (B + 1) // 2
BE = 2 * PB
CW = 16
CPB = P // CW
NCH = PB * CPB
HP, HT = 125, 825
HTP = 832
GT = 16
GC = -(-(E + SLOT) // (P * GT))
EP = GC * P * GT
VN = B + 2
LN_EPS = 1e-5
EPS = 1e-9
BIG = 1e30


def mlp_out(v, link, blk_gelu, blk_used, GB, w2_s, wE, b):
    g3 = GB[b % 3].rearrange("p (s f) -> p s f", f=HID)
    v.wait_ge(blk_gelu, b + 1)
    link(v.tensor_tensor(g3, g3, w2_s[:, None, :].broadcast_to([P, SLOT, HID]), ALU.mult))
    link(v.tensor_reduce(wE[:, b, :], g3, AX.X, ALU.add))
    v.nop().then_inc(blk_used, 1)


def build(nc, x, src, dst, etype, eweight, w_self, b_self, w_nb, b_nb, gamma, beta,
          w1, b1, w2, b2, conv_w, conv_b, rel, w_lin_t, w_attn, out):
    ctx = ExitStack()
    with ctx:
        def sb(name, shape, dt=F32):
            return ctx.enter_context(nc.sbuf_tensor(name, shape, dt))

        def sem(name):
            return ctx.enter_context(nc.semaphore(name))

        X = sb("X", [P, B, F])
        Hn = sb("Hn", [P, B, F])
        TB = sb("TB", [P, B, F])
        AGG = sb("AGG", [P, BE, F])
        STR = sb("STR", [P, 2, 2, B, P])
        stream = STR[:].rearrange("p a q h d -> p (a q h d)")
        T1 = stream[:, 0:B * F].rearrange("p (b f) -> p b f", f=F)
        T2 = stream[:, B * F:2 * B * F].rearrange("p (b f) -> p b f", f=F)
        inT = stream[:, 2 * B * F:2 * B * F + 4 * 4 * P].rearrange("p (a n) -> p a n", a=4)
        GB = [stream[:, i * SLOT * HID:(i + 1) * SLOT * HID] for i in range(3)]
        BC = [stream[:, i * 1024:(i + 1) * 1024].bitcast(BF16) for i in range(4)]
        srcE = sb("srcE", [P, BE, SLOT], I32)
        typE = sb("typE", [P, BE, SLOT], I32)
        ewE = sb("ewE", [P, BE, SLOT])
        maskE = sb("maskE", [P, BE, SLOT])
        wE = srcE[:].bitcast(F32)
        loT = sb("loT", [P, PB * P], BF16)
        hiT = sb("hiT", [P, PB * P], BF16)
        thT = sb("thT", [P, PB * P], BF16)
        wT = [sb(f"wT{i}", [P, PB * P], BF16) for i in range(3)]
        mT = sb("mT", [P, PB * P], BF16)
        rT = sb("rT", [P, PB * P])
        LO = [sb(f"LO{i}", [P, P, CW], BF16) for i in range(4)]
        HM = [sb(f"HM{i}", [P, VN, CW], BF16) for i in range(4)]
        HW = [sb(f"HW{i}", [P, 3, B, CW], BF16) for i in range(4)]
        VP = sb("VP", [P, VN, CW])
        PG = [LO[i][:].rearrange("p a b -> p (a b)").bitcast(F32).rearrange("p (t f) -> p t f", f=HID)
              for i in range(3)]
        LS = [LO[i][:].rearrange("p a b -> p (a b)") for i in range(4)]
        iotaLo = sb("iotaLo", [P, P, CW], BF16)
        iotaHi = sb("iotaHi", [P, VN, CW], BF16)
        iotaP = sb("iotaP", [P, 1])
        slotI = sb("slotI", [P, SLOT])
        ident = sb("ident", [P, P])
        upper = sb("upper", [P, P])
        ones = sb("ones", [P, P])
        wself_s = sb("wself_s", [F, F])
        wnb_s = sb("wnb_s", [F, F])
        w1_s = sb("w1_s", [F, 2 * HID])
        conv_s = sb("conv_s", [F, F])
        wlin_s = sb("wlin_s", [F, F])
        bias0 = sb("bias0", [P, 2, F])
        bias1 = sb("bias1", [P, 2 * HID])
        biasc = sb("biasc", [P, F])
        gam_s = sb("gam_s", [P, F])
        bet_s = sb("bet_s", [P, F])
        wat_s = sb("wat_s", [P, F])
        w2_s = sb("w2_s", [P, HID])
        b2_s = sb("b2_s", [P, 1])
        rel_s = sb("rel_s", [P, 2, F])
        dstS = T2[:, 0:7, :].rearrange("p b f -> p (b f)")[:, 0:HTP].bitcast(I32)
        dloI = T2[:, 7:14, :].rearrange("p b f -> p (b f)")[:, 0:HTP].bitcast(I32)
        dlo = T1[:, 0:4, :].rearrange("p b f -> p (b f)").bitcast(BF16)[:, 0:HTP]
        dhi = T1[:, 4:8, :].rearrange("p b f -> p (b f)").bitcast(BF16)[:, 0:HTP]
        tmpE = T1[:, 0:13, :].rearrange("p b f -> p (b f)").rearrange("p (b s) -> p b s", s=SLOT)
        tmpI = T2[:, 0:13, :].rearrange("p b f -> p (b f)").bitcast(I32).rearrange("p (b s) -> p b s", s=SLOT)
        bfE = T1[:, 13:20, :].rearrange("p b f -> p (b f)").bitcast(BF16)[:, 0:BE * SLOT].rearrange(
            "p (b s) -> p b s", s=SLOT)
        bfT = T2[:, 13:20, :].rearrange("p b f -> p (b f)").bitcast(BF16)[:, 0:BE * SLOT].rearrange(
            "p (b s) -> p b s", s=SLOT)
        deg = sb("deg", [P, BE])
        tot = sb("tot", [P, B])
        scn = sb("scn", [P, B])
        rowf = sb("rowf", [P, B])
        rowI = sb("rowI", [P, B], I32)
        c1 = sb("c1", [P, BE])
        c2 = sb("c2", [P, BE])
        c3 = sb("c3", [P, BE])
        c4 = sb("c4", [P, BE])
        gate = sb("gate", [P, 1])
        dinv = sb("dinv", [P, B])
        dis = sb("dis", [P, B])
        stab = sb("stab", [P, 3, B], BF16)
        rtab = sb("rtab", [P, 3, 2], BF16)
        rcol = sb("rcol", [P, 2])
        idxA = sb("idxA", [P, GC, GT], I32)
        idxS = [sb(f"idxS{i}", [P, GT], I32) for i in range(3)]

        zero_l = sb("zero_l", [1, P], BF16)[:]
        zero_r = sb("zero_r", [1, B], BF16)[:]
        bank = [ctx.enter_context(nc.psum_tensor(f"bank{i}", [P, 512], F32)) for i in range(8)]

        p_tab = nc.dram_tensor("p_tab", (B * P, HID), F32).ap()
        p_flat = nc.dram_tensor("p_flat", (EP, HID), F32).ap()
        lo_dram = nc.dram_tensor("lo_dram", (PB, P, P), BF16).ap()
        tl_dram = nc.dram_tensor("tl_dram", (PB, P, P), BF16).ap()

        x_loaded = sem("x_loaded")
        dst_loaded = sem("dst_loaded")
        w_loaded = sem("w_loaded")
        idx_loaded = sem("idx_loaded")
        const_made = sem("const_made")
        dve_step = sem("dve_step")
        zeros_made = sem("zeros_made")
        hist_full = sem("hist_full")
        hist_used = sem("hist_used")
        hist_done = sem("hist_done")
        deg_ready = sem("deg_ready")
        prefix_done = sem("prefix_done")
        row_ready = sem("row_ready")
        src_rows = sem("src_rows")
        ew_rows = sem("ew_rows")
        typ_rows = sem("typ_rows")
        tin_ready = sem("tin_ready")
        tout_ready = sem("tout_ready")
        tout_used = sem("tout_used")
        lo_ready = sem("lo_ready")
        lo_stored = sem("lo_stored")
        col_ready = sem("col_ready")
        col_done = sem("col_done")
        lin_in = sem("lin_in")
        tp_ready = sem("tp_ready")
        inT_ready = sem("inT_ready")
        lin_ready = sem("lin_ready")
        lin_taken = sem("lin_taken")
        pass_in = sem("pass_in")
        hot_full = sem("hot_full")
        chunk_built = sem("chunk_built")
        chunk_saved = sem("chunk_saved")
        spmm_done = sem("spmm_done")
        agg_saved = sem("agg_saved")
        p_ready = sem("p_ready")
        p_stored = sem("p_stored")
        q_saved = sem("q_saved")
        idx_set = sem("idx_set")
        p_got = [sem(f"p_got{i}") for i in range(3)]
        p_put = [sem(f"p_put{i}") for i in range(3)]
        blk_got = [sem(f"blk_got{i}") for i in range(3)]
        blk_added = sem("blk_added")
        blk_gelu = sem("blk_gelu")
        blk_used = sem("blk_used")
        s_ready = sem("s_ready")
        bc_got = [sem(f"bc_got{i}") for i in range(4)]
        bc_hot = sem("bc_hot")
        look_done = sem("look_done")
        look_used = sem("look_used")
        final_ready = sem("final_ready")
        out_stored = sem("out_stored")

        block = ctx.enter_context(nc.Block())
        x_v = x.rearrange("(b p) f -> p b f", p=P)
        out_v = out.rearrange("(b p) f -> p b f", p=P)

        NPASS = 5
        PARTS = [3, 3, 3, 1, 1]
        KP = PB

        NSP_W = 18

        @block.sync
        def _(sp):
            sp.dma_start(dstS[0:HP, 0:HT], dst).then_inc(dst_loaded, 16)
            sp.dma_start(X[:], x_v).then_inc(x_loaded, 16)
            for t, a in ((wself_s[:], w_self), (wnb_s[:], w_nb), (w1_s[:, 0:HID], w1[0:F, :]),
                         (w1_s[:, HID:2 * HID], w1[F:2 * F, :]), (conv_s[:], conv_w), (wlin_s[:], w_lin_t),
                         (bias0[:, 0, :], b_self.broadcast_to([P, F])), (bias0[:, 1, :], b_nb.broadcast_to([P, F])),
                         (bias1[:, HID:2 * HID], b1.broadcast_to([P, HID])), (biasc[:], conv_b.broadcast_to([P, F])),
                         (gam_s[:], gamma.broadcast_to([P, F])), (bet_s[:], beta.broadcast_to([P, F])),
                         (wat_s[:], w_attn.broadcast_to([P, F])), (w2_s[:], w2.broadcast_to([P, HID])),
                         (b2_s[:], b2.broadcast_to([P, 1])), (rel_s[:, 0, :], rel[0:P, :]),
                         (rel_s[0:NREL - P, 1, :], rel[P:NREL, :])):
                sp.dma_start(t, a).then_inc(w_loaded, 16)
            sp.dma_start(idxA[:], src[0:EP, 0:1].rearrange("(c p t) o -> p c (t o)", p=P, t=GT)).then_inc(idx_loaded, 16)
            sp.wait_ge(lo_ready, 1)
            sp.dma_start(lo_dram.rearrange("k d e -> d k e"), bfE.rearrange("p (k q) s -> p k (q s)", q=2)).then_inc(lo_stored, 16)
            sp.wait_ge(lo_ready, 2)
            sp.dma_start(tl_dram.rearrange("k d e -> d k e"), bfT.rearrange("p (k q) s -> p k (q s)", q=2)).then_inc(lo_stored, 16)
            sp.wait_ge(p_ready, 1)
            sp.dma_start(p_tab.rearrange("(b p) f -> p b f", p=P), T1[:, :, 0:HID]).then_inc(p_stored, 16)
            flat = p_flat.rearrange("(c p t) f -> c p (t f)", p=P, t=GT)
            with sp.Fori(0, GC // 3) as i:
                for u in range(3):
                    sp.wait_ge(p_got[u], i * (16 * GT) + 16 * GT)
                    sp.dma_start(flat[bass.ds(i * 3 + u, 1), :, :].rearrange("c p f -> p (c f)"),
                                 PG[u].rearrange("p t f -> p (t f)")).then_inc(p_put[u], 16)
            sp.wait_ge(s_ready, 1)
            lod = lo_dram.rearrange("k (c d) e -> (k c) (d e)", d=CW)
            tld = tl_dram.rearrange("k (c d) e -> (k c) (d e)", d=CW)

            def broadcast(c, u):
                sp.dma_start(BC[2 * u], lod[bass.ds(c, 1), :].broadcast_to([P, CW * P])).then_inc(bc_got[2 * u], 16)
                sp.dma_start(BC[2 * u + 1], tld[bass.ds(c, 1), :].broadcast_to([P, CW * P])).then_inc(bc_got[2 * u + 1], 16)

            for u in range(2):
                broadcast(u, u)
            with sp.Fori(1, NCH // 2) as i:
                for u in range(2):
                    sp.wait_ge(bc_hot, i * 2 + (u - 1))
                    broadcast(i * 2 + u, u)
            sp.wait_ge(final_ready, 1)
            sp.dma_start(out_v, T1).then_inc(out_stored, 16)
            sp.wait_ge(out_stored, 16)

        @block.gpsimd
        def _(pool):
            made = [0]

            def made_one(ins):
                made[0] += 1
                ins.then_inc(const_made, 1)

            made_one(pool.iota(T1[:, 8:24, :].rearrange("p b f -> p (b f)").bitcast(I32), [[1, P], [0, CW]], base=0, channel_multiplier=0))
            made_one(pool.iota(slotI[:].bitcast(I32), [[1, SLOT]], base=0, channel_multiplier=0))
            made_one(pool.iota(iotaP[:].bitcast(I32), [[0, 1]], base=0, channel_multiplier=1))
            made_one(pool.memset(ones[:], 1.0))
            pool.wait_ge(const_made, 4)
            made_one(pool.affine_select(out=ident[:], in_=ones[:], compare_op=ALU.is_equal, fill=0.0,
                                        base=0, pattern=[[-1, P]], channel_multiplier=1))
            made_one(pool.affine_select(out=upper[:], in_=ones[:], compare_op=ALU.is_gt, fill=0.0,
                                        base=0, pattern=[[1, P]], channel_multiplier=-1))
            pool.wait_ge(row_ready, 1)
            for arr, dstt, s in ((src, srcE, src_rows), (eweight, ewE, ew_rows), (etype, typE, typ_rows)):
                for b in range(B):
                    pool.indirect_dma_start(out=dstt[:, b, :], out_offset=None, in_=arr,
                                            in_offset=bass.IndirectOffsetOnAxis(ap=rowI[:, b:b + 1], axis=0)).then_inc(s, 16)
            pool.wait_ge(idx_loaded, 16)
            pool.wait_ge(p_stored, 16)

            def gather(c, u, k):
                pool.tensor_copy(idxS[u][:], idxA[:, bass.ds(c, 1), :].rearrange("p c t -> p (c t)")).then_inc(idx_set, 1)
                pool.wait_ge(idx_set, k)
                pool.tensor_tensor(gate[:], ones[:, 0:1], ones[:, 0:1], ALU.mult)
                for t in range(GT):
                    pool.indirect_dma_start(out=PG[u][:, t, :], out_offset=None, in_=p_tab,
                                            in_offset=bass.IndirectOffsetOnAxis(ap=idxS[u][:, t:t + 1], axis=0)).then_inc(p_got[u], 16)

            for u in range(3):
                gather(u, u, u + 1)
            with pool.Fori(1, GC // 3) as i:
                for u in range(3):
                    pool.wait_ge(p_put[u], i * 16)
                    gather(i * 3 + u, u, i * 3 + (u + 1))
            for u in range(3):
                pool.wait_ge(p_put[u], 16 * (GC // 3))
            pool.wait_ge(q_saved, 1)
            for b in range(B):
                if b >= 3:
                    pool.wait_ge(blk_used, b - 2)
                pool.indirect_dma_start(out=GB[b % 3], out_offset=None, in_=p_flat,
                                        in_offset=bass.IndirectOffsetOnAxis(ap=rowI[:, b:b + 1], axis=0)).then_inc(blk_got[b % 3], 16)

        @block.scalar
        def _(act):
            cols = [0]

            def column(o, i, func, **kw):
                act.wait_ge(col_ready, cols[0] + 1)
                cols[0] += 1
                act.activation(o, i, func, **kw).then_inc(col_done, 1)

            turned = [0]

            def transposed(n):
                for j in range(NG * n):
                    k, w = turned[0], min(4, B - 4 * (j // n)) * P
                    act.wait_ge(tp_ready, k + 1)
                    act.copy(inT[:, k % 4, 0:w], bank[k % 2][:, 0:w]).then_inc(inT_ready, 1)
                    turned[0] += 1

            def one_pass(g):
                c0, k0 = g * NCH, g * PB

                def chunks(k, par, first):
                    for c in range(CPB):
                        act.wait_ge(chunk_built, k * CPB + (c0 + c + 1))
                        if c == 0 and not first:
                            act.wait_ge(spmm_done, k + (k0 - 1))
                        for q in range(2):
                            m = act.copy(STR[:, par, q, :, c * CW:(c + 1) * CW],
                                         bank[2 * (c % 2) + q][:, 0:CW * B].rearrange("p (d h) -> p h d", h=B))
                        m.then_inc(chunk_saved, 1)

                def agg(k, par):
                    act.wait_ge(spmm_done, k + (k0 + 1))
                    act.copy(AGG[:, bass.ds(k * 2, 2), :], bank[4 + par][:, 0:2 * F].rearrange("p (q f) -> p q f", q=2)).then_inc(agg_saved, 1)

                chunks(0, 0, True)
                chunks(1, 1, True)
                agg(0, 0)
                chunks(2, 0, False)
                agg(1, 1)
                with act.Fori(1, (PB - 1) // 2) as m:
                    chunks(m * 2 + 1, 1, False)
                    agg(m * 2, 0)
                    chunks(m * 2 + 2, 0, False)
                    agg(m * 2 + 1, 1)
                agg(PB - 1, 0)

            column(c2[:, 0:B], c1[:, 0:B], ACT.Sqrt)
            column(wE, wE, ACT.Exp)
            one_pass(0)
            column(c2[:, 0:B], c1[:, 0:B], ACT.Sqrt)
            transposed(2)
            column(c2[:, 0:B], c1[:, 0:B], ACT.Sqrt)
            column(c2[:, 0:B], c1[:, 0:B], ACT.Sqrt)
            column(c2[:, 0:B], c1[:, 0:B], ACT.Sqrt)
            transposed(1)
            for b in range(B):
                act.wait_ge(blk_added, b + 1)
                act.activation(GB[b % 3], GB[b % 3], ACT.Gelu).then_inc(blk_gelu, 1)
            column(wE[:, 0:B, :], wE[:, 0:B, :], ACT.Sigmoid, bias=b2_s[:, 0:1])
            column(c2[:, 0:B], c1[:, 0:B], ACT.Sqrt)
            one_pass(1)
            transposed(1)
            column(c2[:, 0:B], c1[:, 0:B], ACT.Sqrt)
            column(rT[:], rT[:], ACT.Sigmoid)
            one_pass(2)
            transposed(1)
            column(c2[:, 0:B], c1[:, 0:B], ACT.Sqrt)
            column(c2[:, 0:B], c1[:, 0:B], ACT.Sqrt)
            one_pass(3)
            one_pass(4)

        @block.tensor
        def _(pe):
            pe.wait_ge(const_made, 6)
            pe.wait_ge(zeros_made, 2)
            pe.matmul(bank[0][:, 0:B], zero_l, zero_r, start=True, stop=False, skip_group_check=True)
            with pe.Fori(0, HTP // CW // 4) as i:
                for u in range(4):
                    pe.wait_ge(hist_full, i * 4 + (u + 1))
                    for t in range(CW):
                        m = pe.matmul(bank[0][:, 0:B], LO[u][0:HP, :, t], HM[u][0:HP, 0:B, t],
                                      start=False, stop=False, skip_group_check=True)
                    m.then_inc(hist_used, 1)
            pe.matmul(bank[0][:, 0:B], zero_l, zero_r, start=False, stop=True, skip_group_check=True).then_inc(hist_done, 1)
            pe.wait_ge(deg_ready, 1)
            pe.matmul(bank[1][:, 0:B], upper[:], deg[:, 0:B], start=True, stop=True)
            pe.matmul(bank[1][:, 32:32 + B], ones[:], deg[:, 0:B], start=True, stop=True).then_inc(prefix_done, 1)

            turns = [0]

            def turn(t):
                pe.wait_ge(tin_ready, turns[0] + 1)
                if turns[0]:
                    pe.wait_ge(tout_used, turns[0])
                for k in range(PB):
                    m = pe.transpose(bank[k // 4][:, (k % 4) * P:(k % 4 + 1) * P],
                                     t[:, 2 * k:2 * k + 2, :].rearrange("p q s -> p (q s)"), ident[:])
                m.then_inc(tout_ready, 1)
                turns[0] += 1

            lins = [0, 0, 0]

            def linear(pairs):
                lins[0] += 1
                pe.wait_ge(lin_in, lins[0])
                n = len(pairs)
                for j in range(NG * n + 1):
                    if j < NG * n:
                        k = lins[1] + j
                        if k >= 2:
                            pe.wait_ge(inT_ready, k - 1)
                        for i, b in enumerate(range(4 * (j // n), min(4 * (j // n) + 4, B))):
                            m = pe.transpose(bank[k % 2][:, i * P:(i + 1) * P], pairs[j % n][0][:, b, :], ident[:])
                        m.then_inc(tp_ready, 1)
                    if j >= 1:
                        g, i = divmod(j - 1, n)
                        k, o = lins[1] + j - 1, lins[2] + g
                        if i < n - 1:
                            continue
                        pe.wait_ge(inT_ready, k + 1)
                        if o >= 2:
                            pe.wait_ge(lin_taken, o - 1)
                        for c in range(min(4, B - 4 * g)):
                            for i in range(n):
                                m = pe.matmul(bank[2 + o % 2][:, c * P:(c + 1) * P],
                                              inT[:, (k - n + 1 + i) % 4, c * P:(c + 1) * P],
                                              pairs[i][1], start=(i == 0), stop=(i == n - 1))
                        m.then_inc(lin_ready, 1)
                lins[1] += NG * n
                lins[2] += NG

            def one_pass(g):
                c0, k0, parts = g * NCH, g * PB, PARTS[g]
                pe.wait_ge(pass_in, g + 1)

                def columns(k, first):
                    for c in range(CPB):
                        pe.wait_ge(hot_full, k * CPB + (c0 + c + 1))
                        if not (first and c < 2):
                            pe.wait_ge(chunk_saved, k * CPB + (c0 + c - 1))
                        for i in range(CW):
                            for q in range(2):
                                rows = slice(q * SLOT, (q + 1) * SLOT)
                                for w in range(parts):
                                    m = pe.matmul(bank[2 * (c % 2) + q][:, i * B:(i + 1) * B],
                                                  LO[c % 4][rows, :, i], HW[c % 4][rows, w, :, i],
                                                  start=(w == 0), stop=(w == parts - 1))
                        m.then_inc(chunk_built, 1)

                def product(k, par, first):
                    pe.wait_ge(chunk_saved, k * CPB + (c0 + CPB))
                    if not first:
                        pe.wait_ge(agg_saved, k + (k0 - 1))
                    for q in range(2):
                        for h in range(B):
                            m = pe.matmul(bank[4 + par][:, q * F:(q + 1) * F], STR[:, par, q, h, :], TB[:, h, :],
                                          start=(h == 0), stop=(h == B - 1))
                    m.then_inc(spmm_done, 1)

                columns(0, g == 0)
                columns(1, False)
                product(0, 0, True)
                columns(2, False)
                product(1, 1, True)
                with pe.Fori(1, (PB - 1) // 2) as m:
                    columns(m * 2 + 1, False)
                    product(m * 2, 0, False)
                    columns(m * 2 + 2, False)
                    product(m * 2 + 1, 1, False)
                product(PB - 1, 0, False)

            turn(tmpE)
            turn(tmpE)
            turn(maskE)
            turn(wE)
            one_pass(0)
            linear([(Hn, wself_s[:]), (AGG, wnb_s[:])])
            turn(tmpE)
            linear([(Hn, w1_s[:])])
            turn(wE)
            one_pass(1)
            linear([(AGG, conv_s[:])])
            pe.wait_ge(s_ready, 1)

            def look_up(c, u, first):
                pe.wait_ge(bc_hot, c + 1)
                if not first:
                    pe.wait_ge(look_used, c - 1)
                for i in range(CW):
                    for t, tab, w, n in ((LS[2 * u], stab, 0, B), (LS[2 * u + 1], rtab, B, 2)):
                        for k in range(3):
                            m = pe.matmul(bank[u][:, i * VN + w:i * VN + w + n], t[:, i * P:(i + 1) * P], tab[:, k, :],
                                          start=(k == 0), stop=(k == 2))
                m.then_inc(look_done, 1)

            for u in range(2):
                look_up(u, u, True)
            with pe.Fori(1, NCH // 2) as i:
                for u in range(2):
                    look_up(i * 2 + u, u, False)
            one_pass(2)
            linear([(AGG, wlin_s[:])])
            one_pass(3)
            one_pass(4)

        @block.vector
        def _(v):
            n = [0, 0]

            def link(ins):
                n[0] += 1
                ins.then_inc(dve_step, 1)
                v.wait_ge(dve_step, n[1] + n[0])

            def tt(o, a, b, op):
                link(v.tensor_tensor(o, a, b, op))

            def ts(o, a, s1, s2, op0, op1=ALU.bypass):
                link(v.tensor_scalar(o, a, s1, s2, op0, op1) if s2 is not None else v.tensor_scalar(o, a, s1, None, op0))

            def red(o, a, op):
                link(v.tensor_reduce(o, a, AX.X, op))

            def bcb(c):
                return c[:, :, None].broadcast_to([P, B, F])

            def row(r):
                return r[:, None, :].broadcast_to([P, B, F])

            cols = [0]

            def ask_column():
                cols[0] += 1
                v.wait_ge(col_done, cols[0])

            def rstd(scale, add):
                n[0] += 1
                v.tensor_scalar(c1[:, 0:B], c1[:, 0:B], scale, add, ALU.mult, ALU.add).then_inc(dve_step, 1)
                v.wait_ge(dve_step, n[1] + n[0])
                v.nop().then_inc(col_ready, 1)
                ask_column()
                link(v.reciprocal(c2[:, 0:B], c2[:, 0:B]))

            def ask(ins):
                link(ins)
                v.nop().then_inc(col_ready, 1)
                ask_column()

            def centred(o, i):
                red(c3[:, 0:B], i, ALU.add)
                ts(c3[:, 0:B], c3[:, 0:B], 1.0 / F, None, ALU.mult)
                tt(o, i, bcb(c3[:, 0:B]), ALU.subtract)
                tt(T2, o, o, ALU.mult)
                red(c1[:, 0:B], T2, ALU.add)

            def norm_in():
                centred(Hn[:], X[:])
                rstd(1.0 / F, LN_EPS)
                link(v.scalar_tensor_tensor(out=Hn[:], in0=Hn[:], scalar=0.0, in1=bcb(c2[:, 0:B]),
                                            op0=ALU.max, op1=ALU.mult))

            v.memset(zero_l, 0.0).then_inc(zeros_made, 1)
            v.memset(zero_r, 0.0).then_inc(zeros_made, 1)
            link(v.memset(dlo, -1.0))
            link(v.memset(dhi, -1.0))
            v.wait_ge(const_made, 3)
            link(v.tensor_copy(iotaLo[:].rearrange("p a b -> p (a b)"), T1[:, 8:24, :].rearrange("p b f -> p (b f)").bitcast(I32)))
            link(v.tensor_copy(iotaHi[:], iotaLo[:, 0:VN, :]))
            link(v.tensor_copy(slotI[:], slotI[:].bitcast(I32)))
            link(v.tensor_copy(iotaP[:], iotaP[:].bitcast(I32)))

            v.wait_ge(dst_loaded, 16)
            ts(dloI[0:HP, 0:HT], dstS[0:HP, 0:HT], P - 1, None, ALU.bitwise_and)
            ts(dstS[0:HP, 0:HT], dstS[0:HP, 0:HT], 7, None, ALU.logical_shift_right)
            link(v.tensor_copy(dlo[0:HP, 0:HT], dloI[0:HP, 0:HT]))
            link(v.tensor_copy(dhi[0:HP, 0:HT], dstS[0:HP, 0:HT]))

            def hist(c, u, wait):
                if wait is not None:
                    v.wait_ge(hist_used, wait)
                v.tensor_tensor(LO[u][0:HP], dlo[0:HP, None, bass.ds(c * CW, CW)].broadcast_to([HP, P, CW]),
                                iotaLo[0:HP], ALU.is_equal)
                v.tensor_tensor(HM[u][0:HP, 0:B, :], dhi[0:HP, None, bass.ds(c * CW, CW)].broadcast_to([HP, B, CW]),
                                iotaHi[0:HP, 0:B, :], ALU.is_equal).then_inc(hist_full, 1)

            for u in range(4):
                hist(u, u, None)
            with v.Fori(1, HTP // CW // 4) as i:
                for u in range(4):
                    hist(i * 4 + u, u, i * 4 + (u - 3))
            v.wait_ge(hist_done, 1)
            link(v.memset(deg[:], 0.0))
            v.tensor_copy(deg[:, 0:B], bank[0][:, 0:B]).then_inc(deg_ready, 1)
            v.wait_ge(deg_ready, 1)
            v.wait_ge(prefix_done, 1)
            link(v.tensor_copy(tot[:], bank[1][:, 32:32 + B]))
            link(v.tensor_tensor_scan(scn[:], tot[:], tot[:], 0.0, ALU.add, ALU.bypass))
            tt(scn[:], scn[:], tot[:], ALU.subtract)
            tt(rowf[:], scn[:], bank[1][:, 0:B], ALU.add)
            v.tensor_copy(rowI[:], rowf[:]).then_inc(row_ready, 1)
            tt(maskE[:], slotI[:, None, :].broadcast_to([P, BE, SLOT]), deg[:, :, None].broadcast_to([P, BE, SLOT]), ALU.is_lt)

            v.wait_ge(x_loaded, 16)
            norm_in()
            link(v.tensor_copy(TB[:], Hn[:]))

            turns = [0]

            def turned(fn):
                turns[0] += 1
                v.wait_ge(tout_ready, turns[0])
                for b4 in range(4):
                    w = min(512, PB * P - b4 * 512)
                    fn(slice(b4 * 512, b4 * 512 + w), bank[b4][:, 0:w])
                v.nop().then_inc(tout_used, 1)

            def turn_in():
                v.nop().then_inc(tin_ready, 1)

            def split3(cols, a):
                link(v.tensor_copy(wT[0][:, cols], a))
                tt(rT[:, cols], a, wT[0][:, cols], ALU.subtract)
                link(v.tensor_copy(wT[1][:, cols], rT[:, cols]))
                tt(rT[:, cols], rT[:, cols], wT[1][:, cols], ALU.subtract)
                link(v.tensor_copy(wT[2][:, cols], rT[:, cols]))

            v.wait_ge(src_rows, 16 * B)
            link(v.memset(srcE[:, B:BE, :], 0))
            ts(tmpI, srcE[:], P - 1, None, ALU.bitwise_and)
            link(v.tensor_copy(tmpE, tmpI))
            turn_in()
            link(v.tensor_copy(bfE, tmpI))
            v.nop().then_inc(lo_ready, 1)
            turned(lambda c, a: link(v.tensor_copy(loT[:, c], a)))
            ts(tmpI, srcE[:], 7, None, ALU.logical_shift_right)
            link(v.tensor_copy(tmpE, tmpI))
            turn_in()
            turned(lambda c, a: link(v.tensor_copy(hiT[:, c], a)))
            turn_in()
            turned(lambda c, a: link(v.tensor_copy(mT[:, c], a)))
            v.wait_ge(typ_rows, 16 * B)
            link(v.memset(typE[:, B:BE, :], 0))
            ts(tmpI, typE[:], P - 1, None, ALU.bitwise_and)
            link(v.tensor_copy(bfT, tmpI))
            v.nop().then_inc(lo_ready, 1)
            v.wait_ge(lo_stored, 32)

            v.wait_ge(ew_rows, 16 * B)
            link(v.memset(ewE[:, B:BE, :], 0.0))
            ts(tmpE, maskE[:], 1.0, BIG, ALU.subtract, ALU.mult)
            tt(wE, ewE[:], maskE[:], ALU.mult)
            tt(wE, wE, tmpE, ALU.add)
            red(c1[:], wE, ALU.max)
            ask(v.tensor_tensor(wE, wE, c1[:, :, None].broadcast_to([P, BE, SLOT]), ALU.subtract))
            tt(wE, wE, maskE[:], ALU.mult)
            turn_in()
            red(c4[:], wE, ALU.add)
            ts(c4[:], c4[:], 1e-30, None, ALU.max)
            link(v.reciprocal(c4[:], c4[:]))
            turned(split3)

            def one_pass(g):
                c0, parts = g * NCH, PARTS[g]
                weights = wT if g < 3 else [mT]
                v.nop().then_inc(pass_in, 1)

                def chunk(k, c, first, step):
                    at = bass.ds(k * P + c * CW, CW)
                    u = c % 4
                    if not (first and c < 4):
                        v.wait_ge(chunk_built, k * CPB + (c0 + c - 3))
                    v.tensor_tensor(HM[u][:, 0:B, :], hiT[:, None, at].broadcast_to([P, B, CW]),
                                    iotaHi[:, 0:B, :], ALU.is_equal).then_inc(dve_step, 1)
                    v.tensor_tensor(LO[u][:], loT[:, None, at].broadcast_to([P, P, CW]), iotaLo[:], ALU.is_equal)
                    v.wait_ge(dve_step, step)
                    for w in range(parts):
                        m = v.tensor_tensor(HW[u][:, w, :, :], HM[u][:, 0:B, :],
                                            weights[w][:, None, at].broadcast_to([P, B, CW]), ALU.mult)
                    m.then_inc(hot_full, 1)

                for c in range(CPB):
                    chunk(0, c, g == 0, n[0] + c + 1)
                with v.Fori(1, PB) as k:
                    for c in range(CPB):
                        chunk(k, c, False, k * CPB + (n[0] + c + 1))
                n[0] += NCH
                v.wait_ge(agg_saved, (g + 1) * PB)

            outs = [0]

            def linear(o, bias):
                v.nop().then_inc(lin_in, 1)
                for g in range(NG):
                    k, m = outs[0], min(4, B - 4 * g)
                    v.wait_ge(lin_ready, k + 1)
                    got = bank[2 + k % 2][:, 0:m * P].rearrange("p (b f) -> p b f", f=F)
                    if bias is None:
                        i = v.tensor_copy(o[:, 4 * g:4 * g + m, :], got)
                    else:
                        i = v.tensor_tensor(o[:, 4 * g:4 * g + m, :], got, bias[:, None, :].broadcast_to([P, m, F]), ALU.add)
                    i.then_inc(lin_taken, 1)
                    outs[0] += 1
                v.wait_ge(lin_taken, outs[0])

            A = AGG[:, 0:B, :]
            one_pass(0)
            tt(A, A, bcb(c4[:, 0:B]), ALU.mult)
            tt(T2, A, A, ALU.mult)
            red(c1[:, 0:B], T2, ALU.add)
            v.nop().then_inc(col_ready, 1)
            ask_column()
            ts(c2[:, 0:B], c2[:, 0:B], EPS, None, ALU.add)
            link(v.reciprocal(c2[:, 0:B], c2[:, 0:B]))
            tt(A, A, bcb(c2[:, 0:B]), ALU.mult)
            v.wait_ge(w_loaded, 16 * 17)
            tt(bias0[:, 0, :], bias0[:, 0, :], bias0[:, 1, :], ALU.add)
            linear(T1, bias0[:, 0, :])
            ts(T1, T1, 0.5, None, ALU.mult)
            tt(T2, T1, T1, ALU.mult)
            red(c1[:, 0:B], T2, ALU.add)
            v.nop().then_inc(col_ready, 1)
            ask_column()
            ts(c2[:, 0:B], c2[:, 0:B], EPS, None, ALU.add)
            link(v.reciprocal(c2[:, 0:B], c2[:, 0:B]))
            tt(T1, T1, bcb(c2[:, 0:B]), ALU.mult)
            centred(T1, T1)
            rstd(1.0 / F, LN_EPS)
            tt(T1, T1, bcb(c2[:, 0:B]), ALU.mult)
            tt(T1, T1, row(gam_s[:]), ALU.mult)
            tt(T1, T1, row(bet_s[:]), ALU.add)
            tt(X[:], X[:], T1, ALU.add)

            ts(tmpI, typE[:], 7, None, ALU.logical_shift_right)
            link(v.tensor_copy(tmpE, tmpI))
            turn_in()
            turned(lambda c, a: link(v.tensor_scalar(thT[:, c], a, float(B), None, ALU.add)))
            norm_in()
            link(v.memset(bias1[:, 0:HID], 0.0))
            linear(T1, bias1[:])
            v.nop().then_inc(p_ready, 1)
            link(v.tensor_copy(AGG[:, 0:B, 0:HID], T1[:, :, HID:2 * HID]))
            v.nop().then_inc(q_saved, 1)
            v.wait_ge(p_stored, 16)
            link(v.memset(wE, 0.0))
            for b in range(B):
                g3 = GB[b % 3].rearrange("p (s f) -> p s f", f=HID)
                v.wait_ge(blk_got[b % 3], 16 * (b // 3 + 1))
                v.tensor_tensor(g3, g3, AGG[:, b, None, 0:HID].broadcast_to([P, SLOT, HID]), ALU.add).then_inc(blk_added, 1)
                if b >= 1:
                    mlp_out(v, link, blk_gelu, blk_used, GB, w2_s, wE, b - 1)
            mlp_out(v, link, blk_gelu, blk_used, GB, w2_s, wE, B - 1)
            v.nop().then_inc(col_ready, 1)
            ask_column()
            tt(wE, wE, maskE[:], ALU.mult)
            turn_in()
            red(c1[:], wE, ALU.add)
            rstd(1.0, 1.0)
            link(v.tensor_copy(dinv[:], c2[:, 0:B]))
            tt(TB[:], Hn[:], bcb(dinv[:]), ALU.mult)
            turned(split3)
            one_pass(1)
            tt(A, A, TB[:], ALU.add)
            tt(A, A, bcb(dinv[:]), ALU.mult)
            linear(T1, biasc[:])
            tt(X[:], X[:], T1, ALU.add)

            norm_in()
            tt(T1, Hn[:], row(wat_s[:]), ALU.mult)
            red(c3[:, 0:B], T1, ALU.add)
            tt(T2[:, 0, :], rel_s[:, 0, :], wat_s[:], ALU.mult)
            red(rcol[:, 0:1], T2[:, 0, :], ALU.add)
            link(v.memset(rcol[:, 1:2], 0.0))
            tt(T2[0:NREL - P, 1, :], rel_s[0:NREL - P, 1, :], wat_s[0:NREL - P, :], ALU.mult)
            red(rcol[0:NREL - P, 1:2], T2[0:NREL - P, 1, :], ALU.add)
            for tab, col in ((stab, c3[:, 0:B]), (rtab, rcol[:])):
                for k in range(3):
                    link(v.tensor_copy(tab[:, k, :], col))
                    if k < 2:
                        tt(col, col, tab[:, k, :], ALU.subtract)
            v.nop().then_inc(s_ready, 1)

            def hot(c, u, k, first):
                for j in range(2):
                    v.wait_ge(bc_got[2 * u + j], k * 16)
                if not first:
                    v.wait_ge(look_done, c - 1)
                v.tensor_scalar(LS[2 * u], BC[2 * u], iotaP[:, 0:1], None, ALU.is_equal)
                v.tensor_scalar(LS[2 * u + 1], BC[2 * u + 1], iotaP[:, 0:1], None, ALU.is_equal).then_inc(bc_hot, 1)

            def pick(c, u, at, step):
                v.tensor_tensor(HM[u][:, 0:B, :], hiT[:, None, at].broadcast_to([P, B, CW]), iotaHi[:, 0:B, :], ALU.is_equal)
                v.tensor_tensor(HM[u][:, B:VN, :], thT[:, None, at].broadcast_to([P, 2, CW]), iotaHi[:, B:VN, :],
                                ALU.is_equal).then_inc(dve_step, 1)
                v.wait_ge(dve_step, step + 1)
                v.wait_ge(look_done, c + 1)
                v.tensor_tensor(VP[:], bank[u][:, 0:CW * VN].rearrange("p (i h) -> p h i", h=VN), HM[u][:], ALU.mult).then_inc(dve_step, 1)
                v.wait_ge(dve_step, step + 2)
                v.tensor_reduce(rT[:, at], VP[:].rearrange("p h i -> p i h"), AX.X, ALU.add).then_inc(dve_step, 1)
                v.wait_ge(dve_step, step + 3)
                v.nop().then_inc(look_used, 1)

            hot(0, 0, 1, True)
            hot(1, 1, 1, True)
            pick(0, 0, bass.ds(0, CW), n[0])
            with v.Fori(1, NCH // 2) as i:
                hot(i * 2, 0, i + 1, False)
                pick(i * 2 - 1, 1, bass.ds(i * (2 * CW) - CW, CW), i * 6 + (n[0] - 3))
                hot(i * 2 + 1, 1, i + 1, False)
                pick(i * 2, 0, bass.ds(i * (2 * CW), CW), i * 6 + n[0])
            pick(NCH - 1, 1, bass.ds((NCH - 1) * CW, CW), n[0] + 3 * (NCH - 1))
            n[0] += 3 * NCH
            v.nop().then_inc(col_ready, 1)
            ask_column()
            tt(rT[:], rT[:], mT[:], ALU.mult)
            link(v.tensor_copy(wT[0][:], rT[:]))
            tt(rT[:], rT[:], wT[0][:], ALU.subtract)
            link(v.tensor_copy(wT[1][:], rT[:]))
            tt(rT[:], rT[:], wT[1][:], ALU.subtract)
            link(v.tensor_copy(wT[2][:], rT[:]))
            link(v.tensor_copy(TB[:], Hn[:]))
            one_pass(2)
            linear(T1, None)
            link(v.scalar_tensor_tensor(out=X[:], in0=T1, scalar=0.0, in1=X[:], op0=ALU.max, op1=ALU.add))

            norm_in()
            ts(c1[:, 0:B], deg[:, 0:B], 1.0, None, ALU.max)
            v.nop().then_inc(col_ready, 1)
            ask_column()
            link(v.reciprocal(c2[:, 0:B], c2[:, 0:B]))
            ts(c3[:, 0:B], deg[:, 0:B], 1.0, None, ALU.min)
            tt(dis[:], c2[:, 0:B], c3[:, 0:B], ALU.mult)
            tt(TB[:], Hn[:], bcb(dis[:]), ALU.mult)
            one_pass(3)
            tt(A, A, bcb(dis[:]), ALU.mult)
            tt(Hn[:], Hn[:], A, ALU.add)
            tt(TB[:], A, bcb(dis[:]), ALU.mult)
            one_pass(4)
            tt(A, A, bcb(dis[:]), ALU.mult)
            tt(Hn[:], Hn[:], A, ALU.add)
            link(v.scalar_tensor_tensor(out=T1, in0=Hn[:], scalar=1.0 / 3.0, in1=X[:], op0=ALU.mult, op1=ALU.add))
            v.nop().then_inc(final_ready, 1)


_INS = [("x", "x"), ("src", "src"), ("dst", "dst"), ("etype", "edge_type_200"), ("eweight", "edge_weight"),
        ("w_self", "L0_gnn_W_self"), ("b_self", "L0_gnn_b_self"), ("w_nb", "L0_gnn_W_nb"), ("b_nb", "L0_gnn_b_nb"),
        ("gamma", "L0_gnn_gamma"), ("beta", "L0_gnn_beta"), ("w1", "L1_gnn_mlp_w1"), ("b1", "L1_gnn_mlp_b1"),
        ("w2", "L1_gnn_mlp_w2"), ("b2", "L1_gnn_mlp_b2"), ("conv_w", "L1_gnn_conv_w"), ("conv_b", "L1_gnn_conv_b"),
        ("rel", "L2_gnn_rel_emb"), ("w_lin_t", "L2_gnn_W_lin"), ("w_attn", "L2_gnn_W_attn")]


def kernel(**inputs):
    import numpy as np
    import concourse.bacc as bacc
    from concourse.bass_utils import run_bass_kernel_spmd

    a = {short: np.asarray(inputs[name]) for short, name in _INS}
    a["x"] = np.concatenate([a["x"], np.zeros((B * P - N, F), a["x"].dtype)])
    for k in ("src", "etype", "eweight"):
        a[k] = np.concatenate([a[k], np.zeros(EP - E, a[k].dtype)]).reshape(EP, 1)
    a["dst"] = a["dst"].reshape(HP, HT)
    a["w_lin_t"] = a["w_lin_t"].T
    for k in ("b_self", "b_nb", "gamma", "beta", "b1", "w2", "b2", "conv_b", "w_attn"):
        a[k] = a[k].reshape(1, -1)
    a = {f"{k}_dram": np.ascontiguousarray(v) for k, v in a.items()}
    nc = bacc.Bacc("TRN2", target_bir_lowering=False, num_devices=1)
    args = [nc.dram_tensor(k, v.shape, mybir.dt.from_np(v.dtype), kind="ExternalInput").ap() for k, v in a.items()]
    out = nc.dram_tensor("out_dram", (B * P, F), F32, kind="ExternalOutput").ap()
    build(nc, *args, out)
    r = run_bass_kernel_spmd(nc, [a], core_ids=[0])
    return r.results[0]["out_dram"][:N]
```

```python
from contextlib import ExitStack

import concourse.bass as bass
from concourse import mybir

F32 = mybir.dt.float32
BF16 = mybir.dt.bfloat16
I32 = mybir.dt.int32
ALU = mybir.AluOpType
ACT = mybir.ActivationFunctionType
AX = mybir.AxisListType

P = 128
N = 3125
F = 128
HID = 64
NREL = 200
E = 103125
B = (N + P - 1) // P
SLOT = 64
NG = -(-B // 4)
PB = (B + 1) // 2
BE = 2 * PB
CW = 16
CPB = P // CW
NCH = PB * CPB
HP, HT = 125, 825
HTP = 832
GT = 16
GC = -(-(E + SLOT) // (P * GT))
EP = GC * P * GT
ST = EP // P
AW = F + 4
AR = B * P + P
B2 = 2 * B
VN = B + 2
LN_EPS = 1e-5
EPS = 1e-9
BIG = 1e30


def mlp_out(v, link, blk_gelu, blk_used, GB, w2_s, wE, b):
    g3 = GB[b % 3].rearrange("p (s f) -> p s f", f=HID)
    v.wait_ge(blk_gelu, b + 1)
    link(v.tensor_tensor(g3, g3, w2_s[:, None, :].broadcast_to([P, SLOT, HID]), ALU.mult))
    link(v.tensor_reduce(wE[:, b, :], g3, AX.X, ALU.add))
    v.nop().then_inc(blk_used, 1)


def build(nc, x, src, dst, etype, eweight, w_self, b_self, w_nb, b_nb, gamma, beta,
          w1, b1, w2, b2, conv_w, conv_b, rel, w_lin_t, w_attn, out):
    ctx = ExitStack()
    with ctx:
        def sb(name, shape, dt=F32):
            return ctx.enter_context(nc.sbuf_tensor(name, shape, dt))

        def sem(name):
            return ctx.enter_context(nc.semaphore(name))

        X = sb("X", [P, B, F])
        Hn = sb("Hn", [P, B, F])
        TB = sb("TB", [P, B, F])
        AGG = sb("AGG", [P, BE, F])
        STR = sb("STR", [P, 2, 2, B, P])
        stream = STR[:].rearrange("p a q h d -> p (a q h d)")
        T1 = stream[:, 0:B * F].rearrange("p (b f) -> p b f", f=F)
        T2 = stream[:, B * F:2 * B * F].rearrange("p (b f) -> p b f", f=F)
        STC = stream[:, 0:B2 * P].bitcast(BF16).rearrange("p (a x d) -> p a x d", a=2, x=B2)
        TB3 = stream[:, B2 * P:B2 * P + 3 * B * F // 2].bitcast(BF16).rearrange("p (b w f) -> p b w f", w=3, f=F)
        inT = stream[:, 2 * B * F:2 * B * F + 4 * 4 * P].rearrange("p (a n) -> p a n", a=4)
        GB = [stream[:, i * SLOT * HID:(i + 1) * SLOT * HID] for i in range(3)]
        BC = [stream[:, i * 1024:(i + 1) * 1024].bitcast(BF16) for i in range(4)]
        srcE = sb("srcE", [P, BE, SLOT], I32)
        typE = sb("typE", [P, BE, SLOT], I32)
        ewE = sb("ewE", [P, BE, SLOT])
        maskE = sb("maskE", [P, BE, SLOT])
        wE = srcE[:].bitcast(F32)
        loT = sb("loT", [P, PB * P], BF16)
        hiT = sb("hiT", [P, PB * P], BF16)
        thT = sb("thT", [P, PB * P], BF16)
        W3 = sb("W3", [P, 3, PB * P], BF16)
        wT = [W3[:, i, :] for i in range(3)]
        mT = sb("mT", [P, PB * P], BF16)
        rT = sb("rT", [P, PB * P])
        LO = [sb(f"LO{i}", [P, P, CW], BF16) for i in range(4)]
        HM = [sb(f"HM{i}", [P, B2, CW], BF16) for i in range(2)]
        HW = [sb(f"HW{i}", [P, 3, B2, CW], BF16) for i in range(2)]
        HH = [HW[i // 2][:, i % 2, 0:B, :] for i in range(4)]
        VP = sb("VP", [P, VN, CW])
        PG = [LO[i][:].rearrange("p a b -> p (a b)").bitcast(F32).rearrange("p (t f) -> p t f", f=HID)
              for i in range(3)]
        LS = [LO[i][:].rearrange("p a b -> p (a b)") for i in range(4)]
        iotaLo = sb("iotaLo", [P, P, CW], BF16)
        iotaHi = sb("iotaHi", [P, VN, CW], BF16)
        iotaP = sb("iotaP", [P, 1])
        halfB = sb("halfB", [P, 1])
        slotI = sb("slotI", [P, SLOT])
        ident = sb("ident", [P, P])
        upper = sb("upper", [P, P])
        ones = sb("ones", [P, P])
        wself_s = sb("wself_s", [F, F])
        wnb_s = sb("wnb_s", [F, F])
        w1_s = sb("w1_s", [F, 2 * HID])
        conv_s = sb("conv_s", [F, F])
        wlin_s = sb("wlin_s", [F, F])
        bias0 = sb("bias0", [P, 2, F])
        bias1 = sb("bias1", [P, 2 * HID])
        biasc = sb("biasc", [P, F])
        gam_s = sb("gam_s", [P, F])
        bet_s = sb("bet_s", [P, F])
        wat_s = sb("wat_s", [P, F])
        w2_s = sb("w2_s", [P, HID])
        b2_s = sb("b2_s", [P, 1])
        rel_s = sb("rel_s", [P, 2, F])
        dstS = T2[:, 0:7, :].rearrange("p b f -> p (b f)")[:, 0:HTP].bitcast(I32)
        dnext = AGG[:, 0:7, :].rearrange("p b f -> p (b f)")[:, 0:HT].bitcast(I32)
        ddiff = AGG[:, 7:14, :].rearrange("p b f -> p (b f)")[:, 0:HT]
        dloI = T2[:, 7:14, :].rearrange("p b f -> p (b f)")[:, 0:HTP].bitcast(I32)
        dlo = T1[:, 0:4, :].rearrange("p b f -> p (b f)").bitcast(BF16)[:, 0:HTP]
        dhi = T1[:, 4:8, :].rearrange("p b f -> p (b f)").bitcast(BF16)[:, 0:HTP]
        tmpE = T1[:, 0:13, :].rearrange("p b f -> p (b f)").rearrange("p (b s) -> p b s", s=SLOT)
        tmpI = T2[:, 0:13, :].rearrange("p b f -> p (b f)").bitcast(I32).rearrange("p (b s) -> p b s", s=SLOT)
        bfE = T1[:, 13:20, :].rearrange("p b f -> p (b f)").bitcast(BF16)[:, 0:BE * SLOT].rearrange(
            "p (b s) -> p b s", s=SLOT)
        bfT = T2[:, 13:20, :].rearrange("p b f -> p (b f)").bitcast(BF16)[:, 0:BE * SLOT].rearrange(
            "p (b s) -> p b s", s=SLOT)
        deg = sb("deg", [P, BE])
        tot = sb("tot", [P, B])
        scn = sb("scn", [P, B])
        rowf = sb("rowf", [P, B])
        rowI = sb("rowI", [P, B], I32)
        c1 = sb("c1", [P, BE])
        c2 = sb("c2", [P, BE])
        c3 = sb("c3", [P, BE])
        c4 = sb("c4", [P, BE])
        flagI = sb("flagI", [1, 1], I32)
        bad = sb("bad", [P, 4])
        dinv = sb("dinv", [P, B])
        dis = sb("dis", [P, B])
        stab = sb("stab", [P, 3, B], BF16)
        rtab = sb("rtab", [P, 3, 2], BF16)
        rcol = sb("rcol", [P, 2])
        idxA = sb("idxA", [P, GC, GT], I32)
        idxS = [sb(f"idxS{i}", [P, GT], I32) for i in range(3)]

        zero_l = sb("zero_l", [1, P], BF16)[:]
        zero_r = sb("zero_r", [1, B], BF16)[:]
        bank = [ctx.enter_context(nc.psum_tensor(f"bank{i}", [P, 512], F32)) for i in range(8)]

        gsrc, gdst, gtyp = (t[:].bitcast(I32)[:, 0:ST] for t in (loT, hiT, thT))
        gdstF, gwF, gew = (t.bitcast(F32)[:, 0:ST] for t in (wT[0], wT[2], mT[:]))
        gadj = wT[1].bitcast(I32)[:, 0:ST]
        LOf = [LO[i][:].rearrange("p a b -> p (a b)").bitcast(F32) for i in range(4)]
        gA, gB, gM, gMx = (LOf[0][:, i * P:(i + 1) * P] for i in range(4))
        gG, gO = LOf[1][:, 0:AW], LOf[1][:, AW:2 * AW]
        gPQ = LOf[1][:, 2 * AW:2 * AW + 2 * HID]
        gLow = LOf[2][:, 0:P]
        gc = LOf[2][:, P:P + 16]
        gi = LOf[2][:, P + 16:P + 20].bitcast(I32)
        zeros = stream[:, 0:AR * AW // P]

        p_tab = nc.dram_tensor("p_tab", (B * P, HID), F32).ap()
        p_flat = nc.dram_tensor("p_flat", (EP, HID), F32).ap()
        lo_dram = nc.dram_tensor("lo_dram", (PB, P, P), BF16).ap()
        tl_dram = nc.dram_tensor("tl_dram", (PB, P, P), BF16).ap()

        q_tab = nc.dram_tensor("q_tab", (B * P, HID), F32).ap()
        tab = nc.dram_tensor("tab", (B * P, F), F32).ap()
        acc = nc.dram_tensor("acc", (AR, AW), F32).ap()
        seg = nc.dram_tensor("seg", (AR, 1), F32).ap()
        s_tab = nc.dram_tensor("s_tab", (B * P, 1), F32).ap()
        r_tab = nc.dram_tensor("r_tab", (2 * P, 1), F32).ap()

        strips = nc.dram_tensor("strips", (PB, P, B2 * P), BF16).ap()

        x_loaded = sem("x_loaded")
        dst_loaded = sem("dst_loaded")
        w_loaded = sem("w_loaded")
        idx_loaded = sem("idx_loaded")
        const_made = sem("const_made")
        dve_step = sem("dve_step")
        zeros_made = sem("zeros_made")
        hist_full = sem("hist_full")
        hist_used = sem("hist_used")
        hist_done = sem("hist_done")
        deg_ready = sem("deg_ready")
        prefix_done = sem("prefix_done")
        row_ready = sem("row_ready")
        src_rows = sem("src_rows")
        ew_rows = sem("ew_rows")
        typ_rows = sem("typ_rows")
        tin_ready = sem("tin_ready")
        tout_ready = sem("tout_ready")
        tout_used = sem("tout_used")
        lo_ready = sem("lo_ready")
        lo_stored = sem("lo_stored")
        col_ready = sem("col_ready")
        col_done = sem("col_done")
        lin_in = sem("lin_in")
        tp_ready = sem("tp_ready")
        inT_ready = sem("inT_ready")
        lin_ready = sem("lin_ready")
        lin_taken = sem("lin_taken")
        pass_in = sem("pass_in")
        hot_full = sem("hot_full")
        chunk_built = sem("chunk_built")
        chunk_saved = sem("chunk_saved")
        spmm_done = sem("spmm_done")
        agg_saved = sem("agg_saved")
        strip_put = [sem(f"strip_put{i}") for i in range(2)]
        strip_got = [sem(f"strip_got{i}") for i in range(2)]
        p_ready = sem("p_ready")
        p_stored = sem("p_stored")
        q_saved = sem("q_saved")
        idx_set = sem("idx_set")
        p_got = [sem(f"p_got{i}") for i in range(3)]
        p_put = [sem(f"p_put{i}") for i in range(3)]
        blk_got = [sem(f"blk_got{i}") for i in range(3)]
        blk_added = sem("blk_added")
        blk_gelu = sem("blk_gelu")
        blk_used = sem("blk_used")
        s_ready = sem("s_ready")
        bc_got = [sem(f"bc_got{i}") for i in range(4)]
        bc_hot = sem("bc_hot")
        look_done = sem("look_done")
        look_used = sem("look_used")
        flag_ready = sem("flag_ready")
        bad_ready = sem("bad_ready")
        bad_summed = sem("bad_summed")
        g_loaded = sem("g_loaded")
        g_low = sem("g_low")
        g_seg_in = sem("g_seg_in")
        g_seg_set = sem("g_seg_set")
        g_pass_in = sem("g_pass_in")
        g_tab_set = sem("g_tab_set")
        g_sums = sem("g_sums")
        g_col = sem("g_col")
        g_col_set = sem("g_col_set")
        names = ["first"] + [f"wt{i}" for i in range(3)] + [f"pass{i}" for i in range(6)]
        tile_sems = {k: {x: sem(f"{k}_{x}") for x in
                         ("staged", "got", "row", "scaled", "summed", "ready", "added")} for k in names}
        final_ready = sem("final_ready")
        out_stored = sem("out_stored")

        block = ctx.enter_context(nc.Block())
        x_v = x.rearrange("(b p) f -> p b f", p=P)
        out_v = out.rearrange("(b p) f -> p b f", p=P)

        NPASS = 5
        PARTS = [3, 3, 3, 1, 1]
        KP = PB

        NSP_W = 18

        def choose(eng, rows, general):
            eng.wait_ge(flag_ready, 1)
            flag = eng.value_load(flagI[0:1, 0:1])
            with eng.If(flag == 1):
                rows()
            with eng.Else():
                general()

        @block.sync
        def _(sp):
            sp.dma_start(dstS[0:HP, 0:HT], dst[0:E, :].rearrange("(p t) o -> p (t o)", p=HP)).then_inc(dst_loaded, 16)
            sp.dma_start(dnext[0:HP, :], dst[1:E + 1, :].rearrange("(p t) o -> p (t o)", p=HP)).then_inc(dst_loaded, 16)
            sp.dma_start(X[:], x_v).then_inc(x_loaded, 16)
            for t, a in ((wself_s[:], w_self), (wnb_s[:], w_nb), (w1_s[:, 0:HID], w1[0:F, :]),
                         (w1_s[:, HID:2 * HID], w1[F:2 * F, :]), (conv_s[:], conv_w), (wlin_s[:], w_lin_t),
                         (bias0[:, 0, :], b_self.broadcast_to([P, F])), (bias0[:, 1, :], b_nb.broadcast_to([P, F])),
                         (bias1[:, HID:2 * HID], b1.broadcast_to([P, HID])), (biasc[:], conv_b.broadcast_to([P, F])),
                         (gam_s[:], gamma.broadcast_to([P, F])), (bet_s[:], beta.broadcast_to([P, F])),
                         (wat_s[:], w_attn.broadcast_to([P, F])), (w2_s[:], w2.broadcast_to([P, HID])),
                         (b2_s[:], b2.broadcast_to([P, 1])), (rel_s[:, 0, :], rel[0:P, :]),
                         (rel_s[0:NREL - P, 1, :], rel[P:NREL, :])):
                sp.dma_start(t, a).then_inc(w_loaded, 16)
            sp.dma_start(idxA[:], src[0:EP, 0:1].rearrange("(c p t) o -> p c (t o)", p=P, t=GT)).then_inc(idx_loaded, 16)
            def rows():
                sp.wait_ge(lo_ready, 1)
                sp.dma_start(lo_dram.rearrange("k d e -> d k e"), bfE.rearrange("p (k q) s -> p k (q s)", q=2)).then_inc(lo_stored, 16)
                sp.wait_ge(lo_ready, 2)
                sp.dma_start(tl_dram.rearrange("k d e -> d k e"), bfT.rearrange("p (k q) s -> p k (q s)", q=2)).then_inc(lo_stored, 16)
                sp.wait_ge(p_ready, 1)
                sp.dma_start(p_tab.rearrange("(b p) f -> p b f", p=P), T1[:, :, 0:HID]).then_inc(p_stored, 16)
                flat = p_flat.rearrange("(c p t) f -> c p (t f)", p=P, t=GT)
                with sp.Fori(0, GC // 3) as i:
                    for u in range(3):
                        sp.wait_ge(p_got[u], i * (16 * GT) + 16 * GT)
                        sp.dma_start(flat[bass.ds(i * 3 + u, 1), :, :].rearrange("c p f -> p (c f)"),
                                     PG[u].rearrange("p t f -> p (t f)")).then_inc(p_put[u], 16)
                sp.wait_ge(s_ready, 1)
                lod = lo_dram.rearrange("k (c d) e -> (k c) (d e)", d=CW)
                tld = tl_dram.rearrange("k (c d) e -> (k c) (d e)", d=CW)

                def broadcast(c, u):
                    sp.dma_start(BC[2 * u], lod[bass.ds(c, 1), :].broadcast_to([P, CW * P])).then_inc(bc_got[2 * u], 16)
                    sp.dma_start(BC[2 * u + 1], tld[bass.ds(c, 1), :].broadcast_to([P, CW * P])).then_inc(bc_got[2 * u + 1], 16)

                for u in range(2):
                    broadcast(u, u)
                with sp.Fori(1, NCH // 2) as i:
                    for u in range(2):
                        sp.wait_ge(bc_hot, i * 2 + (u - 1))
                        broadcast(i * 2 + u, u)

                def stash(k, par):
                    sp.wait_ge(chunk_saved, k * CPB + (3 * NCH + CPB))
                    sp.dma_start(strips[bass.ds(k, 1)].rearrange("k p n -> p (k n)"),
                                 STC[:, par].rearrange("p x d -> p (x d)")).then_inc(strip_put[par], 16)

                def fetch(k, par):
                    sp.wait_ge(spmm_done, k + (4 * PB - 1))
                    sp.dma_start(STC[:, par].rearrange("p x d -> p (x d)"),
                                 strips[bass.ds(k, 1)].rearrange("k p n -> p (k n)")).then_inc(strip_got[par], 16)

                with sp.Fori(0, PB // 2) as m:
                    stash(m * 2, 0)
                    stash(m * 2 + 1, 1)
                stash(PB - 1, 0)
                sp.wait_ge(strip_put[0], 16 * (PB - PB // 2))
                sp.wait_ge(strip_put[1], 16 * (PB // 2))
                sp.wait_ge(spmm_done, 4 * PB)
                with sp.Fori(0, PB // 2) as m:
                    fetch(m * 2, 0)
                    fetch(m * 2 + 1, 1)
                fetch(PB - 1, 0)

            def general():
                for t, a in ((gsrc, src), (gdst, dst), (gtyp, etype), (gew, eweight)):
                    sp.dma_start(t, a.rearrange("(p t) o -> p (t o)", p=P)).then_inc(g_loaded, 16)
                sp.wait_ge(g_seg_in, 1)
                sp.dma_start(seg.rearrange("(p k) o -> p (k o)", p=P), zeros[:, 0:AR // P]).then_inc(g_seg_set, 16)

                def sums(g):
                    sp.wait_ge(g_pass_in, g + 1)
                    sp.dma_start(tab.rearrange("(b p) f -> p b f", p=P), TB[:]).then_inc(g_tab_set, 16)
                    sp.dma_start(acc.rearrange("(p k) f -> p (k f)", p=P), zeros).then_inc(g_tab_set, 16)
                    sp.wait_ge(tile_sems[f"pass{g}"]["added"], 16 * ST)
                    sp.dma_start(AGG[:, 0:B, :], acc[0:B * P, 0:F].rearrange("(b p) f -> p b f", p=P)).then_inc(g_sums, 16)
                    with nc.allow_non_contiguous_dma(reason="a column of sums"):
                        sp.dma_start(c1[:, 0:B], acc[0:B * P, F:F + 1].rearrange("(b p) f -> p (b f)", p=P)).then_inc(g_sums, 16)

                sums(0)
                sp.wait_ge(p_ready, 1)
                sp.dma_start(p_tab.rearrange("(b p) f -> p b f", p=P), T1[:, :, 0:HID]).then_inc(p_stored, 16)
                sp.dma_start(q_tab.rearrange("(b p) f -> p b f", p=P), T1[:, :, HID:2 * HID]).then_inc(p_stored, 16)
                sums(1)
                sums(2)
                sp.wait_ge(g_col, 1)
                with nc.allow_non_contiguous_dma(reason="columns of the look-ups"):
                    sp.dma_start(s_tab.rearrange("(b p) o -> p (b o)", p=P), c3[:, 0:B]).then_inc(g_col_set, 16)
                    sp.dma_start(r_tab.rearrange("(b p) o -> p (b o)", p=P), rcol[:]).then_inc(g_col_set, 16)
                sums(3)
                sums(4)
                sums(5)

            choose(sp, rows, general)
            sp.wait_ge(final_ready, 1)
            sp.dma_start(out_v, T1).then_inc(out_stored, 16)
            sp.wait_ge(out_stored, 16)

        @block.gpsimd
        def _(pool):
            made = [0]

            def made_one(ins):
                made[0] += 1
                ins.then_inc(const_made, 1)

            made_one(pool.iota(T1[:, 8:24, :].rearrange("p b f -> p (b f)").bitcast(I32), [[1, P], [0, CW]], base=0, channel_multiplier=0))
            made_one(pool.iota(slotI[:].bitcast(I32), [[1, SLOT]], base=0, channel_multiplier=0))
            made_one(pool.iota(iotaP[:].bitcast(I32), [[0, 1]], base=0, channel_multiplier=1))
            made_one(pool.memset(ones[:], 1.0))
            pool.wait_ge(const_made, 4)
            made_one(pool.affine_select(out=ident[:], in_=ones[:], compare_op=ALU.is_equal, fill=0.0,
                                        base=0, pattern=[[-1, P]], channel_multiplier=1))
            made_one(pool.affine_select(out=upper[:], in_=ones[:], compare_op=ALU.is_gt, fill=0.0,
                                        base=0, pattern=[[1, P]], channel_multiplier=-1))
            def rows():
                pool.wait_ge(row_ready, 1)
                for arr, dstt, s in ((src, srcE, src_rows), (eweight, ewE, ew_rows), (etype, typE, typ_rows)):
                    for b in range(B):
                        pool.indirect_dma_start(out=dstt[:, b, :], out_offset=None, in_=arr,
                                                in_offset=bass.IndirectOffsetOnAxis(ap=rowI[:, b:b + 1], axis=0)).then_inc(s, 16)
                pool.wait_ge(idx_loaded, 16)
                pool.wait_ge(p_stored, 16)

                def gather(c, u, k):
                    pool.tensor_copy(idxS[u][:], idxA[:, bass.ds(c, 1), :].rearrange("p c t -> p (c t)")).then_inc(idx_set, 1)
                    pool.wait_ge(idx_set, k)
                    pool.nop(nofuse=True)
                    for t in range(GT):
                        pool.indirect_dma_start(out=PG[u][:, t, :], out_offset=None, in_=p_tab,
                                                in_offset=bass.IndirectOffsetOnAxis(ap=idxS[u][:, t:t + 1], axis=0)).then_inc(p_got[u], 16)

                for u in range(3):
                    gather(u, u, u + 1)
                with pool.Fori(1, GC // 3) as i:
                    for u in range(3):
                        pool.wait_ge(p_put[u], i * 16)
                        gather(i * 3 + u, u, i * 3 + (u + 1))
                for u in range(3):
                    pool.wait_ge(p_put[u], 16 * (GC // 3))
                pool.wait_ge(q_saved, 1)
                for b in range(B):
                    if b >= 3:
                        pool.wait_ge(blk_used, b - 2)
                    pool.indirect_dma_start(out=GB[b % 3], out_offset=None, in_=p_flat,
                                            in_offset=bass.IndirectOffsetOnAxis(ap=rowI[:, b:b + 1], axis=0)).then_inc(blk_got[b % 3], 16)

            def general():
                def gate():
                    pool.nop(nofuse=True)

                def gather(o, t, i, s):
                    pool.indirect_dma_start(out=o, out_offset=None, in_=t,
                                            in_offset=bass.IndirectOffsetOnAxis(ap=gi[:, i:i + 1], axis=0)).then_inc(s, 16)

                pool.affine_select(out=gLow, in_=ones[:], compare_op=ALU.is_gt, fill=0.0,
                                   base=0, pattern=[[-1, P]], channel_multiplier=1).then_inc(g_low, 1)
                s = tile_sems["first"]
                pool.wait_ge(g_seg_set, 16)
                with pool.Fori(0, ST) as t:
                    pool.wait_ge(s["staged"], t + 1)
                    gate()
                    gather(gc[:, 0:1], seg, 0, s["got"])
                    pool.wait_ge(s["ready"], t + 1)
                    gate()
                    pool.indirect_dma_start(out=seg, out_offset=bass.IndirectOffsetOnAxis(ap=gi[:, 1:2], axis=0),
                                            in_=gc[:, 1:2], in_offset=None).then_inc(s["added"], 16)
                    pool.wait_ge(s["added"], t * 16 + 16)
                    gate()

                def weights(g, tables):
                    s = tile_sems[f"wt{g}"]
                    with pool.Fori(0, ST) as t:
                        pool.wait_ge(s["staged"], t + 1)
                        gate()
                        for o, tb, i in tables:
                            gather(o, tb, i, s["got"])

                def add_rows(g):
                    s = tile_sems[f"pass{g}"]
                    pool.wait_ge(g_tab_set, 32 * (g + 1))
                    with pool.Fori(0, ST) as t:
                        pool.wait_ge(s["staged"], t + 1)
                        gate()
                        gather(gG[:, 0:F], tab, 0, s["got"])
                        pool.wait_ge(s["ready"], t + 1)
                        gate()
                        pool.indirect_dma_start(out=acc, out_offset=bass.IndirectOffsetOnAxis(ap=gi[:, 1:2], axis=0),
                                                in_=gO, in_offset=None, compute_op=ALU.add).then_inc(s["added"], 16)
                        pool.wait_ge(s["added"], t * 16 + 16)
                        gate()

                weights(0, [(gc[:, 0:1], seg, 0)])
                add_rows(0)
                pool.wait_ge(p_stored, 32)
                weights(1, [(gPQ[:, 0:HID], p_tab, 0), (gPQ[:, HID:2 * HID], q_tab, 1)])
                add_rows(1)
                add_rows(2)
                pool.wait_ge(g_col_set, 32)
                weights(2, [(gc[:, 0:1], s_tab, 0), (gc[:, 1:2], r_tab, 1)])
                add_rows(3)
                add_rows(4)
                add_rows(5)

            choose(pool, rows, general)

        @block.scalar
        def _(act):
            cols = [0]

            def column(o, i, func, **kw):
                act.wait_ge(col_ready, cols[0] + 1)
                cols[0] += 1
                act.activation(o, i, func, **kw).then_inc(col_done, 1)

            turned = [0]

            def transposed(n):
                for j in range(NG * n):
                    k, w = turned[0], min(4, B - 4 * (j // n)) * P
                    act.wait_ge(tp_ready, k + 1)
                    act.copy(inT[:, k % 4, 0:w], bank[k % 2][:, 0:w]).then_inc(inT_ready, 1)
                    turned[0] += 1

            def one_pass(g):
                c0, k0 = g * NCH, g * PB

                def chunks(k, par, first, stored=None):
                    for c in range(CPB):
                        act.wait_ge(chunk_built, k * CPB + (c0 + c + 1))
                        if c == 0 and not first:
                            act.wait_ge(spmm_done, k + (k0 - 1))
                            if g == 3:
                                act.wait_ge(strip_put[par], stored)
                        to = STC[:, par] if g == 3 else STR[:, par].rearrange("p q h d -> p (q h) d")
                        for j in range(2):
                            m = act.copy(to[:, :, c * CW + j * 8:c * CW + j * 8 + 8],
                                         bank[2 * (c % 2) + j][:, 0:8 * B2].rearrange("p (d x) -> p x d", x=B2))
                        m.then_inc(chunk_saved, 1)

                def agg(k, par):
                    act.wait_ge(spmm_done, k + (k0 + 1))
                    act.copy(AGG[:, bass.ds(k * 2, 2), :], bank[4 + par][:, 0:2 * F].rearrange("p (q f) -> p q f", q=2)).then_inc(agg_saved, 1)

                if g == 4:
                    with act.Fori(0, PB // 2) as m:
                        agg(m * 2, 0)
                        agg(m * 2 + 1, 1)
                    agg(PB - 1, 0)
                    return
                chunks(0, 0, True)
                chunks(1, 1, True)
                agg(0, 0)
                chunks(2, 0, False, 16)
                agg(1, 1)
                with act.Fori(1, (PB - 1) // 2) as m:
                    chunks(m * 2 + 1, 1, False, m * 16)
                    agg(m * 2, 0)
                    chunks(m * 2 + 2, 0, False, m * 16 + 16)
                    agg(m * 2 + 1, 1)
                agg(PB - 1, 0)

            column(c2[:, 0:B], c1[:, 0:B], ACT.Sqrt)

            def rows():
                column(wE, wE, ACT.Exp)
                one_pass(0)
                column(c2[:, 0:B], c1[:, 0:B], ACT.Sqrt)
                transposed(2)
                column(c2[:, 0:B], c1[:, 0:B], ACT.Sqrt)
                column(c2[:, 0:B], c1[:, 0:B], ACT.Sqrt)
                column(c2[:, 0:B], c1[:, 0:B], ACT.Sqrt)
                transposed(1)
                for b in range(B):
                    act.wait_ge(blk_added, b + 1)
                    act.activation(GB[b % 3], GB[b % 3], ACT.Gelu).then_inc(blk_gelu, 1)
                column(wE[:, 0:B, :], wE[:, 0:B, :], ACT.Sigmoid, bias=b2_s[:, 0:1])
                column(c2[:, 0:B], c1[:, 0:B], ACT.Sqrt)
                one_pass(1)
                transposed(1)
                column(c2[:, 0:B], c1[:, 0:B], ACT.Sqrt)
                column(rT[:], rT[:], ACT.Sigmoid)
                one_pass(2)
                transposed(1)
                column(c2[:, 0:B], c1[:, 0:B], ACT.Sqrt)
                column(c2[:, 0:B], c1[:, 0:B], ACT.Sqrt)
                one_pass(3)
                one_pass(4)

            def general():
                root = (c2[:, 0:B], c1[:, 0:B], ACT.Sqrt)
                column(gwF, gwF, ACT.Exp)
                column(*root)
                transposed(2)
                column(*root)
                column(*root)
                column(*root)
                transposed(1)
                s = tile_sems["wt1"]
                with act.Fori(0, ST) as t:
                    act.wait_ge(s["row"], t + 1)
                    act.activation(gG[:, 0:HID], gPQ[:, 0:HID], ACT.Gelu).then_inc(s["scaled"], 1)
                column(gwF, gwF, ACT.Sigmoid, bias=b2_s[:, 0:1])
                column(*root)
                transposed(1)
                column(*root)
                column(gwF, gwF, ACT.Sigmoid)
                transposed(1)
                column(*root)
                column(*root)

            start = cols[0], turned[0]

            def afresh():
                cols[0], turned[0] = start
                general()

            choose(act, rows, afresh)

        @block.tensor
        def _(pe):
            pe.wait_ge(const_made, 6)
            pe.wait_ge(zeros_made, 2)
            pe.matmul(bank[0][:, 0:B], zero_l, zero_r, start=True, stop=False, skip_group_check=True)
            with pe.Fori(0, HTP // CW // 4) as i:
                for u in range(4):
                    pe.wait_ge(hist_full, i * 4 + (u + 1))
                    for t in range(CW):
                        m = pe.matmul(bank[0][:, 0:B], LO[u][0:HP, :, t], HH[u][0:HP, :, t],
                                      start=False, stop=False, skip_group_check=True)
                    m.then_inc(hist_used, 1)
            pe.matmul(bank[0][:, 0:B], zero_l, zero_r, start=False, stop=True, skip_group_check=True).then_inc(hist_done, 1)
            pe.wait_ge(bad_ready, 1)
            pe.matmul(bank[2][:, 0:1], ones[:], bad[:, 0:1], start=True, stop=True).then_inc(bad_summed, 1)
            pe.wait_ge(deg_ready, 1)
            pe.matmul(bank[1][:, 0:B], upper[:], deg[:, 0:B], start=True, stop=True)
            pe.matmul(bank[1][:, 32:32 + B], ones[:], deg[:, 0:B], start=True, stop=True).then_inc(prefix_done, 1)

            turns = [0]

            def turn(t):
                pe.wait_ge(tin_ready, turns[0] + 1)
                if turns[0]:
                    pe.wait_ge(tout_used, turns[0])
                for k in range(PB):
                    m = pe.transpose(bank[k // 4][:, (k % 4) * P:(k % 4 + 1) * P],
                                     t[:, 2 * k:2 * k + 2, :].rearrange("p q s -> p (q s)"), ident[:])
                m.then_inc(tout_ready, 1)
                turns[0] += 1

            lins = [0, 0, 0]

            def linear(pairs):
                lins[0] += 1
                pe.wait_ge(lin_in, lins[0])
                n = len(pairs)
                for j in range(NG * n + 1):
                    if j < NG * n:
                        k = lins[1] + j
                        if k >= 2:
                            pe.wait_ge(inT_ready, k - 1)
                        for i, b in enumerate(range(4 * (j // n), min(4 * (j // n) + 4, B))):
                            m = pe.transpose(bank[k % 2][:, i * P:(i + 1) * P], pairs[j % n][0][:, b, :], ident[:])
                        m.then_inc(tp_ready, 1)
                    if j >= 1:
                        g, i = divmod(j - 1, n)
                        k, o = lins[1] + j - 1, lins[2] + g
                        if i < n - 1:
                            continue
                        pe.wait_ge(inT_ready, k + 1)
                        if o >= 2:
                            pe.wait_ge(lin_taken, o - 1)
                        for c in range(min(4, B - 4 * g)):
                            for i in range(n):
                                m = pe.matmul(bank[2 + o % 2][:, c * P:(c + 1) * P],
                                              inT[:, (k - n + 1 + i) % 4, c * P:(c + 1) * P],
                                              pairs[i][1], start=(i == 0), stop=(i == n - 1))
                        m.then_inc(lin_ready, 1)
                lins[1] += NG * n
                lins[2] += NG

            def one_pass(g):
                c0, k0, parts = g * NCH, g * PB, PARTS[g]
                pe.wait_ge(pass_in, g + 1)

                def step(par, q, h):
                    o = bank[4 + par][:, q * F:(q + 1) * F]
                    if g < 3:
                        return pe.matmul(o, STR[:, par, q, h, :], TB[:, h, :], start=(h == 0), stop=(h == B - 1))
                    for w in range(3):
                        m = pe.matmul(o, STC[:, par, q * B + h, :], TB3[:, h, w, :],
                                      start=(h == 0 and w == 0), stop=(h == B - 1 and w == 2))
                    return m

                def product(k, par, first, some=range(B2)):
                    if some[0] == 0:
                        pe.wait_ge(chunk_saved, k * CPB + (c0 + CPB))
                        if not first:
                            pe.wait_ge(agg_saved, k + (k0 - 1))
                    for x in some:
                        m = step(par, x // B, x % B)
                    if some[-1] == B2 - 1:
                        m.then_inc(spmm_done, 1)

                def pair(k, par, first, before, first_sums):
                    for c in range(CPB):
                        pe.wait_ge(hot_full, k * CPB + (c0 + c + 1))
                        if not (first and c < 2):
                            pe.wait_ge(chunk_saved, k * CPB + (c0 + c - 1))
                        for i in range(CW):
                            for w in range(parts):
                                m = pe.matmul(bank[2 * (c % 2) + i // 8][:, (i % 8) * B2:(i % 8 + 1) * B2],
                                              LO[c % 2][:, :, i], HW[c % 2][:, w, :, i],
                                              start=(w == 0), stop=(w == parts - 1))
                        m.then_inc(chunk_built, 1)
                        if before:
                            product(k - 1, 1 - par, first_sums, range(B2 * c // CPB, B2 * (c + 1) // CPB))

                if g == 4:
                    def hop(k, par, got, first):
                        pe.wait_ge(strip_got[par], got)
                        if not first:
                            pe.wait_ge(agg_saved, k + (k0 - 1))
                        for x in range(B2):
                            m = step(par, x // B, x % B)
                        m.then_inc(spmm_done, 1)

                    hop(0, 0, 16, True)
                    hop(1, 1, 16, True)
                    with pe.Fori(1, PB // 2) as m:
                        hop(m * 2, 0, m * 16 + 16, False)
                        hop(m * 2 + 1, 1, m * 16 + 16, False)
                    hop(PB - 1, 0, 16 * (PB - PB // 2), False)
                    return
                pair(0, 0, g == 0, False, False)
                pair(1, 1, False, True, True)
                pair(2, 0, False, True, True)
                with pe.Fori(1, (PB - 1) // 2) as m:
                    pair(m * 2 + 1, 1, False, True, False)
                    pair(m * 2 + 2, 0, False, True, False)
                product(PB - 1, 0, False)

            def rows():
                turn(tmpE)
                turn(tmpE)
                turn(maskE)
                turn(wE)
                one_pass(0)
                linear([(Hn, wself_s[:]), (AGG, wnb_s[:])])
                turn(tmpE)
                linear([(Hn, w1_s[:])])
                turn(wE)
                one_pass(1)
                linear([(AGG, conv_s[:])])
                pe.wait_ge(s_ready, 1)

                def look_up(c, u, first):
                    pe.wait_ge(bc_hot, c + 1)
                    if not first:
                        pe.wait_ge(look_used, c - 1)
                    for i in range(CW):
                        for t, tab, w, n in ((LS[2 * u], stab, 0, B), (LS[2 * u + 1], rtab, B, 2)):
                            for k in range(3):
                                m = pe.matmul(bank[u][:, i * VN + w:i * VN + w + n], t[:, i * P:(i + 1) * P], tab[:, k, :],
                                              start=(k == 0), stop=(k == 2))
                    m.then_inc(look_done, 1)

                for u in range(2):
                    look_up(u, u, True)
                with pe.Fori(1, NCH // 2) as i:
                    for u in range(2):
                        look_up(i * 2 + u, u, False)
                one_pass(2)
                linear([(AGG, wlin_s[:])])
                one_pass(3)
                one_pass(4)

            def general():
                s = tile_sems["first"]
                with pe.Fori(0, ST) as t:
                    pe.wait_ge(s["staged"], t + 1)
                    pe.matmul(bank[0][:, 0:P], gA, ident[:], start=True, stop=True)
                    pe.matmul(bank[1][:, 0:P], gB, ident[:], start=True, stop=True).then_inc(s["row"], 1)

                def add_rows(g):
                    s = tile_sems[f"pass{g}"]
                    with pe.Fori(0, ST) as t:
                        pe.wait_ge(s["staged"], t + 1)
                        pe.matmul(bank[0][:, 0:P], gA, ident[:], start=True, stop=True).then_inc(s["row"], 1)
                        pe.wait_ge(s["scaled"], t + 1)
                        pe.matmul(bank[1][:, 0:AW], gM, gG, start=True, stop=True).then_inc(s["summed"], 1)

                add_rows(0)
                linear([(Hn, wself_s[:]), (AGG, wnb_s[:])])
                linear([(Hn, w1_s[:])])
                add_rows(1)
                add_rows(2)
                linear([(AGG, conv_s[:])])
                add_rows(3)
                linear([(AGG, wlin_s[:])])
                add_rows(4)
                add_rows(5)

            def afresh():
                lins[:] = [0, 0, 0]
                general()

            choose(pe, rows, afresh)

        @block.vector
        def _(v):
            n = [0, 0]

            def link(ins):
                n[0] += 1
                ins.then_inc(dve_step, 1)
                v.wait_ge(dve_step, n[1] + n[0])

            def tt(o, a, b, op):
                link(v.tensor_tensor(o, a, b, op))

            def ts(o, a, s1, s2, op0, op1=ALU.bypass):
                link(v.tensor_scalar(o, a, s1, s2, op0, op1) if s2 is not None else v.tensor_scalar(o, a, s1, None, op0))

            def red(o, a, op):
                link(v.tensor_reduce(o, a, AX.X, op))

            def bcb(c):
                return c[:, :, None].broadcast_to([P, B, F])

            def row(r):
                return r[:, None, :].broadcast_to([P, B, F])

            cols = [0]

            def ask_column():
                cols[0] += 1
                v.wait_ge(col_done, cols[0])

            def rstd(scale, add):
                n[0] += 1
                v.tensor_scalar(c1[:, 0:B], c1[:, 0:B], scale, add, ALU.mult, ALU.add).then_inc(dve_step, 1)
                v.wait_ge(dve_step, n[1] + n[0])
                v.nop().then_inc(col_ready, 1)
                ask_column()
                link(v.reciprocal(c2[:, 0:B], c2[:, 0:B]))

            def ask(ins):
                link(ins)
                v.nop().then_inc(col_ready, 1)
                ask_column()

            def centred(o, i):
                red(c3[:, 0:B], i, ALU.add)
                ts(c3[:, 0:B], c3[:, 0:B], 1.0 / F, None, ALU.mult)
                tt(o, i, bcb(c3[:, 0:B]), ALU.subtract)
                tt(T2, o, o, ALU.mult)
                red(c1[:, 0:B], T2, ALU.add)

            def norm_in():
                centred(Hn[:], X[:])
                rstd(1.0 / F, LN_EPS)
                link(v.scalar_tensor_tensor(out=Hn[:], in0=Hn[:], scalar=0.0, in1=bcb(c2[:, 0:B]),
                                            op0=ALU.max, op1=ALU.mult))

            v.memset(zero_l, 0.0).then_inc(zeros_made, 1)
            v.memset(zero_r, 0.0).then_inc(zeros_made, 1)
            link(v.memset(dlo, -1.0))
            link(v.memset(dhi, -1.0))
            v.wait_ge(const_made, 3)
            link(v.tensor_copy(iotaLo[:].rearrange("p a b -> p (a b)"), T1[:, 8:24, :].rearrange("p b f -> p (b f)").bitcast(I32)))
            link(v.tensor_copy(slotI[:], slotI[:].bitcast(I32)))
            link(v.tensor_copy(iotaP[:], iotaP[:].bitcast(I32)))
            ts(halfB[:], iotaP[:], float(SLOT), float(B), ALU.is_ge, ALU.mult)
            link(v.tensor_copy(iotaHi[:], iotaLo[:, 0:VN, :]))
            ts(iotaHi[:, 0:B, :], iotaLo[:, 0:B, :], halfB[:, 0:1], None, ALU.add)

            v.wait_ge(dst_loaded, 32)
            link(v.memset(bad[:], 0.0))
            tt(ddiff[0:HP, :], dnext[0:HP, :], dstS[0:HP, 0:HT], ALU.subtract)
            red(bad[0:HP, 1:2], ddiff[0:HP, :], ALU.min)
            ts(bad[0:HP, 0:1], bad[0:HP, 1:2], 0.0, None, ALU.is_lt)
            ts(dloI[0:HP, 0:HT], dstS[0:HP, 0:HT], P - 1, None, ALU.bitwise_and)
            ts(dstS[0:HP, 0:HT], dstS[0:HP, 0:HT], 7, None, ALU.logical_shift_right)
            link(v.tensor_copy(dlo[0:HP, 0:HT], dloI[0:HP, 0:HT]))
            link(v.tensor_copy(dhi[0:HP, 0:HT], dstS[0:HP, 0:HT]))

            def hist(c, u, wait):
                if wait is not None:
                    v.wait_ge(hist_used, wait)
                v.tensor_tensor(LO[u][0:HP], dlo[0:HP, None, bass.ds(c * CW, CW)].broadcast_to([HP, P, CW]),
                                iotaLo[0:HP], ALU.is_equal)
                v.tensor_tensor(HH[u][0:HP], dhi[0:HP, None, bass.ds(c * CW, CW)].broadcast_to([HP, B, CW]),
                                iotaLo[0:HP, 0:B, :], ALU.is_equal).then_inc(hist_full, 1)

            for u in range(4):
                hist(u, u, None)
            with v.Fori(1, HTP // CW // 4) as i:
                for u in range(4):
                    hist(i * 4 + u, u, i * 4 + (u - 3))
            v.wait_ge(hist_done, 1)
            link(v.memset(deg[:], 0.0))
            v.tensor_copy(deg[:, 0:B], bank[0][:, 0:B]).then_inc(deg_ready, 1)
            v.wait_ge(deg_ready, 1)
            red(bad[:, 2:3], deg[:, 0:B], ALU.max)
            ts(bad[:, 2:3], bad[:, 2:3], float(SLOT), None, ALU.is_gt)
            n[0] += 1
            v.tensor_tensor(bad[:, 0:1], bad[:, 0:1], bad[:, 2:3], ALU.add).then_inc(dve_step, 1)
            v.wait_ge(dve_step, n[0])
            v.nop().then_inc(bad_ready, 1)
            v.wait_ge(bad_summed, 1)
            v.tensor_scalar(flagI[0:1, 0:1], bank[2][0:1, 0:1], 0.0, None, ALU.is_equal).then_inc(flag_ready, 1)
            v.wait_ge(prefix_done, 1)
            link(v.tensor_copy(tot[:], bank[1][:, 32:32 + B]))
            link(v.tensor_tensor_scan(scn[:], tot[:], tot[:], 0.0, ALU.add, ALU.bypass))
            tt(scn[:], scn[:], tot[:], ALU.subtract)
            tt(rowf[:], scn[:], bank[1][:, 0:B], ALU.add)
            v.tensor_copy(rowI[:], rowf[:]).then_inc(row_ready, 1)
            tt(maskE[:], slotI[:, None, :].broadcast_to([P, BE, SLOT]), deg[:, :, None].broadcast_to([P, BE, SLOT]), ALU.is_lt)

            v.wait_ge(x_loaded, 16)
            norm_in()
            link(v.tensor_copy(TB[:], Hn[:]))

            turns = [0]

            def turned(fn):
                turns[0] += 1
                v.wait_ge(tout_ready, turns[0])
                for b4 in range(4):
                    w = min(512, PB * P - b4 * 512)
                    fn(slice(b4 * 512, b4 * 512 + w), bank[b4][:, 0:w])
                v.nop().then_inc(tout_used, 1)

            def turn_in():
                v.nop().then_inc(tin_ready, 1)

            def split3(cols, a):
                link(v.tensor_copy(wT[0][:, cols], a))
                tt(rT[:, cols], a, wT[0][:, cols], ALU.subtract)
                link(v.tensor_copy(wT[1][:, cols], rT[:, cols]))
                tt(rT[:, cols], rT[:, cols], wT[1][:, cols], ALU.subtract)
                link(v.tensor_copy(wT[2][:, cols], rT[:, cols]))

            def one_pass(g):
                c0, parts = g * NCH, PARTS[g]
                weights = W3[:] if g < 3 else mT[:, None, :]
                v.nop().then_inc(pass_in, 1)
                if g == 4:
                    v.wait_ge(agg_saved, (g + 1) * PB)
                    return

                def chunk(k, c, first, step):
                    at = bass.ds(k * P + c * CW, CW)
                    u = c % 2
                    if not (first and c < 2):
                        v.wait_ge(chunk_built, k * CPB + (c0 + c - 1))
                    v.tensor_tensor(HM[u][:], hiT[:, None, at].broadcast_to([P, B2, CW]),
                                    iotaLo[:, 0:B2, :], ALU.is_equal).then_inc(dve_step, 1)
                    v.tensor_tensor(LO[u][:], loT[:, None, at].broadcast_to([P, P, CW]), iotaLo[:], ALU.is_equal)
                    v.wait_ge(dve_step, step)
                    v.tensor_tensor(HW[u][:, 0:parts], HM[u][:, None, :, :].broadcast_to([P, parts, B2, CW]),
                                    weights[:, :, None, at].broadcast_to([P, parts, B2, CW]), ALU.mult).then_inc(hot_full, 1)

                for c in range(CPB):
                    chunk(0, c, g == 0, n[0] + c + 1)
                with v.Fori(1, PB) as k:
                    for c in range(CPB):
                        chunk(k, c, False, k * CPB + (n[0] + c + 1))
                n[0] += NCH
                v.wait_ge(agg_saved, (g + 1) * PB)

            outs = [0]

            def linear(o, bias):
                v.nop().then_inc(lin_in, 1)
                for g in range(NG):
                    k, m = outs[0], min(4, B - 4 * g)
                    v.wait_ge(lin_ready, k + 1)
                    got = bank[2 + k % 2][:, 0:m * P].rearrange("p (b f) -> p b f", f=F)
                    if bias is None:
                        i = v.tensor_copy(o[:, 4 * g:4 * g + m, :], got)
                    else:
                        i = v.tensor_tensor(o[:, 4 * g:4 * g + m, :], got, bias[:, None, :].broadcast_to([P, m, F]), ALU.add)
                    i.then_inc(lin_taken, 1)
                    outs[0] += 1
                v.wait_ge(lin_taken, outs[0])

            A = AGG[:, 0:B, :]

            def l0_output():
                tt(A, A, bcb(c4[:, 0:B]), ALU.mult)
                tt(T2, A, A, ALU.mult)
                red(c1[:, 0:B], T2, ALU.add)
                v.nop().then_inc(col_ready, 1)
                ask_column()
                ts(c2[:, 0:B], c2[:, 0:B], EPS, None, ALU.add)
                link(v.reciprocal(c2[:, 0:B], c2[:, 0:B]))
                tt(A, A, bcb(c2[:, 0:B]), ALU.mult)
                v.wait_ge(w_loaded, 16 * 17)
                tt(bias0[:, 0, :], bias0[:, 0, :], bias0[:, 1, :], ALU.add)
                linear(T1, bias0[:, 0, :])
                ts(T1, T1, 0.5, None, ALU.mult)
                tt(T2, T1, T1, ALU.mult)
                red(c1[:, 0:B], T2, ALU.add)
                v.nop().then_inc(col_ready, 1)
                ask_column()
                ts(c2[:, 0:B], c2[:, 0:B], EPS, None, ALU.add)
                link(v.reciprocal(c2[:, 0:B], c2[:, 0:B]))
                tt(T1, T1, bcb(c2[:, 0:B]), ALU.mult)
                centred(T1, T1)
                rstd(1.0 / F, LN_EPS)
                tt(T1, T1, bcb(c2[:, 0:B]), ALU.mult)
                tt(T1, T1, row(gam_s[:]), ALU.mult)
                tt(T1, T1, row(bet_s[:]), ALU.add)
                tt(X[:], X[:], T1, ALU.add)


            def l1_project():
                norm_in()
                link(v.memset(bias1[:, 0:HID], 0.0))
                linear(T1, bias1[:])
                v.nop().then_inc(p_ready, 1)

            def l1_output():
                tt(A, A, TB[:], ALU.add)
                tt(A, A, bcb(dinv[:]), ALU.mult)
                linear(T1, biasc[:])
                tt(X[:], X[:], T1, ALU.add)


            def l2_columns():
                norm_in()
                tt(T1, Hn[:], row(wat_s[:]), ALU.mult)
                red(c3[:, 0:B], T1, ALU.add)
                tt(T2[:, 0, :], rel_s[:, 0, :], wat_s[:], ALU.mult)
                red(rcol[:, 0:1], T2[:, 0, :], ALU.add)
                link(v.memset(rcol[:, 1:2], 0.0))
                tt(T2[0:NREL - P, 1, :], rel_s[0:NREL - P, 1, :], wat_s[0:NREL - P, :], ALU.mult)
                red(rcol[0:NREL - P, 1:2], T2[0:NREL - P, 1, :], ALU.add)

            def l2_output():
                linear(T1, None)
                link(v.scalar_tensor_tensor(out=X[:], in0=T1, scalar=0.0, in1=X[:], op0=ALU.max, op1=ALU.add))


            def l3_input():
                norm_in()
                ts(c1[:, 0:B], deg[:, 0:B], 1.0, None, ALU.max)
                v.nop().then_inc(col_ready, 1)
                ask_column()
                link(v.reciprocal(c2[:, 0:B], c2[:, 0:B]))
                ts(c3[:, 0:B], deg[:, 0:B], 1.0, None, ALU.min)
                tt(dis[:], c2[:, 0:B], c3[:, 0:B], ALU.mult)
                tt(TB[:], Hn[:], bcb(dis[:]), ALU.mult)

            def split_table():
                for w in range(3):
                    link(v.tensor_copy(TB3[:, :, w, :], TB[:]))
                    if w < 2:
                        tt(TB[:], TB[:], TB3[:, :, w, :], ALU.subtract)

            def l3_middle():
                tt(A, A, bcb(dis[:]), ALU.mult)
                tt(Hn[:], Hn[:], A, ALU.add)
                tt(TB[:], A, bcb(dis[:]), ALU.mult)

            def l3_output():
                tt(A, A, bcb(dis[:]), ALU.mult)
                tt(Hn[:], Hn[:], A, ALU.add)
                link(v.scalar_tensor_tensor(out=T1, in0=Hn[:], scalar=1.0 / 3.0, in1=X[:], op0=ALU.mult, op1=ALU.add))
                v.nop().then_inc(final_ready, 1)

            def rows():
                v.wait_ge(src_rows, 16 * B)
                link(v.memset(srcE[:, B:BE, :], 0))
                ts(tmpI, srcE[:], P - 1, None, ALU.bitwise_and)
                link(v.tensor_copy(tmpE, tmpI))
                turn_in()
                link(v.tensor_copy(bfE, tmpI))
                v.nop().then_inc(lo_ready, 1)
                turned(lambda c, a: link(v.tensor_copy(loT[:, c], a)))
                ts(tmpI, srcE[:], 7, None, ALU.logical_shift_right)
                link(v.tensor_copy(tmpE, tmpI))
                turn_in()
                turned(lambda c, a: link(v.tensor_scalar(hiT[:, c], a, halfB[:, 0:1], None, ALU.add)))
                turn_in()
                turned(lambda c, a: link(v.tensor_copy(mT[:, c], a)))
                v.wait_ge(typ_rows, 16 * B)
                link(v.memset(typE[:, B:BE, :], 0))
                ts(tmpI, typE[:], P - 1, None, ALU.bitwise_and)
                link(v.tensor_copy(bfT, tmpI))
                v.nop().then_inc(lo_ready, 1)
                v.wait_ge(lo_stored, 32)

                v.wait_ge(ew_rows, 16 * B)
                link(v.memset(ewE[:, B:BE, :], 0.0))
                ts(tmpE, maskE[:], 1.0, BIG, ALU.subtract, ALU.mult)
                tt(wE, ewE[:], maskE[:], ALU.mult)
                tt(wE, wE, tmpE, ALU.add)
                red(c1[:], wE, ALU.max)
                ask(v.tensor_tensor(wE, wE, c1[:, :, None].broadcast_to([P, BE, SLOT]), ALU.subtract))
                tt(wE, wE, maskE[:], ALU.mult)
                turn_in()
                red(c4[:], wE, ALU.add)
                ts(c4[:], c4[:], 1e-30, None, ALU.max)
                link(v.reciprocal(c4[:], c4[:]))
                turned(split3)

                one_pass(0)
                l0_output()
                ts(tmpI, typE[:], 7, None, ALU.logical_shift_right)
                link(v.tensor_copy(tmpE, tmpI))
                turn_in()
                turned(lambda c, a: link(v.tensor_scalar(thT[:, c], a, float(B), None, ALU.add)))
                l1_project()
                link(v.tensor_copy(AGG[:, 0:B, 0:HID], T1[:, :, HID:2 * HID]))
                v.nop().then_inc(q_saved, 1)
                v.wait_ge(p_stored, 16)
                link(v.memset(wE, 0.0))
                for b in range(B):
                    g3 = GB[b % 3].rearrange("p (s f) -> p s f", f=HID)
                    v.wait_ge(blk_got[b % 3], 16 * (b // 3 + 1))
                    v.tensor_tensor(g3, g3, AGG[:, b, None, 0:HID].broadcast_to([P, SLOT, HID]), ALU.add).then_inc(blk_added, 1)
                    if b >= 1:
                        mlp_out(v, link, blk_gelu, blk_used, GB, w2_s, wE, b - 1)
                mlp_out(v, link, blk_gelu, blk_used, GB, w2_s, wE, B - 1)
                v.nop().then_inc(col_ready, 1)
                ask_column()
                tt(wE, wE, maskE[:], ALU.mult)
                turn_in()
                red(c1[:], wE, ALU.add)
                rstd(1.0, 1.0)
                link(v.tensor_copy(dinv[:], c2[:, 0:B]))
                tt(TB[:], Hn[:], bcb(dinv[:]), ALU.mult)
                turned(split3)
                one_pass(1)
                l1_output()
                l2_columns()
                for tab, col in ((stab, c3[:, 0:B]), (rtab, rcol[:])):
                    for k in range(3):
                        link(v.tensor_copy(tab[:, k, :], col))
                        if k < 2:
                            tt(col, col, tab[:, k, :], ALU.subtract)
                v.nop().then_inc(s_ready, 1)

                def hot(c, u, k, first):
                    for j in range(2):
                        v.wait_ge(bc_got[2 * u + j], k * 16)
                    if not first:
                        v.wait_ge(look_done, c - 1)
                    v.tensor_scalar(LS[2 * u], BC[2 * u], iotaP[:, 0:1], None, ALU.is_equal)
                    v.tensor_scalar(LS[2 * u + 1], BC[2 * u + 1], iotaP[:, 0:1], None, ALU.is_equal).then_inc(bc_hot, 1)

                def pick(c, u, at, step):
                    v.tensor_tensor(HM[u][:, 0:B, :], hiT[:, None, at].broadcast_to([P, B, CW]), iotaHi[:, 0:B, :], ALU.is_equal)
                    v.tensor_tensor(HM[u][:, B:VN, :], thT[:, None, at].broadcast_to([P, 2, CW]), iotaHi[:, B:VN, :],
                                    ALU.is_equal).then_inc(dve_step, 1)
                    v.wait_ge(dve_step, step + 1)
                    v.wait_ge(look_done, c + 1)
                    v.tensor_tensor(VP[:], bank[u][:, 0:CW * VN].rearrange("p (i h) -> p h i", h=VN), HM[u][:, 0:VN, :], ALU.mult).then_inc(dve_step, 1)
                    v.wait_ge(dve_step, step + 2)
                    v.tensor_reduce(rT[:, at], VP[:].rearrange("p h i -> p i h"), AX.X, ALU.add).then_inc(dve_step, 1)
                    v.wait_ge(dve_step, step + 3)
                    v.nop().then_inc(look_used, 1)

                hot(0, 0, 1, True)
                hot(1, 1, 1, True)
                pick(0, 0, bass.ds(0, CW), n[0])
                with v.Fori(1, NCH // 2) as i:
                    hot(i * 2, 0, i + 1, False)
                    pick(i * 2 - 1, 1, bass.ds(i * (2 * CW) - CW, CW), i * 6 + (n[0] - 3))
                    hot(i * 2 + 1, 1, i + 1, False)
                    pick(i * 2, 0, bass.ds(i * (2 * CW), CW), i * 6 + n[0])
                pick(NCH - 1, 1, bass.ds((NCH - 1) * CW, CW), n[0] + 3 * (NCH - 1))
                n[0] += 3 * NCH
                v.nop().then_inc(col_ready, 1)
                ask_column()
                tt(rT[:], rT[:], mT[:], ALU.mult)
                link(v.tensor_copy(wT[0][:], rT[:]))
                tt(rT[:], rT[:], wT[0][:], ALU.subtract)
                link(v.tensor_copy(wT[1][:], rT[:]))
                tt(rT[:], rT[:], wT[1][:], ALU.subtract)
                link(v.tensor_copy(wT[2][:], rT[:]))
                link(v.tensor_copy(TB[:], Hn[:]))
                one_pass(2)
                l2_output()
                l3_input()
                split_table()
                one_pass(3)
                l3_middle()
                split_table()
                one_pass(4)
                l3_output()

            def general():
                def tile_loop(steps, body):
                    n0 = n[0]
                    with v.Fori(0, ST) as t:
                        n[1] = t * steps
                        body(t)
                        assert n[0] - n0 == steps, n[0] - n0
                    n[1] = 0
                    n[0] = n0 + steps * ST

                def at(a, t):
                    return a[:, bass.ds(t, 1)]

                v.wait_ge(g_loaded, 64)
                link(v.tensor_copy(gdstF, gdst))
                link(v.memset(zeros, -BIG))
                v.nop().then_inc(g_seg_in, 1)
                v.wait_ge(g_low, 1)
                ts(gc[:, 5:6], iotaP[:], float(B * P), None, ALU.add)

                def first(t):
                    s = tile_sems["first"]
                    link(v.tensor_copy(gc[:, 2:3], at(gdstF, t)))
                    link(v.tensor_copy(gc[:, 3:4], at(gew, t)))
                    link(v.tensor_copy(gi[:, 0:1], at(gdst, t)))
                    link(v.tensor_copy(gA, gc[:, 2:3].broadcast_to([P, P])))
                    v.tensor_copy(gB, gc[:, 3:4].broadcast_to([P, P])).then_inc(s["staged"], 1)
                    v.wait_ge(s["row"], t + 1)
                    ts(gM, bank[0][:, 0:P], gc[:, 2:3], None, ALU.is_equal)
                    tt(gMx, gM, gLow, ALU.mult)
                    red(gc[:, 4:5], gMx, ALU.add)
                    ts(gc[:, 4:5], gc[:, 4:5], 0.0, None, ALU.is_equal)
                    tt(gc[:, 6:7], gc[:, 2:3], gc[:, 5:6], ALU.subtract)
                    tt(gc[:, 6:7], gc[:, 6:7], gc[:, 4:5], ALU.mult)
                    tt(gc[:, 6:7], gc[:, 6:7], gc[:, 5:6], ALU.add)
                    link(v.tensor_copy(gi[:, 1:2], gc[:, 6:7]))
                    link(v.tensor_copy(at(gadj, t), gc[:, 6:7]))
                    tt(gMx, bank[1][:, 0:P], gM, ALU.mult)
                    ts(gM, gM, 1.0, BIG, ALU.subtract, ALU.mult)
                    tt(gMx, gMx, gM, ALU.add)
                    red(gc[:, 7:8], gMx, ALU.max)
                    v.wait_ge(s["got"], t * 16 + 16)
                    v.tensor_tensor(gc[:, 1:2], gc[:, 0:1], gc[:, 7:8], ALU.max).then_inc(s["ready"], 1)
                    v.wait_ge(s["added"], t * 16 + 16)

                tile_loop(17, first)

                def wt0(t):
                    s = tile_sems["wt0"]
                    v.tensor_copy(gi[:, 0:1], at(gdst, t)).then_inc(s["staged"], 1)
                    v.wait_ge(s["got"], t * 16 + 16)
                    tt(at(gwF, t), at(gew, t), gc[:, 0:1], ALU.subtract)

                tile_loop(1, wt0)
                v.nop().then_inc(col_ready, 1)
                ask_column()

                def add_rows(g):
                    s = tile_sems[f"pass{g}"]
                    link(v.memset(zeros, 0.0))
                    link(v.memset(gG, 0.0))
                    v.nop().then_inc(g_pass_in, 1)

                    def tile(t):
                        link(v.tensor_copy(gc[:, 2:3], at(gdstF, t)))
                        link(v.tensor_copy(gc[:, 3:4], at(gwF, t)))
                        link(v.tensor_copy(gi[:, 0:1], at(gsrc, t)))
                        link(v.tensor_copy(gi[:, 1:2], at(gadj, t)))
                        v.tensor_copy(gA, gc[:, 2:3].broadcast_to([P, P])).then_inc(s["staged"], 1)
                        v.wait_ge(s["row"], t + 1)
                        ts(gM, bank[0][:, 0:P], gc[:, 2:3], None, ALU.is_equal)
                        v.wait_ge(s["got"], t * 16 + 16)
                        link(v.tensor_scalar(gG[:, 0:F], gG[:, 0:F], gc[:, 3:4], None, ALU.mult))
                        v.tensor_copy(gG[:, F:F + 1], gc[:, 3:4]).then_inc(s["scaled"], 1)
                        v.wait_ge(s["summed"], t + 1)
                        v.tensor_copy(gO, bank[1][:, 0:AW]).then_inc(s["ready"], 1)
                        v.wait_ge(s["added"], t * 16 + 16)

                    tile_loop(6, tile)
                    v.wait_ge(g_sums, 32 * (g + 1))

                add_rows(0)
                ts(c4[:, 0:B], c1[:, 0:B], 1e-30, None, ALU.max)
                link(v.reciprocal(c4[:, 0:B], c4[:, 0:B]))
                l0_output()
                l1_project()
                v.wait_ge(p_stored, 32)

                def wt1(t):
                    s = tile_sems["wt1"]
                    link(v.tensor_copy(gi[:, 0:1], at(gsrc, t)))
                    v.tensor_copy(gi[:, 1:2], at(gdst, t)).then_inc(s["staged"], 1)
                    v.wait_ge(s["got"], t * 32 + 32)
                    v.tensor_tensor(gPQ[:, 0:HID], gPQ[:, 0:HID], gPQ[:, HID:2 * HID], ALU.add).then_inc(s["row"], 1)
                    v.wait_ge(s["scaled"], t + 1)
                    tt(gG[:, 0:HID], gG[:, 0:HID], w2_s[:], ALU.mult)
                    red(at(gwF, t), gG[:, 0:HID], ALU.add)

                tile_loop(3, wt1)
                v.nop().then_inc(col_ready, 1)
                ask_column()
                add_rows(1)
                rstd(1.0, 1.0)
                link(v.tensor_copy(dinv[:], c2[:, 0:B]))
                tt(TB[:], Hn[:], bcb(dinv[:]), ALU.mult)
                add_rows(2)
                l1_output()
                l2_columns()
                v.nop().then_inc(g_col, 1)

                def wt2(t):
                    s = tile_sems["wt2"]
                    link(v.tensor_copy(gi[:, 0:1], at(gsrc, t)))
                    v.tensor_copy(gi[:, 1:2], at(gtyp, t)).then_inc(s["staged"], 1)
                    v.wait_ge(s["got"], t * 32 + 32)
                    tt(at(gwF, t), gc[:, 0:1], gc[:, 1:2], ALU.add)

                tile_loop(2, wt2)
                v.nop().then_inc(col_ready, 1)
                ask_column()
                link(v.tensor_copy(TB[:], Hn[:]))
                add_rows(3)
                l2_output()
                l3_input()
                link(v.memset(gwF, 1.0))
                add_rows(4)
                l3_middle()
                add_rows(5)
                l3_output()

            count0 = list(n), list(cols), list(turns), list(outs)
            def fresh():
                for c, c0 in zip((n, cols, turns, outs), count0):
                    c[:] = c0

            choose(v, rows, lambda: (fresh(), general()))


_INS = [("x", "x"), ("src", "src"), ("dst", "dst"), ("etype", "edge_type_200"), ("eweight", "edge_weight"),
        ("w_self", "L0_gnn_W_self"), ("b_self", "L0_gnn_b_self"), ("w_nb", "L0_gnn_W_nb"), ("b_nb", "L0_gnn_b_nb"),
        ("gamma", "L0_gnn_gamma"), ("beta", "L0_gnn_beta"), ("w1", "L1_gnn_mlp_w1"), ("b1", "L1_gnn_mlp_b1"),
        ("w2", "L1_gnn_mlp_w2"), ("b2", "L1_gnn_mlp_b2"), ("conv_w", "L1_gnn_conv_w"), ("conv_b", "L1_gnn_conv_b"),
        ("rel", "L2_gnn_rel_emb"), ("w_lin_t", "L2_gnn_W_lin"), ("w_attn", "L2_gnn_W_attn")]


def kernel(**inputs):
    import numpy as np
    import concourse.bacc as bacc
    from concourse.bass_utils import run_bass_kernel_spmd

    a = {short: np.asarray(inputs[name]) for short, name in _INS}
    a["x"] = np.concatenate([a["x"], np.zeros((B * P - N, F), a["x"].dtype)])
    for k in ("src", "dst", "etype", "eweight"):
        a[k] = np.concatenate([a[k], np.full(EP - E, N if k == "dst" else 0, a[k].dtype)]).reshape(EP, 1)
    a["w_lin_t"] = a["w_lin_t"].T
    for k in ("b_self", "b_nb", "gamma", "beta", "b1", "w2", "b2", "conv_b", "w_attn"):
        a[k] = a[k].reshape(1, -1)
    a = {f"{k}_dram": np.ascontiguousarray(v) for k, v in a.items()}
    nc = bacc.Bacc("TRN2", target_bir_lowering=False, num_devices=1)
    args = [nc.dram_tensor(k, v.shape, mybir.dt.from_np(v.dtype), kind="ExternalInput").ap() for k, v in a.items()]
    out = nc.dram_tensor("out_dram", (B * P, F), F32, kind="ExternalOutput").ap()
    build(nc, *args, out)
    r = run_bass_kernel_spmd(nc, [a], core_ids=[0])
    return r.results[0]["out_dram"][:N]
```

```python
from contextlib import ExitStack

import concourse.bass as bass
from concourse import mybir

F32 = mybir.dt.float32
BF16 = mybir.dt.bfloat16
I32 = mybir.dt.int32
ALU = mybir.AluOpType
ACT = mybir.ActivationFunctionType
AX = mybir.AxisListType

P = 128
N = 3125
F = 128
HID = 64
NREL = 200
E = 103125
B = (N + P - 1) // P
SLOT = 64
NG = -(-B // 4)
PB = (B + 1) // 2
BE = 2 * PB
CW = 16
CPB = P // CW
NCH = PB * CPB
HP, HT = 125, 825
HTP = 832
GT = 16
GC = -(-(E + SLOT) // (P * GT))
EP = GC * P * GT
ST = EP // P
AW = F + 4
AR = B * P + P
B2 = 2 * B
LN_EPS = 1e-5
EPS = 1e-9
BIG = 1e30


def build(nc, x, src, dst, etype, eweight, w_self, b_self, w_nb, b_nb, gamma, beta,
          w1, b1, w2, b2, conv_w, conv_b, rel, w_lin_t, w_attn, out):
    ctx = ExitStack()
    with ctx:
        def sb(name, shape, dt=F32):
            return ctx.enter_context(nc.sbuf_tensor(name, shape, dt))

        def sem(name):
            return ctx.enter_context(nc.semaphore(name))

        X = sb("X", [P, B, F])
        Hn = sb("Hn", [P, B, F])
        TB = sb("TB", [P, B, F])
        AGG = sb("AGG", [P, BE, F])
        STR = sb("STR", [P, 2, 2, B, P])
        stream = STR[:].rearrange("p a q h d -> p (a q h d)")
        T1 = stream[:, 0:B * F].rearrange("p (b f) -> p b f", f=F)
        T2 = stream[:, B * F:2 * B * F].rearrange("p (b f) -> p b f", f=F)
        STC = stream[:, 0:B2 * P].bitcast(BF16).rearrange("p (a x d) -> p a x d", a=2, x=B2)
        TB3 = stream[:, B2 * P:B2 * P + 3 * B * F // 2].bitcast(BF16).rearrange("p (b w f) -> p b w f", w=3, f=F)
        inT = stream[:, 2 * B * F:2 * B * F + 4 * 4 * P].rearrange("p (a n) -> p a n", a=4)
        GB = [stream[:, i * SLOT * HID:(i + 1) * SLOT * HID] for i in range(2)]
        SB = [t.bitcast(BF16).rearrange("p (x d) -> p x d", d=P) for t in
              (stream[:, 2 * SLOT * HID:2 * SLOT * HID + B2 * P // 2], TB[:].rearrange("p b f -> p (b f)"))]
        aggf = AGG[:].rearrange("p b f -> p (b f)")
        QB = aggf[:, 0:B * HID].rearrange("p (b f) -> p b f", f=HID)
        BC = [stream[:, i * 1024:(i + 1) * 1024].bitcast(BF16) for i in range(4)]
        srcE = sb("srcE", [P, BE, SLOT], I32)
        typE = sb("typE", [P, BE, SLOT], I32)
        ewE = sb("ewE", [P, BE, SLOT])
        maskE = sb("maskE", [P, BE, SLOT])
        wE = srcE[:].bitcast(F32)
        RV = ewE[:].rearrange("p b s -> p (b s)")
        loT = sb("loT", [P, PB * P], BF16)
        hiT = sb("hiT", [P, PB * P], BF16)
        thT = sb("thT", [P, PB * P], BF16)
        W3 = sb("W3", [P, 3, PB * P], BF16)
        wT = [W3[:, i, :] for i in range(3)]
        mT = sb("mT", [P, PB * P], BF16)
        rT = sb("rT", [P, PB * P])
        LO = [sb(f"LO{i}", [P, P, CW], BF16) for i in range(4)]
        HM = [sb(f"HM{i}", [P, B2, CW], BF16) for i in range(2)]
        HW = [sb(f"HW{i}", [P, 3, B2, CW], BF16) for i in range(2)]
        HH = [HW[i // 2][:, i % 2, 0:B, :] for i in range(4)]
        VP = sb("VP", [P, B, CW])
        HR = sb("HR", [P, 2, 4 * CW], BF16)
        VR = sb("VR", [P, 2, 4 * CW])
        VPS = [VP[:], stream[:, 4096:4096 + B * CW].rearrange("p (h i) -> p h i", i=CW)]
        BR = [W3[:].rearrange("p w c -> p (w c)")[:, i * CW * P:(i + 1) * CW * P] for i in range(2)]
        free = 2 * SLOT * HID + B2 * P // 2
        PG = [t.rearrange("p (t f) -> p t f", f=HID) for t in
              (LO[2][:].rearrange("p a b -> p (a b)").bitcast(F32), LO[3][:].rearrange("p a b -> p (a b)").bitcast(F32),
               stream[:, free:free + GT * HID], aggf[:, B * HID:B * HID + GT * HID])]
        LS = [LO[i][:].rearrange("p a b -> p (a b)") for i in range(4)]
        iotaLo = sb("iotaLo", [P, P, CW], BF16)
        iotaHi = sb("iotaHi", [P, B, CW], BF16)
        iotaP = sb("iotaP", [P, 1])
        halfB = sb("halfB", [P, 1])
        slotI = sb("slotI", [P, SLOT])
        ident = sb("ident", [P, P])
        upper = sb("upper", [P, P])
        ones = sb("ones", [P, P])
        wself_s = sb("wself_s", [F, F])
        wnb_s = sb("wnb_s", [F, F])
        w1_s = sb("w1_s", [F, 2 * HID])
        conv_s = sb("conv_s", [F, F])
        wlin_s = sb("wlin_s", [F, F])
        bias0 = sb("bias0", [P, 2, F])
        bias1 = sb("bias1", [P, 2 * HID])
        biasc = sb("biasc", [P, F])
        gam_s = sb("gam_s", [P, F])
        bet_s = sb("bet_s", [P, F])
        wat_s = sb("wat_s", [P, F])
        w2_s = sb("w2_s", [P, HID])
        b2_s = sb("b2_s", [P, 1])
        rel_s = sb("rel_s", [P, 2, F])
        dstS = T2[:, 0:7, :].rearrange("p b f -> p (b f)")[:, 0:HTP].bitcast(I32)
        dnext = AGG[:, 0:7, :].rearrange("p b f -> p (b f)")[:, 0:HT].bitcast(I32)
        ddiff = AGG[:, 7:14, :].rearrange("p b f -> p (b f)")[:, 0:HT]
        dloI = T2[:, 7:14, :].rearrange("p b f -> p (b f)")[:, 0:HTP].bitcast(I32)
        dlo = T1[:, 0:4, :].rearrange("p b f -> p (b f)").bitcast(BF16)[:, 0:HTP]
        dhi = T1[:, 4:8, :].rearrange("p b f -> p (b f)").bitcast(BF16)[:, 0:HTP]
        tmpE = T1[:, 0:13, :].rearrange("p b f -> p (b f)").rearrange("p (b s) -> p b s", s=SLOT)
        tmpI = T2[:, 0:13, :].rearrange("p b f -> p (b f)").bitcast(I32).rearrange("p (b s) -> p b s", s=SLOT)
        bfE = T1[:, 13:20, :].rearrange("p b f -> p (b f)").bitcast(BF16)[:, 0:BE * SLOT].rearrange(
            "p (b s) -> p b s", s=SLOT)
        bfT = T2[:, 13:20, :].rearrange("p b f -> p (b f)").bitcast(BF16)[:, 0:BE * SLOT].rearrange(
            "p (b s) -> p b s", s=SLOT)
        deg = sb("deg", [P, BE])
        tot = sb("tot", [P, B])
        scn = sb("scn", [P, B])
        rowf = sb("rowf", [P, B])
        rowI = sb("rowI", [P, B], I32)
        c1 = sb("c1", [P, BE])
        c2 = sb("c2", [P, BE])
        c3 = sb("c3", [P, BE])
        c4 = sb("c4", [P, BE])
        flagI = sb("flagI", [1, 1], I32)
        bad = sb("bad", [P, 4])
        dinv = sb("dinv", [P, B])
        dis = sb("dis", [P, B])
        dev, fac = dinv, dis
        stab = sb("stab", [P, 3, B], BF16)
        rtab = sb("rtab", [P, 3, 2], BF16)
        rcol = sb("rcol", [P, 2])
        idxA = sb("idxA", [P, GC, GT], I32)
        idxS = [sb(f"idxS{i}", [P, GT], I32) for i in range(4)]
        idxB = [sb(f"idxB{i}", [P, 1], I32) for i in range(2)]

        zero_l = sb("zero_l", [1, P], BF16)[:]
        zero_r = sb("zero_r", [1, B], BF16)[:]
        bank = [ctx.enter_context(nc.psum_tensor(f"bank{i}", [P, 512], F32)) for i in range(8)]

        gsrc, gdst, gtyp = (t[:].bitcast(I32)[:, 0:ST] for t in (loT, hiT, thT))
        gdstF, gwF, gew = (t.bitcast(F32)[:, 0:ST] for t in (wT[0], wT[2], mT[:]))
        gadj = wT[1].bitcast(I32)[:, 0:ST]
        LOf = [LO[i][:].rearrange("p a b -> p (a b)").bitcast(F32) for i in range(4)]
        gA, gB, gM, gMx = (LOf[0][:, i * P:(i + 1) * P] for i in range(4))
        gG, gO = LOf[1][:, 0:AW], LOf[1][:, AW:2 * AW]
        gPQ = LOf[1][:, 2 * AW:2 * AW + 2 * HID]
        gLow = LOf[2][:, 0:P]
        gc = LOf[2][:, P:P + 16]
        gi = LOf[2][:, P + 16:P + 20].bitcast(I32)
        zeros = stream[:, 0:AR * AW // P]
        zrow = LOf[2][:, 0:GT * HID]

        p_tab = nc.dram_tensor("p_tab", (B * P, HID), F32).ap()
        p_flat = nc.dram_tensor("p_flat", (EP, HID), F32).ap()
        lo_dram = nc.dram_tensor("lo_dram", (PB, P, P), BF16).ap()
        tl_dram = nc.dram_tensor("tl_dram", (PB, P, P), BF16).ap()

        q_tab = nc.dram_tensor("q_tab", (B * P, HID), F32).ap()
        tab = nc.dram_tensor("tab", (B * P, F), F32).ap()
        acc = nc.dram_tensor("acc", (AR, AW), F32).ap()
        seg = nc.dram_tensor("seg", (AR, 1), F32).ap()
        s_tab = nc.dram_tensor("s_tab", (B * P, 1), F32).ap()
        r_tab = nc.dram_tensor("r_tab", (2 * P, 1), F32).ap()

        strips = nc.dram_tensor("strips", (PB, P, B2 * P), BF16).ap()

        x_loaded = sem("x_loaded")
        dst_loaded = sem("dst_loaded")
        w_loaded = sem("w_loaded")
        idx_loaded = sem("idx_loaded")
        const_made = sem("const_made")
        dve_step = sem("dve_step")
        zeros_made = sem("zeros_made")
        flat_zeroed = sem("flat_zeroed")
        hist_full = sem("hist_full")
        hist_used = sem("hist_used")
        hist_done = sem("hist_done")
        deg_ready = sem("deg_ready")
        prefix_done = sem("prefix_done")
        row_ready = sem("row_ready")
        src_rows = sem("src_rows")
        ew_rows = sem("ew_rows")
        typ_rows = sem("typ_rows")
        tin_ready = sem("tin_ready")
        tout_ready = sem("tout_ready")
        tout_used = sem("tout_used")
        lo_ready = sem("lo_ready")
        lo_stored = sem("lo_stored")
        col_ready = sem("col_ready")
        col_done = sem("col_done")
        lin_in = sem("lin_in")
        tp_ready = sem("tp_ready")
        inT_ready = sem("inT_ready")
        lin_ready = sem("lin_ready")
        lin_taken = sem("lin_taken")
        pass_in = sem("pass_in")
        hot_full = sem("hot_full")
        chunk_built = sem("chunk_built")
        chunk_saved = sem("chunk_saved")
        spmm_done = sem("spmm_done")
        agg_saved = sem("agg_saved")
        strip_put = [sem(f"strip_put{i}") for i in range(2)]
        strip_got = [sem(f"strip_got{i}") for i in range(2)]
        p_ready = sem("p_ready")
        p_stored = sem("p_stored")
        q_saved = sem("q_saved")
        idx_set = sem("idx_set")
        p_got = [sem(f"p_got{i}") for i in range(4)]
        p_put = [sem(f"p_put{i}") for i in range(4)]
        blk_got = [sem(f"blk_got{i}") for i in range(2)]
        blk_added = sem("blk_added")
        blk_gelu = sem("blk_gelu")
        blk_used = sem("blk_used")
        br_got = [sem(f"br_got{i}") for i in range(2)]
        br_hot = sem("br_hot")
        br_looked = sem("br_looked")
        br_taken = sem("br_taken")
        s_ready = sem("s_ready")
        bc_got = [sem(f"bc_got{i}") for i in range(4)]
        bc_hot = sem("bc_hot")
        look_done = sem("look_done")
        look_used = sem("look_used")
        flag_ready = sem("flag_ready")
        bad_ready = sem("bad_ready")
        bad_summed = sem("bad_summed")
        g_loaded = sem("g_loaded")
        g_low = sem("g_low")
        g_seg_in = sem("g_seg_in")
        g_seg_set = sem("g_seg_set")
        g_pass_in = sem("g_pass_in")
        g_tab_set = sem("g_tab_set")
        g_sums = sem("g_sums")
        g_col = sem("g_col")
        g_col_set = sem("g_col_set")
        names = ["first"] + [f"wt{i}" for i in range(3)] + [f"pass{i}" for i in range(6)]
        tile_sems = {k: {x: sem(f"{k}_{x}") for x in
                         ("staged", "got", "row", "scaled", "summed", "ready", "added")} for k in names}
        final_ready = sem("final_ready")
        out_stored = sem("out_stored")

        block = ctx.enter_context(nc.Block())
        x_v = x.rearrange("(b p) f -> p b f", p=P)
        out_v = out.rearrange("(b p) f -> p b f", p=P)

        CHUNKS_BEFORE = [0, 2 * NCH, 3 * NCH]

        def choose(eng, rows, general):
            eng.wait_ge(flag_ready, 1)
            flag = eng.value_load(flagI[0:1, 0:1])
            with eng.If(flag == 1):
                rows()
            with eng.Else():
                general()

        @block.sync
        def _(sp):
            sp.dma_start(dstS[0:HP, 0:HT], dst[0:E, :].rearrange("(p t) o -> p (t o)", p=HP)).then_inc(dst_loaded, 16)
            sp.dma_start(dnext[0:HP, :], dst[1:E + 1, :].rearrange("(p t) o -> p (t o)", p=HP)).then_inc(dst_loaded, 16)
            sp.dma_start(X[:], x_v).then_inc(x_loaded, 16)
            for t, a in ((wself_s[:], w_self), (wnb_s[:], w_nb), (w1_s[:, 0:HID], w1[0:F, :]),
                         (w1_s[:, HID:2 * HID], w1[F:2 * F, :]), (conv_s[:], conv_w), (wlin_s[:], w_lin_t),
                         (bias0[:, 0, :], b_self.broadcast_to([P, F])), (bias0[:, 1, :], b_nb.broadcast_to([P, F])),
                         (bias1[:, HID:2 * HID], b1.broadcast_to([P, HID])), (biasc[:], conv_b.broadcast_to([P, F])),
                         (gam_s[:], gamma.broadcast_to([P, F])), (bet_s[:], beta.broadcast_to([P, F])),
                         (wat_s[:], w_attn.broadcast_to([P, F])), (w2_s[:], w2.broadcast_to([P, HID])),
                         (b2_s[:], b2.broadcast_to([P, 1])), (rel_s[:, 0, :], rel[0:P, :]),
                         (rel_s[0:NREL - P, 1, :], rel[P:NREL, :])):
                sp.dma_start(t, a).then_inc(w_loaded, 16)
            sp.dma_start(idxA[:], src[0:EP, 0:1].rearrange("(c p t) o -> p c (t o)", p=P, t=GT)).then_inc(idx_loaded, 16)
            def rows():
                sp.wait_ge(lo_ready, 1)
                sp.dma_start(lo_dram.rearrange("k d e -> d k e"), bfE.rearrange("p (k q) s -> p k (q s)", q=2)).then_inc(lo_stored, 16)
                sp.wait_ge(typ_rows, 16 * B)
                sp.wait_ge(zeros_made, 3)
                sp.dma_start(p_flat.rearrange("(p k n) f -> p k (n f)", p=P, n=GT),
                             zrow[:, None, :].broadcast_to([P, ST // GT, GT * HID])).then_inc(flat_zeroed, 16)
                sp.wait_ge(lo_ready, 2)
                sp.dma_start(tl_dram.rearrange("k d e -> d k e"), bfT.rearrange("p (k q) s -> p k (q s)", q=2)).then_inc(lo_stored, 16)
                sp.wait_ge(p_ready, 1)
                sp.dma_start(p_tab.rearrange("(b p) f -> p b f", p=P), T1[:, :, 0:HID]).then_inc(p_stored, 16)
                flat = p_flat.rearrange("(c p t) f -> c p (t f)", p=P, t=GT)
                def put(c, u, k):
                    sp.wait_ge(p_got[u], k)
                    sp.dma_start(flat[bass.ds(c, 1), :, :].rearrange("c p f -> p (c f)"),
                                 PG[u].rearrange("p t f -> p (t f)")).then_inc(p_put[u], 16)

                with sp.Fori(0, GC // 4) as i:
                    for u in range(4):
                        put(i * 4 + u, u, i * (16 * GT) + 16 * GT)
                for c in range(GC // 4 * 4, GC):
                    put(c, c % 4, 16 * GT * (c // 4 + 1))
                sp.wait_ge(s_ready, 1)
                lod = lo_dram.rearrange("k (c d) e -> (k c) (d e)", d=CW)

                def broadcast(c, u):
                    sp.dma_start(BC[u], lod[bass.ds(c, 1), :].broadcast_to([P, CW * P])).then_inc(bc_got[u], 16)

                for u in range(4):
                    broadcast(u, u)
                with sp.Fori(1, NCH // 4) as i:
                    for u in range(4):
                        sp.wait_ge(bc_hot, i * 4 + (u - 3))
                        broadcast(i * 4 + u, u)

                def fetch(g, k, par, first):
                    if not first:
                        sp.wait_ge(spmm_done, k + (g * PB - 1))
                    sp.dma_start(STC[:, par].rearrange("p x d -> p (x d)"),
                                 strips[bass.ds(k, 1)].rearrange("k p n -> p (k n)")).then_inc(strip_got[par], 16)

                sp.wait_ge(strip_put[0], 16 * (PB - PB // 2))
                sp.wait_ge(strip_put[1], 16 * (PB // 2))
                for g in (3, 4):
                    if g == 3:
                        sp.wait_ge(pass_in, g + 1)
                    else:
                        sp.wait_ge(spmm_done, g * PB)
                    fetch(g, 0, 0, True)
                    fetch(g, 1, 1, True)
                    with sp.Fori(1, PB // 2) as m:
                        fetch(g, m * 2, 0, False)
                        fetch(g, m * 2 + 1, 1, False)
                    fetch(g, PB - 1, 0, False)

            def general():
                for t, a in ((gsrc, src), (gdst, dst), (gtyp, etype), (gew, eweight)):
                    sp.dma_start(t, a.rearrange("(p t) o -> p (t o)", p=P)).then_inc(g_loaded, 16)
                sp.wait_ge(g_seg_in, 1)
                sp.dma_start(seg.rearrange("(p k) o -> p (k o)", p=P), zeros[:, 0:AR // P]).then_inc(g_seg_set, 16)

                def sums(g):
                    sp.wait_ge(g_pass_in, g + 1)
                    sp.dma_start(tab.rearrange("(b p) f -> p b f", p=P), TB[:]).then_inc(g_tab_set, 16)
                    sp.dma_start(acc.rearrange("(p k) f -> p (k f)", p=P), zeros).then_inc(g_tab_set, 16)
                    sp.wait_ge(tile_sems[f"pass{g}"]["added"], 16 * ST)
                    sp.dma_start(AGG[:, 0:B, :], acc[0:B * P, 0:F].rearrange("(b p) f -> p b f", p=P)).then_inc(g_sums, 16)
                    with nc.allow_non_contiguous_dma(reason="a column of sums"):
                        sp.dma_start(c1[:, 0:B], acc[0:B * P, F:F + 1].rearrange("(b p) f -> p (b f)", p=P)).then_inc(g_sums, 16)

                sums(0)
                sp.wait_ge(p_ready, 1)
                sp.dma_start(p_tab.rearrange("(b p) f -> p b f", p=P), T1[:, :, 0:HID]).then_inc(p_stored, 16)
                sp.dma_start(q_tab.rearrange("(b p) f -> p b f", p=P), T1[:, :, HID:2 * HID]).then_inc(p_stored, 16)
                sums(1)
                sums(2)
                sp.wait_ge(g_col, 1)
                with nc.allow_non_contiguous_dma(reason="columns of the look-ups"):
                    sp.dma_start(s_tab.rearrange("(b p) o -> p (b o)", p=P), c3[:, 0:B]).then_inc(g_col_set, 16)
                    sp.dma_start(r_tab.rearrange("(b p) o -> p (b o)", p=P), rcol[:]).then_inc(g_col_set, 16)
                sums(3)
                sums(4)
                sums(5)

            choose(sp, rows, general)
            sp.wait_ge(final_ready, 1)
            sp.dma_start(out_v, T1).then_inc(out_stored, 16)
            sp.wait_ge(out_stored, 16)

        @block.gpsimd
        def _(pool):
            made = [0]

            def made_one(ins):
                made[0] += 1
                ins.then_inc(const_made, 1)

            made_one(pool.iota(T1[:, 8:24, :].rearrange("p b f -> p (b f)").bitcast(I32), [[1, P], [0, CW]], base=0, channel_multiplier=0))
            made_one(pool.iota(slotI[:].bitcast(I32), [[1, SLOT]], base=0, channel_multiplier=0))
            made_one(pool.iota(iotaP[:].bitcast(I32), [[0, 1]], base=0, channel_multiplier=1))
            made_one(pool.memset(ones[:], 1.0))
            pool.wait_ge(const_made, 4)
            made_one(pool.affine_select(out=ident[:], in_=ones[:], compare_op=ALU.is_equal, fill=0.0,
                                        base=0, pattern=[[-1, P]], channel_multiplier=1))
            made_one(pool.affine_select(out=upper[:], in_=ones[:], compare_op=ALU.is_gt, fill=0.0,
                                        base=0, pattern=[[1, P]], channel_multiplier=-1))
            def rows():
                pool.wait_ge(row_ready, 1)
                for arr, dstt, s in ((src, srcE, src_rows), (eweight, ewE, ew_rows), (etype, typE, typ_rows)):
                    for b in range(B):
                        pool.indirect_dma_start(out=dstt[:, b, :], out_offset=None, in_=arr,
                                                in_offset=bass.IndirectOffsetOnAxis(ap=rowI[:, b:b + 1], axis=0)).then_inc(s, 16)
                pool.wait_ge(idx_loaded, 16)
                pool.wait_ge(flat_zeroed, 16)
                pool.wait_ge(p_stored, 16)

                def gather(c, u, k, put):
                    if put is not None:
                        pool.wait_ge(p_put[u], put)
                    pool.tensor_copy(idxS[u][:], idxA[:, bass.ds(c, 1), :].rearrange("p c t -> p (c t)")).then_inc(idx_set, 1)
                    pool.wait_ge(idx_set, k)
                    pool.nop(nofuse=True)
                    for t in range(GT):
                        pool.indirect_dma_start(out=PG[u][:, t, :], out_offset=None, in_=p_tab,
                                                in_offset=bass.IndirectOffsetOnAxis(ap=idxS[u][:, t:t + 1], axis=0)).then_inc(p_got[u], 16)

                def slots(b, par, k, used, puts):
                    if used is not None:
                        pool.wait_ge(blk_used, used)
                    pool.tensor_copy(idxB[par][:], rowI[:, bass.ds(b, 1)]).then_inc(idx_set, 1)
                    pool.wait_ge(idx_set, k)
                    for u, n in puts:
                        pool.wait_ge(p_put[u], n)
                    pool.nop(nofuse=True)
                    pool.indirect_dma_start(out=GB[par], out_offset=None, in_=p_flat,
                                            in_offset=bass.IndirectOffsetOnAxis(ap=idxB[par][:], axis=0)).then_inc(blk_got[par], 16)

                def four(m, first, last=False):
                    k = m * 6 + 4
                    gather(m * 4 + 4, 0, k + 1, m * 16 + 16)
                    gather(m * 4 + 5, 1, k + 2, m * 16 + 16)
                    slots(m * 2, 0, k + 3, None if first else m * 2 - 1,
                          [(u, m * 16 + 16) for u in range(4)])
                    gather(m * 4 + 6, 2, k + 4, m * 16 + 16)
                    if not last:
                        gather(m * 4 + 7, 3, k + 5, m * 16 + 16)
                    slots(m * 2 + 1, 1, k + (5 if last else 6), None if first else m * 2,
                          [(u, m * 16 + 32) for u in (0, 1)])

                for u in range(4):
                    gather(u, u, u + 1, None)
                pool.wait_ge(q_saved, 1)
                m4 = GC // 4 - 1
                four(0, True)
                with pool.Fori(1, m4) as m:
                    four(m, False)
                four(m4, False, True)
                slots(B - 1, 0, 6 * m4 + 10, B - 2, [(u, 16 * (m4 + 2)) for u in range(3)])

            def general():
                def gate():
                    pool.nop(nofuse=True)

                def gather(o, t, i, s):
                    pool.indirect_dma_start(out=o, out_offset=None, in_=t,
                                            in_offset=bass.IndirectOffsetOnAxis(ap=gi[:, i:i + 1], axis=0)).then_inc(s, 16)

                pool.affine_select(out=gLow, in_=ones[:], compare_op=ALU.is_gt, fill=0.0,
                                   base=0, pattern=[[-1, P]], channel_multiplier=1).then_inc(g_low, 1)
                s = tile_sems["first"]
                pool.wait_ge(g_seg_set, 16)
                with pool.Fori(0, ST) as t:
                    pool.wait_ge(s["staged"], t + 1)
                    gate()
                    gather(gc[:, 0:1], seg, 0, s["got"])
                    pool.wait_ge(s["ready"], t + 1)
                    gate()
                    pool.indirect_dma_start(out=seg, out_offset=bass.IndirectOffsetOnAxis(ap=gi[:, 1:2], axis=0),
                                            in_=gc[:, 1:2], in_offset=None).then_inc(s["added"], 16)
                    pool.wait_ge(s["added"], t * 16 + 16)
                    gate()

                def weights(g, tables):
                    s = tile_sems[f"wt{g}"]
                    with pool.Fori(0, ST) as t:
                        pool.wait_ge(s["staged"], t + 1)
                        gate()
                        for o, tb, i in tables:
                            gather(o, tb, i, s["got"])

                def add_rows(g):
                    s = tile_sems[f"pass{g}"]
                    pool.wait_ge(g_tab_set, 32 * (g + 1))
                    with pool.Fori(0, ST) as t:
                        pool.wait_ge(s["staged"], t + 1)
                        gate()
                        gather(gG[:, 0:F], tab, 0, s["got"])
                        pool.wait_ge(s["ready"], t + 1)
                        gate()
                        pool.indirect_dma_start(out=acc, out_offset=bass.IndirectOffsetOnAxis(ap=gi[:, 1:2], axis=0),
                                                in_=gO, in_offset=None, compute_op=ALU.add).then_inc(s["added"], 16)
                        pool.wait_ge(s["added"], t * 16 + 16)
                        gate()

                weights(0, [(gc[:, 0:1], seg, 0)])
                add_rows(0)
                pool.wait_ge(p_stored, 32)
                weights(1, [(gPQ[:, 0:HID], p_tab, 0), (gPQ[:, HID:2 * HID], q_tab, 1)])
                add_rows(1)
                add_rows(2)
                pool.wait_ge(g_col_set, 32)
                weights(2, [(gc[:, 0:1], s_tab, 0), (gc[:, 1:2], r_tab, 1)])
                add_rows(3)
                add_rows(4)
                add_rows(5)

            choose(pool, rows, general)

        @block.scalar
        def _(act):
            cols = [0]

            def column(o, i, func, **kw):
                act.wait_ge(col_ready, cols[0] + 1)
                cols[0] += 1
                act.activation(o, i, func, **kw).then_inc(col_done, 1)

            def squares(i):
                for g in range(5):
                    b = slice(g * B // 5, (g + 1) * B // 5)
                    column(T2[:, b, :], i[:, b, :], ACT.Square)

            turned = [0]

            def transposed(n):
                for j in range(NG * n):
                    k, w = turned[0], min(4, B - 4 * (j // n)) * P
                    act.wait_ge(tp_ready, k + 1)
                    act.copy(inT[:, k % 4, 0:w], bank[k % 2][:, 0:w]).then_inc(inT_ready, 1)
                    turned[0] += 1

            def save_chunk(k, c, to, c0):
                act.wait_ge(chunk_built, k * CPB + (c0 + c + 1))
                for j in range(2):
                    m = act.copy(to[:, :, c * CW + j * 8:c * CW + j * 8 + 8],
                                 bank[2 * (c % 2) + j][:, 0:8 * B2].rearrange("p (d x) -> p x d", x=B2))
                m.then_inc(chunk_saved, 1)

            def mlp_and_strips():
                tld = tl_dram.rearrange("k (c d) e -> (k c) (d e)", d=CW)

                def broadcast(c, u):
                    act.dma_start(BR[u], tld[bass.ds(c, 1), :].broadcast_to([P, CW * P])).then_inc(br_got[u], 16)

                act.wait_ge(lo_stored, 32)
                for u in range(2):
                    broadcast(u, u)

                def strips_half(k, par, q, stored, last=False):
                    if q == 0 and stored is not None:
                        act.wait_ge(strip_put[par], stored)
                    for c in range(4 * q, 4 * q + 4):
                        save_chunk(k, c, SB[par], NCH)
                        if not last or c < CPB - 2:
                            act.wait_ge(br_looked, k * CPB + (c + 1))
                            broadcast(k * CPB + (c + 2), c % 2)
                    if q == 1:
                        act.wait_ge(chunk_saved, k * CPB + (NCH + CPB))
                        act.dma_start(strips[bass.ds(k, 1)].rearrange("k p n -> p (k n)"),
                                      SB[par].rearrange("p x d -> p (x d)")).then_inc(strip_put[par], 16)

                def gelu(k, q):
                    act.wait_ge(blk_added, k * 2 + (q + 1))
                    act.activation(GB[q], GB[q], ACT.Gelu).then_inc(blk_gelu, 1)

                for par in range(2):
                    for q in range(2):
                        strips_half(par, par, q, None)
                for par in range(2):
                    for q in range(2):
                        strips_half(par + 2, par, q, 16)
                        gelu(par, q)
                with act.Fori(1, PB // 2 - 1) as i:
                    for par in range(2):
                        for q in range(2):
                            strips_half(i * 2 + (par + 2), par, q, i * 16 + 16)
                            gelu(i * 2 + par, q)
                for q in range(2):
                    strips_half(PB - 1, 0, q, 16 * (PB // 2), last=(q == 1))
                    gelu(PB - 3, q)
                for b in range(2 * (PB - 2), B):
                    gelu(b // 2, b % 2)

            def one_pass(g):
                c0, k0 = CHUNKS_BEFORE[g], g * PB

                def chunks(k, par, first):
                    for c in range(CPB):
                        if c == 0 and not first:
                            act.wait_ge(spmm_done, k + (k0 - 1))
                        save_chunk(k, c, STR[:, par].rearrange("p q h d -> p (q h) d"), c0)

                def agg(k, par):
                    act.wait_ge(spmm_done, k + (k0 + 1))
                    act.copy(AGG[:, bass.ds(k * 2, 2), :], bank[4 + par][:, 0:2 * F].rearrange("p (q f) -> p q f", q=2)).then_inc(agg_saved, 1)

                chunks(0, 0, True)
                chunks(1, 1, True)
                agg(0, 0)
                chunks(2, 0, False)
                agg(1, 1)
                with act.Fori(1, (PB - 1) // 2) as m:
                    chunks(m * 2 + 1, 1, False)
                    agg(m * 2, 0)
                    chunks(m * 2 + 2, 0, False)
                    agg(m * 2 + 1, 1)
                agg(PB - 1, 0)

            squares(Hn)
            column(c2[:, 0:B], c1[:, 0:B], ACT.Sqrt)

            def rows():
                column(wE, wE, ACT.Exp)
                one_pass(0)
                column(c2[:, 0:B], c1[:, 0:B], ACT.Sqrt)
                transposed(2)
                squares(T1)
                column(c2[:, 0:B], c1[:, 0:B], ACT.Sqrt)
                column(c2[:, 0:B], c1[:, 0:B], ACT.Sqrt)
                squares(Hn)
                column(c2[:, 0:B], c1[:, 0:B], ACT.Sqrt)
                transposed(1)
                mlp_and_strips()
                column(wE[:, 0:B, :], wE[:, 0:B, :], ACT.Sigmoid, bias=b2_s[:, 0:1])
                column(c2[:, 0:B], c1[:, 0:B], ACT.Sqrt)
                one_pass(1)
                transposed(1)
                squares(Hn)
                column(c2[:, 0:B], c1[:, 0:B], ACT.Sqrt)
                column(rT[:], rT[:], ACT.Sigmoid)
                one_pass(2)
                transposed(1)
                squares(Hn)
                column(c2[:, 0:B], c1[:, 0:B], ACT.Sqrt)
                column(c2[:, 0:B], c1[:, 0:B], ACT.Sqrt)

            def general():
                root = (c2[:, 0:B], c1[:, 0:B], ACT.Sqrt)
                column(gwF, gwF, ACT.Exp)
                column(*root)
                transposed(2)
                squares(T1)
                column(*root)
                column(*root)
                squares(Hn)
                column(*root)
                transposed(1)
                s = tile_sems["wt1"]
                with act.Fori(0, ST) as t:
                    act.wait_ge(s["row"], t + 1)
                    act.activation(gG[:, 0:HID], gPQ[:, 0:HID], ACT.Gelu).then_inc(s["scaled"], 1)
                column(gwF, gwF, ACT.Sigmoid, bias=b2_s[:, 0:1])
                column(*root)
                transposed(1)
                squares(Hn)
                column(*root)
                column(gwF, gwF, ACT.Sigmoid)
                transposed(1)
                squares(Hn)
                column(*root)
                column(*root)

            start = cols[0], turned[0]

            def afresh():
                cols[0], turned[0] = start
                general()

            choose(act, rows, afresh)

        @block.tensor
        def _(pe):
            pe.wait_ge(const_made, 6)
            pe.wait_ge(zeros_made, 2)
            pe.matmul(bank[0][:, 0:B], zero_l, zero_r, start=True, stop=False, skip_group_check=True)
            with pe.Fori(0, HTP // CW // 4) as i:
                for u in range(4):
                    pe.wait_ge(hist_full, i * 4 + (u + 1))
                    for t in range(CW):
                        m = pe.matmul(bank[0][:, 0:B], LO[u][0:HP, :, t], HH[u][0:HP, :, t],
                                      start=False, stop=False, skip_group_check=True)
                    m.then_inc(hist_used, 1)
            pe.matmul(bank[0][:, 0:B], zero_l, zero_r, start=False, stop=True, skip_group_check=True).then_inc(hist_done, 1)
            pe.wait_ge(deg_ready, 1)
            pe.matmul(bank[1][:, 0:B], upper[:], deg[:, 0:B], start=True, stop=True)
            pe.matmul(bank[1][:, 32:32 + B], ones[:], deg[:, 0:B], start=True, stop=True).then_inc(prefix_done, 1)
            pe.wait_ge(bad_ready, 1)
            pe.matmul(bank[2][:, 0:1], ones[:], bad[:, 0:1], start=True, stop=True).then_inc(bad_summed, 1)

            turns = [0]

            def turn(t):
                pe.wait_ge(tin_ready, turns[0] + 1)
                if turns[0]:
                    pe.wait_ge(tout_used, turns[0])
                for k in range(PB):
                    m = pe.transpose(bank[k // 4][:, (k % 4) * P:(k % 4 + 1) * P],
                                     t[:, 2 * k:2 * k + 2, :].rearrange("p q s -> p (q s)"), ident[:])
                m.then_inc(tout_ready, 1)
                turns[0] += 1

            lins = [0, 0, 0]

            def linear(pairs):
                lins[0] += 1
                pe.wait_ge(lin_in, lins[0])
                n = len(pairs)
                for j in range(NG * n + 1):
                    if j < NG * n:
                        k = lins[1] + j
                        if k >= 2:
                            pe.wait_ge(inT_ready, k - 1)
                        for i, b in enumerate(range(4 * (j // n), min(4 * (j // n) + 4, B))):
                            m = pe.transpose(bank[k % 2][:, i * P:(i + 1) * P], pairs[j % n][0][:, b, :], ident[:])
                        m.then_inc(tp_ready, 1)
                    if j >= 1:
                        g, i = divmod(j - 1, n)
                        k, o = lins[1] + j - 1, lins[2] + g
                        if i < n - 1:
                            continue
                        pe.wait_ge(inT_ready, k + 1)
                        if o >= 2:
                            pe.wait_ge(lin_taken, o - 1)
                        for c in range(min(4, B - 4 * g)):
                            for i in range(n):
                                m = pe.matmul(bank[2 + o % 2][:, c * P:(c + 1) * P],
                                              inT[:, (k - n + 1 + i) % 4, c * P:(c + 1) * P],
                                              pairs[i][1], start=(i == 0), stop=(i == n - 1))
                        m.then_inc(lin_ready, 1)
                lins[1] += NG * n
                lins[2] += NG

            def build_chunk(k, c, c0, parts, first):
                pe.wait_ge(hot_full, k * CPB + (c0 + c + 1))
                if not first:
                    pe.wait_ge(chunk_saved, k * CPB + (c0 + c - 1))
                for i in range(CW):
                    for w in range(parts):
                        m = pe.matmul(bank[2 * (c % 2) + i // 8][:, (i % 8) * B2:(i % 8 + 1) * B2],
                                      LO[c % 2][:, :, i], HW[c % 2][:, w, :, i],
                                      start=(w == 0), stop=(w == parts - 1))
                m.then_inc(chunk_built, 1)

            def one_pass(g):
                c0, k0, parts = CHUNKS_BEFORE[g], g * PB, 3
                pe.wait_ge(pass_in, g + 1)

                def step(par, q, h):
                    return pe.matmul(bank[4 + par][:, q * F:(q + 1) * F], STR[:, par, q, h, :], TB[:, h, :],
                                     start=(h == 0), stop=(h == B - 1))

                def product(k, par, first, some=range(B2)):
                    if some[0] == 0:
                        pe.wait_ge(chunk_saved, k * CPB + (c0 + CPB))
                        if not first:
                            pe.wait_ge(agg_saved, k + (k0 - 1))
                    for x in some:
                        m = step(par, x // B, x % B)
                    if some[-1] == B2 - 1:
                        m.then_inc(spmm_done, 1)

                def pair(k, par, first, before, first_sums):
                    for c in range(CPB):
                        build_chunk(k, c, c0, parts, first and c < 2)
                        if before:
                            product(k - 1, 1 - par, first_sums, range(B2 * c // CPB, B2 * (c + 1) // CPB))

                pair(0, 0, g == 0, False, False)
                pair(1, 1, False, True, True)
                pair(2, 0, False, True, True)
                with pe.Fori(1, (PB - 1) // 2) as m:
                    pair(m * 2 + 1, 1, False, True, False)
                    pair(m * 2 + 2, 0, False, True, False)
                product(PB - 1, 0, False)

            def hops(g):
                k0 = g * PB
                pe.wait_ge(pass_in, g + 1)

                def hop(k, par, got, first):
                    pe.wait_ge(strip_got[par], got)
                    if not first:
                        pe.wait_ge(agg_saved, k + (k0 - 1))
                    for q in range(2):
                        for h in range(B):
                            m = pe.matmul(bank[4 + 2 * par + q][:, 0:3 * F], STC[:, par, q * B + h, :],
                                          TB3[:, h].rearrange("p w f -> p (w f)"), start=(h == 0), stop=(h == B - 1))
                    m.then_inc(spmm_done, 1)

                g0, g1 = (0, 0) if g == 3 else (16 * (PB - PB // 2), 16 * (PB // 2))
                hop(0, 0, g0 + 16, True)
                hop(1, 1, g1 + 16, True)
                with pe.Fori(1, PB // 2) as m:
                    hop(m * 2, 0, m * 16 + (g0 + 16), False)
                    hop(m * 2 + 1, 1, m * 16 + (g1 + 16), False)
                hop(PB - 1, 0, g0 + 16 * (PB - PB // 2), False)

            def rows():
                turn(tmpE)
                turn(tmpE)
                turn(maskE)
                turn(wE)
                one_pass(0)
                linear([(Hn, wself_s[:]), (AGG, wnb_s[:])])
                turn(tmpE)
                linear([(Hn, w1_s[:])])
                def strips_and_types(k, first):
                    for c in range(CPB):
                        build_chunk(k, c, NCH, 1, False)
                        pe.wait_ge(br_hot, k * CPB + (c + 1))
                        if c % 4 == 0 and not first:
                            pe.wait_ge(br_taken, k * 2 + (c // 4 - 1))
                        for i in range(CW):
                            o = 2 * (c % 4 * CW + i)
                            for w in range(3):
                                m = pe.matmul(bank[4 + c // 4][:, o:o + 2], BR[c % 2][:, i * P:(i + 1) * P], rtab[:, w, :],
                                              start=(w == 0), stop=(w == 2))
                        m.then_inc(br_looked, 1)

                strips_and_types(0, True)
                with pe.Fori(1, PB) as k:
                    strips_and_types(k, False)
                turn(wE)
                one_pass(1)
                linear([(AGG, conv_s[:])])
                pe.wait_ge(s_ready, 1)

                def look_up(c, u, first):
                    pe.wait_ge(bc_hot, c + 1)
                    if not first:
                        pe.wait_ge(look_used, c - 1)
                    for i in range(CW):
                        for w in range(3):
                            m = pe.matmul(bank[u][:, i * B:(i + 1) * B], LS[u][:, i * P:(i + 1) * P], stab[:, w, :],
                                          start=(w == 0), stop=(w == 2))
                    m.then_inc(look_done, 1)

                for u in range(2):
                    look_up(u, u, True)
                with pe.Fori(1, NCH // 2) as i:
                    for u in range(2):
                        look_up(i * 2 + u, u, False)
                one_pass(2)
                linear([(AGG, wlin_s[:])])
                hops(3)
                hops(4)

            def general():
                s = tile_sems["first"]
                with pe.Fori(0, ST) as t:
                    pe.wait_ge(s["staged"], t + 1)
                    pe.matmul(bank[0][:, 0:P], gA, ident[:], start=True, stop=True)
                    pe.matmul(bank[1][:, 0:P], gB, ident[:], start=True, stop=True).then_inc(s["row"], 1)

                def add_rows(g):
                    s = tile_sems[f"pass{g}"]
                    with pe.Fori(0, ST) as t:
                        pe.wait_ge(s["staged"], t + 1)
                        pe.matmul(bank[0][:, 0:P], gA, ident[:], start=True, stop=True).then_inc(s["row"], 1)
                        pe.wait_ge(s["scaled"], t + 1)
                        pe.matmul(bank[1][:, 0:AW], gM, gG, start=True, stop=True).then_inc(s["summed"], 1)

                add_rows(0)
                linear([(Hn, wself_s[:]), (AGG, wnb_s[:])])
                linear([(Hn, w1_s[:])])
                add_rows(1)
                add_rows(2)
                linear([(AGG, conv_s[:])])
                add_rows(3)
                linear([(AGG, wlin_s[:])])
                add_rows(4)
                add_rows(5)

            def afresh():
                lins[:] = [0, 0, 0]
                general()

            choose(pe, rows, afresh)

        @block.vector
        def _(v):
            n = [0, 0]

            def link(ins):
                n[0] += 1
                ins.then_inc(dve_step, 1)
                v.wait_ge(dve_step, n[1] + n[0])

            def tt(o, a, b, op):
                link(v.tensor_tensor(o, a, b, op))

            def ts(o, a, s1, s2, op0, op1=ALU.bypass):
                link(v.tensor_scalar(o, a, s1, s2, op0, op1) if s2 is not None else v.tensor_scalar(o, a, s1, None, op0))

            def red(o, a, op):
                link(v.tensor_reduce(o, a, AX.X, op))

            def bcb(c):
                return c[:, :, None].broadcast_to([P, B, F])

            def row(r):
                return r[:, None, :].broadcast_to([P, B, F])

            cols = [0]

            def ask_column():
                cols[0] += 1
                v.wait_ge(col_done, cols[0])

            def rstd(scale, add):
                n[0] += 1
                v.tensor_scalar(c1[:, 0:B], c1[:, 0:B], scale, add, ALU.mult, ALU.add).then_inc(dve_step, 1)
                v.wait_ge(dve_step, n[1] + n[0])
                v.nop().then_inc(col_ready, 1)
                ask_column()
                link(v.reciprocal(c2[:, 0:B], c2[:, 0:B]))

            def ask(ins):
                link(ins)
                v.nop().then_inc(col_ready, 1)
                ask_column()

            def centred(o, i):
                red(c3[:, 0:B], i, ALU.add)
                ts(c3[:, 0:B], c3[:, 0:B], 1.0 / F, None, ALU.mult)
                for g in range(5):
                    b = slice(g * B // 5, (g + 1) * B // 5)
                    tt(o[:, b, :], i[:, b, :], c3[:, b, None].broadcast_to([P, B // 5, F]), ALU.subtract)
                    v.nop().then_inc(col_ready, 1)
                for g in range(5):
                    b = slice(g * B // 5, (g + 1) * B // 5)
                    ask_column()
                    red(c1[:, b], T2[:, b, :], ALU.add)

            def norm_in():
                centred(Hn[:], X[:])
                rstd(1.0 / F, LN_EPS)
                link(v.scalar_tensor_tensor(out=Hn[:], in0=Hn[:], scalar=0.0, in1=bcb(c2[:, 0:B]),
                                            op0=ALU.max, op1=ALU.mult))

            v.memset(zero_l, 0.0).then_inc(zeros_made, 1)
            v.memset(zero_r, 0.0).then_inc(zeros_made, 1)
            link(v.memset(dlo, -1.0))
            link(v.memset(dhi, -1.0))
            v.wait_ge(const_made, 3)
            link(v.tensor_copy(iotaLo[:].rearrange("p a b -> p (a b)"), T1[:, 8:24, :].rearrange("p b f -> p (b f)").bitcast(I32)))
            link(v.tensor_copy(slotI[:], slotI[:].bitcast(I32)))
            link(v.tensor_copy(iotaP[:], iotaP[:].bitcast(I32)))
            ts(halfB[:], iotaP[:], float(SLOT), float(B), ALU.is_ge, ALU.mult)
            ts(iotaHi[:], iotaLo[:, 0:B, :], halfB[:, 0:1], None, ALU.add)

            v.wait_ge(dst_loaded, 32)
            link(v.memset(bad[:], 0.0))
            tt(ddiff[0:HP, :], dnext[0:HP, :], dstS[0:HP, 0:HT], ALU.subtract)
            red(bad[0:HP, 1:2], ddiff[0:HP, :], ALU.min)
            ts(bad[0:HP, 0:1], bad[0:HP, 1:2], 0.0, None, ALU.is_lt)
            ts(dloI[0:HP, 0:HT], dstS[0:HP, 0:HT], P - 1, None, ALU.bitwise_and)
            ts(dstS[0:HP, 0:HT], dstS[0:HP, 0:HT], 7, None, ALU.logical_shift_right)
            link(v.tensor_copy(dlo[0:HP, 0:HT], dloI[0:HP, 0:HT]))
            link(v.tensor_copy(dhi[0:HP, 0:HT], dstS[0:HP, 0:HT]))

            def hist(c, u, wait):
                if wait is not None:
                    v.wait_ge(hist_used, wait)
                v.tensor_tensor(LO[u][0:HP], dlo[0:HP, None, bass.ds(c * CW, CW)].broadcast_to([HP, P, CW]),
                                iotaLo[0:HP], ALU.is_equal)
                v.tensor_tensor(HH[u][0:HP], dhi[0:HP, None, bass.ds(c * CW, CW)].broadcast_to([HP, B, CW]),
                                iotaLo[0:HP, 0:B, :], ALU.is_equal).then_inc(hist_full, 1)

            for u in range(4):
                hist(u, u, None)
            with v.Fori(1, HTP // CW // 4) as i:
                for u in range(4):
                    hist(i * 4 + u, u, i * 4 + (u - 3))
            v.wait_ge(hist_done, 1)
            link(v.memset(deg[:], 0.0))
            v.tensor_copy(deg[:, 0:B], bank[0][:, 0:B]).then_inc(deg_ready, 1)
            v.wait_ge(deg_ready, 1)
            v.wait_ge(prefix_done, 1)
            link(v.tensor_copy(tot[:], bank[1][:, 32:32 + B]))
            link(v.tensor_tensor_scan(scn[:], tot[:], tot[:], 0.0, ALU.add, ALU.bypass))
            tt(scn[:], scn[:], tot[:], ALU.subtract)
            tt(rowf[:], scn[:], bank[1][:, 0:B], ALU.add)
            v.tensor_copy(rowI[:], rowf[:]).then_inc(row_ready, 1)
            red(bad[:, 2:3], deg[:, 0:B], ALU.max)
            ts(bad[:, 2:3], bad[:, 2:3], float(SLOT), None, ALU.is_gt)
            ts(c3[:, 0:B], slotI[:, 0:B], 2.0 * P * GT, float(2 * P * GT - SLOT), ALU.mult, ALU.add)
            tt(c3[:, 0:B], scn[:], c3[:, 0:B], ALU.is_gt)
            red(bad[:, 3:4], c3[:, 0:B], ALU.max)
            tt(bad[:, 2:3], bad[:, 2:3], bad[:, 3:4], ALU.add)
            n[0] += 1
            v.tensor_tensor(bad[:, 0:1], bad[:, 0:1], bad[:, 2:3], ALU.add).then_inc(dve_step, 1)
            v.wait_ge(dve_step, n[0])
            v.nop().then_inc(bad_ready, 1)
            v.wait_ge(bad_summed, 1)
            v.tensor_scalar(flagI[0:1, 0:1], bank[2][0:1, 0:1], 0.0, None, ALU.is_equal).then_inc(flag_ready, 1)
            tt(maskE[:], slotI[:, None, :].broadcast_to([P, BE, SLOT]), deg[:, :, None].broadcast_to([P, BE, SLOT]), ALU.is_lt)

            v.wait_ge(x_loaded, 16)
            norm_in()
            link(v.tensor_copy(TB[:], Hn[:]))

            turns = [0]

            def turned(fn):
                turns[0] += 1
                v.wait_ge(tout_ready, turns[0])
                for b4 in range(4):
                    w = min(512, PB * P - b4 * 512)
                    fn(slice(b4 * 512, b4 * 512 + w), bank[b4][:, 0:w])
                v.nop().then_inc(tout_used, 1)

            def turn_in():
                v.nop().then_inc(tin_ready, 1)

            def split3(cols, a):
                link(v.tensor_copy(wT[0][:, cols], a))
                tt(rT[:, cols], a, wT[0][:, cols], ALU.subtract)
                link(v.tensor_copy(wT[1][:, cols], rT[:, cols]))
                tt(rT[:, cols], rT[:, cols], wT[1][:, cols], ALU.subtract)
                link(v.tensor_copy(wT[2][:, cols], rT[:, cols]))

            def chunk(k, c, c0, first, weights, parts):
                at = bass.ds(k * P + c * CW, CW)
                u = c % 2
                if not first:
                    v.wait_ge(chunk_built, k * CPB + (c0 + c - 1))
                v.tensor_tensor(HM[u][:], hiT[:, None, at].broadcast_to([P, B2, CW]),
                                iotaLo[:, 0:B2, :], ALU.is_equal).then_inc(dve_step, 1)
                n[0] += 1
                v.tensor_tensor(LO[u][:], loT[:, None, at].broadcast_to([P, P, CW]), iotaLo[:], ALU.is_equal)
                v.wait_ge(dve_step, n[1] + n[0])
                v.tensor_tensor(HW[u][:, 0:parts], HM[u][:, None, :, :].broadcast_to([P, parts, B2, CW]),
                                weights[:, :, None, at].broadcast_to([P, parts, B2, CW]), ALU.mult).then_inc(hot_full, 1)

            def one_pass(g):
                c0 = CHUNKS_BEFORE[g]
                v.nop().then_inc(pass_in, 1)
                for c in range(CPB):
                    chunk(0, c, c0, g == 0 and c < 2, W3[:], 3)
                with v.Fori(1, PB) as k:
                    n[1] = k * CPB - CPB
                    for c in range(CPB):
                        chunk(k, c, c0, False, W3[:], 3)
                n[1] = 0
                n[0] += NCH - 2 * CPB
                v.wait_ge(agg_saved, (g + 1) * PB)

            def hops(g):
                v.nop().then_inc(pass_in, 1)

                def agg(k, par):
                    v.wait_ge(spmm_done, k + (g * PB + 1))
                    for q in range(2):
                        link(v.tensor_reduce(AGG[:, bass.ds(k * 2 + q, 1), :].rearrange("p k f -> p (k f)"),
                                             bank[4 + 2 * par + q][:, 0:3 * F].rearrange("p (w f) -> p f w", w=3), AX.X, ALU.add))
                    v.nop().then_inc(agg_saved, 1)

                n0 = n[0]
                with v.Fori(0, PB // 2) as m:
                    n[1] = m * 4
                    agg(m * 2, 0)
                    agg(m * 2 + 1, 1)
                n[1] = 0
                n[0] = n0 + PB // 2 * 4
                agg(PB - 1, 0)

            outs = [0]

            def linear(o, bias, kind="set", meanwhile=None):
                v.nop().then_inc(lin_in, 1)
                if meanwhile is not None:
                    meanwhile()
                for g in range(NG):
                    k, m = outs[0], min(4, B - 4 * g)
                    v.wait_ge(lin_ready, k + 1)
                    got = bank[2 + k % 2][:, 0:m * P].rearrange("p (b f) -> p b f", f=F)
                    to = o[:, 4 * g:4 * g + m, :]
                    if kind == "add":
                        i = v.tensor_tensor(to, got, to, ALU.add)
                    elif kind == "relu":
                        i = v.scalar_tensor_tensor(out=to, in0=got, scalar=0.0, in1=to, op0=ALU.max, op1=ALU.add)
                    else:
                        i = v.tensor_tensor(o[:, 4 * g:4 * g + m, :], got, bias[:, None, :].broadcast_to([P, m, F]), ALU.add)
                    i.then_inc(lin_taken, 1)
                    outs[0] += 1
                v.wait_ge(lin_taken, outs[0])

            A = AGG[:, 0:B, :]

            def l0_output():
                tt(T2, A, A, ALU.mult)
                red(c1[:, 0:B], T2, ALU.add)
                v.nop().then_inc(col_ready, 1)
                ask_column()
                tt(c2[:, 0:B], c2[:, 0:B], c4[:, 0:B], ALU.mult)
                ts(c2[:, 0:B], c2[:, 0:B], EPS, None, ALU.add)
                link(v.reciprocal(c2[:, 0:B], c2[:, 0:B]))
                tt(c2[:, 0:B], c2[:, 0:B], c4[:, 0:B], ALU.mult)
                tt(A, A, bcb(c2[:, 0:B]), ALU.mult)
                v.wait_ge(w_loaded, 16 * 17)
                tt(bias0[:, 0, :], bias0[:, 0, :], bias0[:, 1, :], ALU.add)
                linear(T1, bias0[:, 0, :], meanwhile=lambda: tt(X[:], X[:], row(bet_s[:]), ALU.add))
                centred(T1, T1)
                link(v.tensor_copy(dev[:], c1[:, 0:B]))
                tt(c3[:, 0:B], c3[:, 0:B], c3[:, 0:B], ALU.mult)
                link(v.scalar_tensor_tensor(out=c1[:, 0:B], in0=c3[:, 0:B], scalar=float(F), in1=dev[:],
                                            op0=ALU.mult, op1=ALU.add))
                v.nop().then_inc(col_ready, 1)
                ask_column()
                ts(c2[:, 0:B], c2[:, 0:B], 0.5, EPS, ALU.mult, ALU.add)
                link(v.reciprocal(c2[:, 0:B], c2[:, 0:B]))
                ts(fac[:], c2[:, 0:B], 0.5, None, ALU.mult)
                tt(dev[:], dev[:], fac[:], ALU.mult)
                tt(c1[:, 0:B], dev[:], fac[:], ALU.mult)
                rstd(1.0 / F, LN_EPS)
                tt(c2[:, 0:B], c2[:, 0:B], fac[:], ALU.mult)
                tt(T1, T1, bcb(c2[:, 0:B]), ALU.mult)
                tt(T1, T1, row(gam_s[:]), ALU.mult)
                tt(X[:], X[:], T1, ALU.add)


            def l1_project():
                norm_in()
                link(v.memset(bias1[:, 0:HID], 0.0))
                linear(T1, bias1[:])
                v.nop().then_inc(p_ready, 1)
                tt(X[:], X[:], row(biasc[:]), ALU.add)

            def l1_output():
                tt(A, A, TB[:], ALU.add)
                tt(A, A, bcb(dinv[:]), ALU.mult)
                linear(X, None, "add")


            def l2_columns():
                norm_in()
                tt(T1, Hn[:], row(wat_s[:]), ALU.mult)
                red(c3[:, 0:B], T1, ALU.add)

            def l2_types():
                v.wait_ge(w_loaded, 16 * 17)
                tt(T2[:, 0, :], rel_s[:, 0, :], wat_s[:], ALU.mult)
                red(rcol[:, 0:1], T2[:, 0, :], ALU.add)
                link(v.memset(rcol[:, 1:2], 0.0))
                tt(T2[0:NREL - P, 1, :], rel_s[0:NREL - P, 1, :], wat_s[0:NREL - P, :], ALU.mult)
                red(rcol[0:NREL - P, 1:2], T2[0:NREL - P, 1, :], ALU.add)

            def parts3(tab, col):
                for k in range(3):
                    link(v.tensor_copy(tab[:, k, :], col))
                    if k < 2:
                        tt(col, col, tab[:, k, :], ALU.subtract)

            def l2_output():
                linear(X, None, "relu")


            def l3_input():
                norm_in()
                ts(c1[:, 0:B], deg[:, 0:B], 1.0, None, ALU.max)
                v.nop().then_inc(col_ready, 1)
                ask_column()
                link(v.reciprocal(c2[:, 0:B], c2[:, 0:B]))
                ts(c3[:, 0:B], deg[:, 0:B], 1.0, None, ALU.min)
                tt(dis[:], c2[:, 0:B], c3[:, 0:B], ALU.mult)
                tt(TB[:], Hn[:], bcb(dis[:]), ALU.mult)

            def split_table():
                for w in range(3):
                    link(v.tensor_copy(TB3[:, :, w, :], TB[:]))
                    if w < 2:
                        tt(TB[:], TB[:], TB3[:, :, w, :], ALU.subtract)

            def l3_middle():
                tt(A, A, bcb(dis[:]), ALU.mult)
                tt(Hn[:], Hn[:], A, ALU.add)
                tt(TB[:], A, bcb(dis[:]), ALU.mult)

            def l3_output():
                tt(A, A, bcb(dis[:]), ALU.mult)
                tt(Hn[:], Hn[:], A, ALU.add)
                link(v.scalar_tensor_tensor(out=T1, in0=Hn[:], scalar=1.0 / 3.0, in1=X[:], op0=ALU.mult, op1=ALU.add))
                v.nop().then_inc(final_ready, 1)

            def rows():
                v.memset(zrow, 0.0).then_inc(zeros_made, 1)
                v.wait_ge(src_rows, 16 * B)
                link(v.memset(srcE[:, B:BE, :], 0))
                ts(tmpI, srcE[:], P - 1, None, ALU.bitwise_and)
                link(v.tensor_copy(tmpE, tmpI))
                turn_in()
                link(v.tensor_copy(bfE, tmpI))
                v.nop().then_inc(lo_ready, 1)
                turned(lambda c, a: link(v.tensor_copy(loT[:, c], a)))
                ts(tmpI, srcE[:], 7, None, ALU.logical_shift_right)
                link(v.tensor_copy(tmpE, tmpI))
                turn_in()
                turned(lambda c, a: link(v.tensor_scalar(hiT[:, c], a, halfB[:, 0:1], None, ALU.add)))
                turn_in()
                turned(lambda c, a: link(v.tensor_copy(mT[:, c], a)))
                v.wait_ge(ew_rows, 16 * B)
                link(v.memset(ewE[:, B:BE, :], 0.0))
                ts(tmpE, maskE[:], 1.0, BIG, ALU.subtract, ALU.mult)
                tt(wE, ewE[:], maskE[:], ALU.mult)
                tt(wE, wE, tmpE, ALU.add)
                red(c1[:], wE, ALU.max)
                ask(v.tensor_tensor(wE, wE, c1[:, :, None].broadcast_to([P, BE, SLOT]), ALU.subtract))
                tt(wE, wE, maskE[:], ALU.mult)
                turn_in()
                red(c4[:], wE, ALU.add)
                ts(c4[:], c4[:], 0.5, None, ALU.max)
                link(v.reciprocal(c4[:], c4[:]))
                turned(split3)
                v.wait_ge(lo_stored, 16)

                one_pass(0)
                l0_output()
                v.wait_ge(typ_rows, 16 * B)
                link(v.memset(typE[:, B:BE, :], 0))
                ts(tmpI, typE[:], P - 1, None, ALU.bitwise_and)
                link(v.tensor_copy(bfT, tmpI))
                v.nop().then_inc(lo_ready, 1)
                ts(tmpI, typE[:], 7, None, ALU.logical_shift_right)
                link(v.tensor_copy(tmpE, tmpI))
                turn_in()
                turned(lambda c, a: link(v.tensor_copy(thT[:, c], a)))
                v.wait_ge(lo_stored, 32)
                l2_types()
                parts3(rtab, rcol[:])
                l1_project()
                link(v.tensor_copy(QB, T1[:, :, HID:2 * HID]))
                v.nop().then_inc(q_saved, 1)
                v.wait_ge(p_stored, 16)
                link(v.memset(wE, 0.0))

                def slots(par):
                    return GB[par].rearrange("p (s f) -> p s f", f=HID)

                def strips_half(k, q):
                    for c in range(4 * q, 4 * q + 4):
                        chunk(k, c, NCH, False, mT[:, None, :], 1)
                        types(k, c)

                def half(k, q, ahead, first=False):
                    if ahead is not None:
                        strips_half(ahead, q)
                    v.wait_ge(blk_got[q], k * 16 + 16)
                    v.tensor_tensor(slots(q), slots(q), QB[:, bass.ds(k * 2 + q, 1), :].broadcast_to([P, SLOT, HID]),
                                    ALU.add).then_inc(blk_added, 1)
                    if ahead is not None:
                        take(ahead, q)
                    if not first:
                        logits(k * 2 + (q - 1), 1 - q)

                def types(k, c):
                    v.wait_ge(br_got[c % 2], k * (16 * CPB // 2) + 16 * (c // 2 + 1))
                    v.tensor_scalar(BR[c % 2], BR[c % 2], iotaP[:, 0:1], None, ALU.is_equal).then_inc(br_hot, 1)

                def take(k, q):
                    at = bass.ds(k * P + q * (4 * CW), 4 * CW)
                    tt(HR[:], thT[:, None, at].broadcast_to([P, 2, 4 * CW]),
                       iotaLo[:, 0:2, 0:1].broadcast_to([P, 2, 4 * CW]), ALU.is_equal)
                    v.wait_ge(br_looked, k * CPB + (4 * q + 4))
                    tt(VR[:], bank[4 + q][:, 0:8 * CW].rearrange("p (i h) -> p h i", h=2), HR[:], ALU.mult)
                    v.nop().then_inc(br_taken, 1)
                    tt(RV[:, at], VR[:, 0, :], VR[:, 1, :], ALU.add)

                def logits(b, par):
                    v.wait_ge(blk_gelu, b + 1)
                    link(v.tensor_tensor(slots(par), slots(par), w2_s[:, None, :].broadcast_to([P, SLOT, HID]), ALU.mult))
                    link(v.tensor_reduce(wE[:, bass.ds(b, 1), :].rearrange("p b s -> p (b s)"), slots(par), AX.X, ALU.add))
                    v.nop().then_inc(blk_used, 1)

                for k in range(2):
                    for q in range(2):
                        strips_half(k, q)
                        take(k, q)
                half(0, 0, 2, True)
                half(0, 1, 2)
                STEPS = CPB + 2 * 5
                n0 = n[0]
                with v.Fori(1, PB - 2) as k:
                    n[1] = (k - 1) * STEPS
                    half(k, 0, k + 2)
                    half(k, 1, k + 2)
                    assert n[0] - n0 == STEPS
                n[1] = 0
                n[0] = n0 + (PB - 3) * STEPS
                for b in range(2 * (PB - 2), B):
                    half(b // 2, b % 2, None)
                logits(B - 1, 0)
                v.nop().then_inc(col_ready, 1)
                ask_column()
                tt(wE, wE, maskE[:], ALU.mult)
                turn_in()
                red(c1[:], wE, ALU.add)
                rstd(1.0, 1.0)
                link(v.tensor_copy(dinv[:], c2[:, 0:B]))
                v.wait_ge(strip_put[0], 16 * (PB - PB // 2))
                v.wait_ge(strip_put[1], 16 * (PB // 2))
                tt(TB[:], Hn[:], bcb(dinv[:]), ALU.mult)
                turned(split3)
                one_pass(1)
                l1_output()
                l2_columns()
                parts3(stab, c3[:, 0:B])
                v.nop().then_inc(s_ready, 1)
                link(v.tensor_copy(TB[:], Hn[:]))

                def low(j, u, k, first):
                    v.wait_ge(bc_got[u], k)
                    if not first:
                        v.wait_ge(look_done, j - 1)
                    v.tensor_scalar(LS[u % 2], BC[u], iotaP[:, 0:1], None, ALU.is_equal).then_inc(bc_hot, 1)

                def high(j, u):
                    n[0] += 1
                    v.tensor_tensor(HM[u % 2][:, 0:B, :], hiT[:, None, bass.ds(j * CW, CW)].broadcast_to([P, B, CW]),
                                    iotaHi[:], ALU.is_equal).then_inc(dve_step, 1)

                def pick(c, u):
                    v.wait_ge(look_done, c + 1)
                    v.tensor_tensor(VPS[u % 2], bank[u % 2][:, 0:CW * B].rearrange("p (i h) -> p h i", h=B),
                                    HM[u % 2][:, 0:B, :], ALU.mult).then_inc(look_used, 1)

                def sum_up(c, u):
                    v.wait_ge(look_used, c + 1)
                    v.wait_ge(dve_step, n[1] + n[0])
                    n[0] += 1
                    v.tensor_reduce(rT[:, bass.ds(c * CW, CW)], VPS[u % 2].rearrange("p h i -> p i h"),
                                    AX.X, ALU.add).then_inc(dve_step, 1)

                low(0, 0, 16, True)
                high(0, 0)
                low(1, 1, 16, True)
                high(1, 1)
                v.wait_ge(dve_step, n[0])
                pick(0, 0)
                for j in (2, 3):
                    low(j, j, 16, False)
                    sum_up(j - 2, j)
                    high(j, j)
                    pick(j - 1, j - 1)
                n0 = n[0]
                with v.Fori(1, NCH // 4) as i:
                    n[1] = (i - 1) * 8
                    for u in range(4):
                        low(i * 4 + u, u, i * 16 + 16, False)
                        sum_up(i * 4 + (u - 2), u)
                        high(i * 4 + u, u)
                        pick(i * 4 + (u - 1), u + 3)
                    assert n[0] - n0 == 8
                n[1] = 0
                n[0] = n0 + 8 * (NCH // 4 - 1)
                sum_up(NCH - 2, 0)
                pick(NCH - 1, 1)
                sum_up(NCH - 1, 1)
                v.wait_ge(dve_step, n[0])
                tt(rT[:], rT[:], RV, ALU.add)
                v.nop().then_inc(col_ready, 1)
                ask_column()
                tt(rT[:], rT[:], mT[:], ALU.mult)
                link(v.tensor_copy(wT[0][:], rT[:]))
                tt(rT[:], rT[:], wT[0][:], ALU.subtract)
                link(v.tensor_copy(wT[1][:], rT[:]))
                tt(rT[:], rT[:], wT[1][:], ALU.subtract)
                link(v.tensor_copy(wT[2][:], rT[:]))
                one_pass(2)
                l2_output()
                l3_input()
                split_table()
                hops(3)
                l3_middle()
                split_table()
                hops(4)
                l3_output()

            def general():
                def tile_loop(steps, body):
                    n0 = n[0]
                    with v.Fori(0, ST) as t:
                        n[1] = t * steps
                        body(t)
                        assert n[0] - n0 == steps, n[0] - n0
                    n[1] = 0
                    n[0] = n0 + steps * ST

                def at(a, t):
                    return a[:, bass.ds(t, 1)]

                v.wait_ge(g_loaded, 64)
                link(v.tensor_copy(gdstF, gdst))
                link(v.memset(zeros, -BIG))
                v.nop().then_inc(g_seg_in, 1)
                v.wait_ge(g_low, 1)
                ts(gc[:, 5:6], iotaP[:], float(B * P), None, ALU.add)

                def first(t):
                    s = tile_sems["first"]
                    link(v.tensor_copy(gc[:, 2:3], at(gdstF, t)))
                    link(v.tensor_copy(gc[:, 3:4], at(gew, t)))
                    link(v.tensor_copy(gi[:, 0:1], at(gdst, t)))
                    link(v.tensor_copy(gA, gc[:, 2:3].broadcast_to([P, P])))
                    v.tensor_copy(gB, gc[:, 3:4].broadcast_to([P, P])).then_inc(s["staged"], 1)
                    v.wait_ge(s["row"], t + 1)
                    ts(gM, bank[0][:, 0:P], gc[:, 2:3], None, ALU.is_equal)
                    tt(gMx, gM, gLow, ALU.mult)
                    red(gc[:, 4:5], gMx, ALU.add)
                    ts(gc[:, 4:5], gc[:, 4:5], 0.0, None, ALU.is_equal)
                    tt(gc[:, 6:7], gc[:, 2:3], gc[:, 5:6], ALU.subtract)
                    tt(gc[:, 6:7], gc[:, 6:7], gc[:, 4:5], ALU.mult)
                    tt(gc[:, 6:7], gc[:, 6:7], gc[:, 5:6], ALU.add)
                    link(v.tensor_copy(gi[:, 1:2], gc[:, 6:7]))
                    link(v.tensor_copy(at(gadj, t), gc[:, 6:7]))
                    tt(gMx, bank[1][:, 0:P], gM, ALU.mult)
                    ts(gM, gM, 1.0, BIG, ALU.subtract, ALU.mult)
                    tt(gMx, gMx, gM, ALU.add)
                    red(gc[:, 7:8], gMx, ALU.max)
                    v.wait_ge(s["got"], t * 16 + 16)
                    v.tensor_tensor(gc[:, 1:2], gc[:, 0:1], gc[:, 7:8], ALU.max).then_inc(s["ready"], 1)
                    v.wait_ge(s["added"], t * 16 + 16)

                tile_loop(17, first)

                def wt0(t):
                    s = tile_sems["wt0"]
                    v.tensor_copy(gi[:, 0:1], at(gdst, t)).then_inc(s["staged"], 1)
                    v.wait_ge(s["got"], t * 16 + 16)
                    tt(at(gwF, t), at(gew, t), gc[:, 0:1], ALU.subtract)

                tile_loop(1, wt0)
                v.nop().then_inc(col_ready, 1)
                ask_column()

                def add_rows(g):
                    s = tile_sems[f"pass{g}"]
                    link(v.memset(zeros, 0.0))
                    link(v.memset(gG, 0.0))
                    v.nop().then_inc(g_pass_in, 1)

                    def tile(t):
                        link(v.tensor_copy(gc[:, 2:3], at(gdstF, t)))
                        link(v.tensor_copy(gc[:, 3:4], at(gwF, t)))
                        link(v.tensor_copy(gi[:, 0:1], at(gsrc, t)))
                        link(v.tensor_copy(gi[:, 1:2], at(gadj, t)))
                        v.tensor_copy(gA, gc[:, 2:3].broadcast_to([P, P])).then_inc(s["staged"], 1)
                        v.wait_ge(s["row"], t + 1)
                        ts(gM, bank[0][:, 0:P], gc[:, 2:3], None, ALU.is_equal)
                        v.wait_ge(s["got"], t * 16 + 16)
                        link(v.tensor_scalar(gG[:, 0:F], gG[:, 0:F], gc[:, 3:4], None, ALU.mult))
                        v.tensor_copy(gG[:, F:F + 1], gc[:, 3:4]).then_inc(s["scaled"], 1)
                        v.wait_ge(s["summed"], t + 1)
                        v.tensor_copy(gO, bank[1][:, 0:AW]).then_inc(s["ready"], 1)
                        v.wait_ge(s["added"], t * 16 + 16)

                    tile_loop(6, tile)
                    v.wait_ge(g_sums, 32 * (g + 1))

                add_rows(0)
                ts(c4[:, 0:B], c1[:, 0:B], 0.5, None, ALU.max)
                link(v.reciprocal(c4[:, 0:B], c4[:, 0:B]))
                l0_output()
                l1_project()
                v.wait_ge(p_stored, 32)

                def wt1(t):
                    s = tile_sems["wt1"]
                    link(v.tensor_copy(gi[:, 0:1], at(gsrc, t)))
                    v.tensor_copy(gi[:, 1:2], at(gdst, t)).then_inc(s["staged"], 1)
                    v.wait_ge(s["got"], t * 32 + 32)
                    v.tensor_tensor(gPQ[:, 0:HID], gPQ[:, 0:HID], gPQ[:, HID:2 * HID], ALU.add).then_inc(s["row"], 1)
                    v.wait_ge(s["scaled"], t + 1)
                    tt(gG[:, 0:HID], gG[:, 0:HID], w2_s[:], ALU.mult)
                    red(at(gwF, t), gG[:, 0:HID], ALU.add)

                tile_loop(3, wt1)
                v.nop().then_inc(col_ready, 1)
                ask_column()
                add_rows(1)
                rstd(1.0, 1.0)
                link(v.tensor_copy(dinv[:], c2[:, 0:B]))
                tt(TB[:], Hn[:], bcb(dinv[:]), ALU.mult)
                add_rows(2)
                l1_output()
                l2_types()
                l2_columns()
                v.nop().then_inc(g_col, 1)

                def wt2(t):
                    s = tile_sems["wt2"]
                    link(v.tensor_copy(gi[:, 0:1], at(gsrc, t)))
                    v.tensor_copy(gi[:, 1:2], at(gtyp, t)).then_inc(s["staged"], 1)
                    v.wait_ge(s["got"], t * 32 + 32)
                    tt(at(gwF, t), gc[:, 0:1], gc[:, 1:2], ALU.add)

                tile_loop(2, wt2)
                v.nop().then_inc(col_ready, 1)
                ask_column()
                link(v.tensor_copy(TB[:], Hn[:]))
                add_rows(3)
                l2_output()
                l3_input()
                link(v.memset(gwF, 1.0))
                add_rows(4)
                l3_middle()
                add_rows(5)
                l3_output()

            count0 = list(n), list(cols), list(turns), list(outs)
            def fresh():
                for c, c0 in zip((n, cols, turns, outs), count0):
                    c[:] = c0

            choose(v, rows, lambda: (fresh(), general()))


_INS = [("x", "x"), ("src", "src"), ("dst", "dst"), ("etype", "edge_type_200"), ("eweight", "edge_weight"),
        ("w_self", "L0_gnn_W_self"), ("b_self", "L0_gnn_b_self"), ("w_nb", "L0_gnn_W_nb"), ("b_nb", "L0_gnn_b_nb"),
        ("gamma", "L0_gnn_gamma"), ("beta", "L0_gnn_beta"), ("w1", "L1_gnn_mlp_w1"), ("b1", "L1_gnn_mlp_b1"),
        ("w2", "L1_gnn_mlp_w2"), ("b2", "L1_gnn_mlp_b2"), ("conv_w", "L1_gnn_conv_w"), ("conv_b", "L1_gnn_conv_b"),
        ("rel", "L2_gnn_rel_emb"), ("w_lin_t", "L2_gnn_W_lin"), ("w_attn", "L2_gnn_W_attn")]


def kernel(**inputs):
    import numpy as np
    import concourse.bacc as bacc
    from concourse.bass_utils import run_bass_kernel_spmd

    a = {short: np.asarray(inputs[name]) for short, name in _INS}
    a["x"] = np.concatenate([a["x"], np.zeros((B * P - N, F), a["x"].dtype)])
    for k in ("src", "dst", "etype", "eweight"):
        a[k] = np.concatenate([a[k], np.full(EP - E, N if k == "dst" else 0, a[k].dtype)]).reshape(EP, 1)
    a["w_lin_t"] = a["w_lin_t"].T
    for k in ("b_self", "b_nb", "gamma", "beta", "b1", "w2", "b2", "conv_b", "w_attn"):
        a[k] = a[k].reshape(1, -1)
    a = {f"{k}_dram": np.ascontiguousarray(v) for k, v in a.items()}
    nc = bacc.Bacc("TRN2", target_bir_lowering=False, num_devices=1)
    args = [nc.dram_tensor(k, v.shape, mybir.dt.from_np(v.dtype), kind="ExternalInput").ap() for k, v in a.items()]
    out = nc.dram_tensor("out_dram", (B * P, F), F32, kind="ExternalOutput").ap()
    build(nc, *args, out)
    r = run_bass_kernel_spmd(nc, [a], core_ids=[0])
    return r.results[0]["out_dram"][:N]
```
